# Optimizing a Trainium2 kernel written in Bass

```python
import numpy as np
import jax
import jax.numpy as jnp

def _softmax(x, axis=-1):
    return jax.nn.softmax(x, axis=axis)

def _gelu(x):
    return jax.nn.gelu(x, approximate=True)

def _silu(x):
    return jax.nn.silu(x)

def _sigmoid(x):
    return jax.nn.sigmoid(x)

def _layernorm(x, axis=-1, eps=1e-05):
    m = jnp.mean(x, axis=axis, keepdims=True)
    v = jnp.var(x, axis=axis, keepdims=True)
    return (x - m) / jnp.sqrt(v + eps)

def _scatter_add(tgt, idx, src, axis=0):
    return tgt.at[idx].add(src)

def _segment_sum(src, seg, n):
    return jax.ops.segment_sum(src, seg, n)
kernel_name = 'mk_flamingo_gated_d4_seqx_r8_118cc3'

def setup_inputs(seed: int=0):
    np.random.seed(seed)
    _w = jnp.asarray

    def _rec_inputs():
        import jax
        import jax.numpy as jnp
        _rk = jax.random.key(seed)
        x = -0.000125 + 0.9999 * jax.random.normal(jax.random.fold_in(_rk, 1), (32, 64, 128), jnp.float32)
        _lenS = 64 - jax.random.randint(jax.random.fold_in(_rk, 7), (32,), 0, max(1, 64 // 4) + 1, jnp.int32)
        _lenS2 = 64 - jax.random.randint(jax.random.fold_in(_rk, 8), (32,), 0, max(1, 64 // 4) + 1, jnp.int32)
        _ctx_768P = jax.random.normal(jax.random.fold_in(_rk, 11), (32, 16, 96), jnp.float32)
        _ctx_768c = jax.random.dirichlet(jax.random.fold_in(_rk, 511), 0.3 * jnp.ones((16,), jnp.float32), (32, 64))
        _ctx_768t = jnp.einsum('bsk,bkd->bsd', _ctx_768c, _ctx_768P)
        _ctx_768t = _ctx_768t * jax.lax.rsqrt(jnp.mean(jnp.square(_ctx_768t)) + 1e-12) * 0.953939
        ctx_768 = -7.36909e-05 + 0.999899 * (_ctx_768t + 0.3 * jax.random.normal(jax.random.fold_in(_rk, 611), (32, 64, 96), jnp.float32))
        _g = jax.random.normal(jax.random.fold_in(_rk, 9001), (2, 4), jnp.float32)
        _g = jnp.sign(_g) * jnp.maximum(jnp.abs(_g), 1.0) + (_g == 0) * 1.0
        g_xattn = _g[0]
        g_ffn = _g[1]
        return (x, ctx_768, g_xattn, g_ffn)
    x, ctx_768, g_xattn, g_ffn = _rec_inputs()

    def _L0_xattn_setup():
        import jax, jax.numpy as jnp
        import numpy as np
        import math
        E = 128
        EV = 128
        FFN = 512
        DINO = 96
        B, S, P = (64, 64, 32)

        def bitnet_linear(x, W, b):
            w_scale = jnp.maximum(jnp.mean(jnp.abs(W)), 1e-05)
            qW = jnp.sign(W) * (jnp.abs(W) > 0.5 * w_scale).astype(W.dtype)
            i_scale = jnp.maximum(jnp.max(jnp.abs(x)), 1e-08) / 127.0
            qx = jnp.clip(jnp.round(x / i_scale), -128.0, 127.0)
            out = jnp.einsum('...i,oi->...o', qx, qW) * (w_scale * i_scale)
            return out + b
        key = jax.random.key(seed)
        ks = iter(jax.random.split(key, 32))

        def lin_w(fin, fout):
            return jax.random.normal(next(ks), (fout, fin), jnp.float32) * math.sqrt(2.0 / fin)
        return {'text_embeddings': jax.random.normal(next(ks), (B, S, E), jnp.float32), 'dinov2_features': jax.random.normal(next(ks), (B, P, DINO), jnp.float32), 'W_d2v': lin_w(DINO, EV), 'b_d2v': jnp.zeros((EV,), jnp.float32), 'W_img': lin_w(EV, E), 'b_img': jnp.zeros((E,), jnp.float32), 'W_txt': lin_w(E, E), 'b_txt': jnp.zeros((E,), jnp.float32), 'W_att0': lin_w(E, E // 2), 'b_att0': jnp.zeros((E // 2,), jnp.float32), 'W_att1': lin_w(E, E // 2), 'b_att1': jnp.zeros((E // 2,), jnp.float32), 'W_f1': lin_w(2 * E, FFN), 'b_f1': jnp.zeros((FFN,), jnp.float32), 'W_f2': lin_w(FFN, E), 'b_f2': jnp.zeros((E,), jnp.float32)}
    _L0_xattn_all = _L0_xattn_setup()
    _L0_xattn_in = {k: v for k, v in _L0_xattn_all.items() if k in ('W_d2v', 'b_d2v', 'W_img', 'b_img', 'W_txt', 'b_txt', 'W_att0', 'b_att0', 'W_att1', 'b_att1', 'W_f1', 'b_f1', 'W_f2', 'b_f2')}
    del _L0_xattn_all

    def _L0_ffn_setup():
        import jax, jax.numpy as jnp
        import numpy as np
        BLOCK = 32
        W_BITS = 4
        ACT_BITS = 16

        def act_qdq(x):
            qmax = 2.0 ** (ACT_BITS - 1) - 1.0
            scale = jnp.maximum(jnp.max(jnp.abs(x)) / qmax, 1e-12)
            return jnp.clip(jnp.round(x / scale), -qmax - 1.0, qmax) * scale

        def fixed_qdq_u16(x):
            scale = 1.0 / 65536.0
            return jnp.clip(jnp.round(x / scale), 0.0, 65535.0) * scale

        def lpbq_dequant(w):
            O, I = w.shape
            qmax = 2.0 ** (W_BITS - 1) - 1.0
            wb = w.reshape(O, I // BLOCK, BLOCK)
            s = jnp.maximum(jnp.max(jnp.abs(wb), axis=-1, keepdims=True) / qmax, 1e-12)
            wq = jnp.clip(jnp.round(wb / s), -qmax - 1.0, qmax) * s
            return wq.reshape(O, I)
        key = jax.random.key(seed)
        k1, k2, k3, k4 = jax.random.split(key, 4)
        B, S, H, I = (2, 512, 128, 384)
        x = jax.random.normal(k1, (B, S, H), jnp.float32)
        w_gate = jax.random.normal(k2, (I, H), jnp.float32) * 0.02
        w_up = jax.random.normal(k3, (I, H), jnp.float32) * 0.02
        w_down = jax.random.normal(k4, (H, I), jnp.float32) * 0.02
        return {'x': x, 'w_gate': w_gate, 'w_up': w_up, 'w_down': w_down}
    _L0_ffn_all = _L0_ffn_setup()
    _L0_ffn_in = {k: v for k, v in _L0_ffn_all.items() if k in ('w_gate', 'w_up', 'w_down')}
    del _L0_ffn_all

    def _L1_xattn_setup():
        import jax, jax.numpy as jnp
        import numpy as np
        LATENT_CH = 128
        INPUT_CH = 96
        QK_CH = 128
        V_CH = 128
        OUT_CH = 128
        NHEADS = 8
        EPS = 1e-05

        def layer_norm(x, gamma, beta):
            mu = jnp.mean(x, axis=-1, keepdims=True)
            var = jnp.var(x, axis=-1, keepdims=True)
            return (x - mu) * jax.lax.rsqrt(var + EPS) * gamma + beta
        key = jax.random.key(seed)
        ks = jax.random.split(key, 6)
        B, Lq, Lkv = (8, 64, 2048)
        latent_q = jax.random.normal(ks[0], (B, Lq, LATENT_CH), dtype=jnp.float32)
        input_kv = jax.random.normal(ks[1], (B, Lkv, INPUT_CH), dtype=jnp.float32)
        W_Q = jax.random.normal(ks[2], (LATENT_CH, QK_CH), dtype=jnp.float32) / np.sqrt(LATENT_CH)
        W_K = jax.random.normal(ks[3], (INPUT_CH, QK_CH), dtype=jnp.float32) / np.sqrt(INPUT_CH)
        W_V = jax.random.normal(ks[4], (INPUT_CH, V_CH), dtype=jnp.float32) / np.sqrt(INPUT_CH)
        W_O = jax.random.normal(ks[5], (V_CH, OUT_CH), dtype=jnp.float32) / np.sqrt(V_CH)
        ln_lat_g = jnp.ones((LATENT_CH,), jnp.float32)
        ln_lat_b = jnp.zeros((LATENT_CH,), jnp.float32)
        ln_in_g = jnp.ones((INPUT_CH,), jnp.float32)
        ln_in_b = jnp.zeros((INPUT_CH,), jnp.float32)
        return dict(latent_q=latent_q, input_kv=input_kv, W_Q=W_Q, W_K=W_K, W_V=W_V, W_O=W_O, ln_lat_g=ln_lat_g, ln_lat_b=ln_lat_b, ln_in_g=ln_in_g, ln_in_b=ln_in_b)
    _L1_xattn_all = _L1_xattn_setup()
    _L1_xattn_in = {k: v for k, v in _L1_xattn_all.items() if k in ('W_Q', 'W_K', 'W_V', 'W_O', 'ln_lat_g', 'ln_lat_b', 'ln_in_g', 'ln_in_b')}
    del _L1_xattn_all

    def _L1_ffn_setup():
        import jax, jax.numpy as jnp
        import numpy as np
        B, S, D = (4, 256, 128)
        E, F = (8, 512)
        key = jax.random.key(seed)
        ks = jax.random.split(key, 5)
        x = jax.random.normal(ks[0], (B, S, D), dtype=jnp.float32)
        switch_w = jax.random.normal(ks[1], (D, E), dtype=jnp.float32) * D ** (-0.5)
        switch_b = jnp.zeros((E,), dtype=jnp.float32)
        w1 = jax.random.normal(ks[2], (E, D, F), dtype=jnp.float32) * D ** (-0.5)
        b1 = jnp.zeros((E, F), dtype=jnp.float32)
        w2 = jax.random.normal(ks[3], (E, F, D), dtype=jnp.float32) * F ** (-0.5)
        b2 = jnp.zeros((E, D), dtype=jnp.float32)
        return {'x': x, 'switch_w': switch_w, 'switch_b': switch_b, 'w1': w1, 'b1': b1, 'w2': w2, 'b2': b2}
    _L1_ffn_all = _L1_ffn_setup()
    _L1_ffn_in = {k: v for k, v in _L1_ffn_all.items() if k in ('switch_w', 'switch_b', 'w1', 'b1', 'w2', 'b2')}
    del _L1_ffn_all

    def _L2_xattn_setup():
        import jax, jax.numpy as jnp
        import numpy as np
        NUM_HEADS = 16
        CLAMP = 10000.0
        key = jax.random.key(seed)
        ks = jax.random.split(key, 8)
        B, Nq, Nkv, Cq, Ckv = (4, 256, 256, 128, 96)
        s_q = 1.0 / np.sqrt(Cq)
        s_kv = 1.0 / np.sqrt(Ckv)
        return {'query': jax.random.normal(ks[0], (B, Nq, Cq), jnp.float32), 'key_value': jax.random.normal(ks[1], (B, Nkv, Ckv), jnp.float32), 'Wq': jax.random.normal(ks[2], (Cq, Cq), jnp.float32) * s_q, 'bq': jnp.zeros((Cq,), jnp.float32), 'Wk': jax.random.normal(ks[3], (Ckv, Cq), jnp.float32) * s_kv, 'bk': jnp.zeros((Cq,), jnp.float32), 'Wv': jax.random.normal(ks[4], (Ckv, Cq), jnp.float32) * s_kv, 'bv': jnp.zeros((Cq,), jnp.float32), 'Wo': jax.random.normal(ks[5], (Cq, Cq), jnp.float32) * s_q, 'bo': jnp.zeros((Cq,), jnp.float32)}
    _L2_xattn_all = _L2_xattn_setup()
    _L2_xattn_in = {k: v for k, v in _L2_xattn_all.items() if k in ('Wq', 'bq', 'Wk', 'bk', 'Wv', 'bv', 'Wo', 'bo')}
    del _L2_xattn_all

    def _L2_ffn_setup():
        import jax, jax.numpy as jnp
        import numpy as np
        HIDDEN = 128
        INTER = 512
        NUM_EXPERTS = 8
        TOP_K = 2
        EPS = 1e-05

        def _layer_norm(x, g, b):
            m = jnp.mean(x, axis=-1, keepdims=True)
            v = jnp.mean(jnp.square(x - m), axis=-1, keepdims=True)
            return (x - m) * jax.lax.rsqrt(v + EPS) * g + b
        key = jax.random.key(seed)
        ks = jax.random.split(key, 8)
        s = 0.02
        return {'x': jax.random.normal(ks[0], (4, 256, HIDDEN), dtype=jnp.float32), 'ln1_g': jnp.ones((HIDDEN,), jnp.float32), 'ln1_b': jnp.zeros((HIDDEN,), jnp.float32), 'attn_w': jax.random.normal(ks[1], (HIDDEN, HIDDEN), jnp.float32) * s, 'ln2_g': jnp.ones((HIDDEN,), jnp.float32), 'ln2_b': jnp.zeros((HIDDEN,), jnp.float32), 'gate_w': jax.random.normal(ks[2], (NUM_EXPERTS, HIDDEN), jnp.float32) * s, 'gate_proj': jax.random.normal(ks[3], (NUM_EXPERTS, INTER, HIDDEN), jnp.float32) * s, 'up_proj': jax.random.normal(ks[4], (NUM_EXPERTS, INTER, HIDDEN), jnp.float32) * s, 'down_proj': jax.random.normal(ks[5], (NUM_EXPERTS, HIDDEN, INTER), jnp.float32) * s}
    _L2_ffn_all = _L2_ffn_setup()
    _L2_ffn_in = {k: v for k, v in _L2_ffn_all.items() if k in ('ln1_g', 'ln1_b', 'attn_w', 'ln2_g', 'ln2_b', 'gate_w', 'gate_proj', 'up_proj', 'down_proj')}
    del _L2_ffn_all

    def _L3_xattn_setup():
        import jax, jax.numpy as jnp
        import numpy as np
        HEADS = 16
        DIM_HEAD = 64
        SCALE = DIM_HEAD ** (-0.5)
        QUERY_DIM = 128
        CONTEXT_DIM = 96
        INNER_DIM = HEADS * DIM_HEAD
        key = jax.random.key(seed)
        ks = jax.random.split(key, 7)
        B, Nq, Nk = (8, 512, 77)
        x = jax.random.normal(ks[0], (B, Nq, QUERY_DIM), dtype=jnp.float32)
        context = jax.random.normal(ks[1], (B, Nk, CONTEXT_DIM), dtype=jnp.float32)
        Wq = jax.random.normal(ks[2], (QUERY_DIM, INNER_DIM), dtype=jnp.float32) * QUERY_DIM ** (-0.5)
        Wk = jax.random.normal(ks[3], (CONTEXT_DIM, INNER_DIM), dtype=jnp.float32) * CONTEXT_DIM ** (-0.5)
        Wv = jax.random.normal(ks[4], (CONTEXT_DIM, INNER_DIM), dtype=jnp.float32) * CONTEXT_DIM ** (-0.5)
        Wo = jax.random.normal(ks[5], (INNER_DIM, QUERY_DIM), dtype=jnp.float32) * INNER_DIM ** (-0.5)
        bo = jnp.zeros((QUERY_DIM,), dtype=jnp.float32)
        return {'x': x, 'context': context, 'Wq': Wq, 'Wk': Wk, 'Wv': Wv, 'Wo': Wo, 'bo': bo}
    _L3_xattn_all = _L3_xattn_setup()
    _L3_xattn_in = {k: v for k, v in _L3_xattn_all.items() if k in ('Wq', 'Wk', 'Wv', 'Wo', 'bo')}
    del _L3_xattn_all

    def _L3_ffn_setup():
        import jax, jax.numpy as jnp
        import numpy as np
        B, S, H, F, E, K = (4, 256, 128, 512, 8, 2)
        key = jax.random.key(seed)
        ks = jax.random.split(key, 4)
        sc = lambda d: 1.0 / np.sqrt(d)
        return {'x': jax.random.normal(ks[0], (B, S, H), jnp.float32), 'gate_w': jax.random.normal(ks[1], (H, E), jnp.float32) * sc(H), 'gate_b': jnp.zeros((E,), jnp.float32), 'w1': jax.random.normal(ks[2], (E, H, F), jnp.float32) * sc(H), 'b1': jnp.zeros((E, F), jnp.float32), 'w2': jax.random.normal(ks[3], (E, F, H), jnp.float32) * sc(F), 'b2': jnp.zeros((E, H), jnp.float32)}
    _L3_ffn_all = _L3_ffn_setup()
    _L3_ffn_in = {k: v for k, v in _L3_ffn_all.items() if k in ('gate_w', 'gate_b', 'w1', 'b1', 'w2', 'b2')}
    del _L3_ffn_all
    return {'x': x, 'ctx_768': ctx_768, 'g_xattn': g_xattn, 'g_ffn': g_ffn, 'L0_xattn_W_d2v': _L0_xattn_in['W_d2v'], 'L0_xattn_b_d2v': _L0_xattn_in['b_d2v'], 'L0_xattn_W_img': _L0_xattn_in['W_img'], 'L0_xattn_b_img': _L0_xattn_in['b_img'], 'L0_xattn_W_txt': _L0_xattn_in['W_txt'], 'L0_xattn_b_txt': _L0_xattn_in['b_txt'], 'L0_xattn_W_att0': _L0_xattn_in['W_att0'], 'L0_xattn_b_att0': _L0_xattn_in['b_att0'], 'L0_xattn_W_att1': _L0_xattn_in['W_att1'], 'L0_xattn_b_att1': _L0_xattn_in['b_att1'], 'L0_xattn_W_f1': _L0_xattn_in['W_f1'], 'L0_xattn_b_f1': _L0_xattn_in['b_f1'], 'L0_xattn_W_f2': _L0_xattn_in['W_f2'], 'L0_xattn_b_f2': _L0_xattn_in['b_f2'], 'L0_ffn_w_gate': _L0_ffn_in['w_gate'], 'L0_ffn_w_up': _L0_ffn_in['w_up'], 'L0_ffn_w_down': _L0_ffn_in['w_down'], 'L1_xattn_W_Q': _L1_xattn_in['W_Q'], 'L1_xattn_W_K': _L1_xattn_in['W_K'], 'L1_xattn_W_V': _L1_xattn_in['W_V'], 'L1_xattn_W_O': _L1_xattn_in['W_O'], 'L1_xattn_ln_lat_g': _L1_xattn_in['ln_lat_g'], 'L1_xattn_ln_lat_b': _L1_xattn_in['ln_lat_b'], 'L1_xattn_ln_in_g': _L1_xattn_in['ln_in_g'], 'L1_xattn_ln_in_b': _L1_xattn_in['ln_in_b'], 'L1_ffn_switch_w': _L1_ffn_in['switch_w'], 'L1_ffn_switch_b': _L1_ffn_in['switch_b'], 'L1_ffn_w1': _L1_ffn_in['w1'], 'L1_ffn_b1': _L1_ffn_in['b1'], 'L1_ffn_w2': _L1_ffn_in['w2'], 'L1_ffn_b2': _L1_ffn_in['b2'], 'L2_xattn_Wq': _L2_xattn_in['Wq'], 'L2_xattn_bq': _L2_xattn_in['bq'], 'L2_xattn_Wk': _L2_xattn_in['Wk'], 'L2_xattn_bk': _L2_xattn_in['bk'], 'L2_xattn_Wv': _L2_xattn_in['Wv'], 'L2_xattn_bv': _L2_xattn_in['bv'], 'L2_xattn_Wo': _L2_xattn_in['Wo'], 'L2_xattn_bo': _L2_xattn_in['bo'], 'L2_ffn_ln1_g': _L2_ffn_in['ln1_g'], 'L2_ffn_ln1_b': _L2_ffn_in['ln1_b'], 'L2_ffn_attn_w': _L2_ffn_in['attn_w'], 'L2_ffn_ln2_g': _L2_ffn_in['ln2_g'], 'L2_ffn_ln2_b': _L2_ffn_in['ln2_b'], 'L2_ffn_gate_w': _L2_ffn_in['gate_w'], 'L2_ffn_gate_proj': _L2_ffn_in['gate_proj'], 'L2_ffn_up_proj': _L2_ffn_in['up_proj'], 'L2_ffn_down_proj': _L2_ffn_in['down_proj'], 'L3_xattn_Wq': _L3_xattn_in['Wq'], 'L3_xattn_Wk': _L3_xattn_in['Wk'], 'L3_xattn_Wv': _L3_xattn_in['Wv'], 'L3_xattn_Wo': _L3_xattn_in['Wo'], 'L3_xattn_bo': _L3_xattn_in['bo'], 'L3_ffn_gate_w': _L3_ffn_in['gate_w'], 'L3_ffn_gate_b': _L3_ffn_in['gate_b'], 'L3_ffn_w1': _L3_ffn_in['w1'], 'L3_ffn_b1': _L3_ffn_in['b1'], 'L3_ffn_w2': _L3_ffn_in['w2'], 'L3_ffn_b2': _L3_ffn_in['b2']}

def reference(x, ctx_768, g_xattn, g_ffn, L0_xattn_W_d2v, L0_xattn_b_d2v, L0_xattn_W_img, L0_xattn_b_img, L0_xattn_W_txt, L0_xattn_b_txt, L0_xattn_W_att0, L0_xattn_b_att0, L0_xattn_W_att1, L0_xattn_b_att1, L0_xattn_W_f1, L0_xattn_b_f1, L0_xattn_W_f2, L0_xattn_b_f2, L0_ffn_w_gate, L0_ffn_w_up, L0_ffn_w_down, L1_xattn_W_Q, L1_xattn_W_K, L1_xattn_W_V, L1_xattn_W_O, L1_xattn_ln_lat_g, L1_xattn_ln_lat_b, L1_xattn_ln_in_g, L1_xattn_ln_in_b, L1_ffn_switch_w, L1_ffn_switch_b, L1_ffn_w1, L1_ffn_b1, L1_ffn_w2, L1_ffn_b2, L2_xattn_Wq, L2_xattn_bq, L2_xattn_Wk, L2_xattn_bk, L2_xattn_Wv, L2_xattn_bv, L2_xattn_Wo, L2_xattn_bo, L2_ffn_ln1_g, L2_ffn_ln1_b, L2_ffn_attn_w, L2_ffn_ln2_g, L2_ffn_ln2_b, L2_ffn_gate_w, L2_ffn_gate_proj, L2_ffn_up_proj, L2_ffn_down_proj, L3_xattn_Wq, L3_xattn_Wk, L3_xattn_Wv, L3_xattn_Wo, L3_xattn_bo, L3_ffn_gate_w, L3_ffn_gate_b, L3_ffn_w1, L3_ffn_b1, L3_ffn_w2, L3_ffn_b2):
    import jax
    import jax.numpy as jnp

    def _L0_xattn_ref(text_embeddings, dinov2_features, W_d2v, b_d2v, W_img, b_img, W_txt, b_txt, W_att0, b_att0, W_att1, b_att1, W_f1, b_f1, W_f2, b_f2):
        import jax, jax.numpy as jnp
        import numpy as np
        import math
        E = 128
        EV = 128
        FFN = 512
        DINO = 96
        B, S, P = (64, 64, 32)

        def bitnet_linear(x, W, b):
            w_scale = jnp.maximum(jnp.mean(jnp.abs(W)), 1e-05)
            qW = jnp.sign(W) * (jnp.abs(W) > 0.5 * w_scale).astype(W.dtype)
            i_scale = jnp.maximum(jnp.max(jnp.abs(x)), 1e-08) / 127.0
            qx = jnp.clip(jnp.round(x / i_scale), -128.0, 127.0)
            out = jnp.einsum('...i,oi->...o', qx, qW) * (w_scale * i_scale)
            return out + b
        b, s, e = text_embeddings.shape
        vis = bitnet_linear(dinov2_features, W_d2v, b_d2v)
        image_embeds = bitnet_linear(vis, W_img, b_img)
        fused = bitnet_linear(text_embeddings, W_txt, b_txt)
        inv_sqrt_e = 1.0 / math.sqrt(e)
        for Wa, ba in ((W_att0, b_att0), (W_att1, b_att1)):
            kv = bitnet_linear(image_embeds, Wa, ba)
            k = jnp.concatenate([kv, kv], axis=-1)
            scores = jnp.einsum('bse,bpe->bsp', fused, k) * inv_sqrt_e
            attn = jax.nn.softmax(scores, axis=-1)
            fused = fused + 0.1 * jnp.einsum('bsp,bpe->bse', attn, k)
        avg_img = jnp.mean(image_embeds, axis=1, keepdims=True)
        concatenated = jnp.concatenate([fused, jnp.broadcast_to(avg_img, (b, s, e))], axis=-1)
        h = jax.nn.relu(bitnet_linear(concatenated, W_f1, b_f1))
        return bitnet_linear(h, W_f2, b_f2)

    def _L0_ffn_ref(x, w_gate, w_up, w_down):
        import jax, jax.numpy as jnp
        import numpy as np
        BLOCK = 32
        W_BITS = 4
        ACT_BITS = 16

        def act_qdq(x):
            qmax = 2.0 ** (ACT_BITS - 1) - 1.0
            scale = jnp.maximum(jnp.max(jnp.abs(x)) / qmax, 1e-12)
            return jnp.clip(jnp.round(x / scale), -qmax - 1.0, qmax) * scale

        def fixed_qdq_u16(x):
            scale = 1.0 / 65536.0
            return jnp.clip(jnp.round(x / scale), 0.0, 65535.0) * scale

        def lpbq_dequant(w):
            O, I = w.shape
            qmax = 2.0 ** (W_BITS - 1) - 1.0
            wb = w.reshape(O, I // BLOCK, BLOCK)
            s = jnp.maximum(jnp.max(jnp.abs(wb), axis=-1, keepdims=True) / qmax, 1e-12)
            wq = jnp.clip(jnp.round(wb / s), -qmax - 1.0, qmax) * s
            return wq.reshape(O, I)
        x = act_qdq(x)
        up = act_qdq(x @ lpbq_dequant(w_up).T)
        gate = act_qdq(x @ lpbq_dequant(w_gate).T)
        sig = fixed_qdq_u16(jax.nn.sigmoid(gate))
        gate = act_qdq(gate * sig)
        o = act_qdq(gate * up)
        return o @ lpbq_dequant(w_down).T

    def _L1_xattn_ref(latent_q, input_kv, W_Q, W_K, W_V, W_O, ln_lat_g, ln_lat_b, ln_in_g, ln_in_b):
        import jax, jax.numpy as jnp
        import numpy as np
        LATENT_CH = 128
        INPUT_CH = 96
        QK_CH = 128
        V_CH = 128
        OUT_CH = 128
        NHEADS = 8
        EPS = 1e-05

        def layer_norm(x, gamma, beta):
            mu = jnp.mean(x, axis=-1, keepdims=True)
            var = jnp.var(x, axis=-1, keepdims=True)
            return (x - mu) * jax.lax.rsqrt(var + EPS) * gamma + beta
        B, Lq, _ = latent_q.shape
        _, Lkv, _ = input_kv.shape
        H = NHEADS
        dqk = QK_CH // H
        dv = V_CH // H
        lat = layer_norm(latent_q, ln_lat_g, ln_lat_b)
        inp = layer_norm(input_kv, ln_in_g, ln_in_b)
        Q = (lat @ W_Q).reshape(B, Lq, H, dqk)
        K = (inp @ W_K).reshape(B, Lkv, H, dqk)
        V = (inp @ W_V).reshape(B, Lkv, H, dv)
        scale = 1.0 / np.sqrt(dqk).astype(np.float32)
        attn = jnp.einsum('bqhd,bkhd->bhqk', Q, K) * scale
        attn = jax.nn.softmax(attn, axis=-1)
        out = jnp.einsum('bhqk,bkhd->bqhd', attn, V).reshape(B, Lq, V_CH)
        return out @ W_O

    def _L1_ffn_ref(x, switch_w, switch_b, w1, b1, w2, b2):
        import jax, jax.numpy as jnp
        import numpy as np
        B, S, D = (4, 256, 128)
        E, F = (8, 512)
        b, s, d = x.shape
        t = x.reshape(-1, d)
        logits = t @ switch_w + switch_b
        route_prob = jax.nn.softmax(logits, axis=-1)
        route_prob_max = jnp.max(route_prob, axis=-1)
        routes = jnp.argmax(route_prob, axis=-1)
        out = jnp.zeros_like(t)
        n_experts = w1.shape[0]
        for e in range(n_experts):
            h = jax.nn.gelu(t @ w1[e] + b1[e])
            y = h @ w2[e] + b2[e]
            mask = (routes == e)[:, None]
            out = jnp.where(mask, y, out)
        out = out * route_prob_max[:, None]
        return out.reshape(b, s, d)

    def _L2_xattn_ref(query, key_value, Wq, bq, Wk, bk, Wv, bv, Wo, bo):
        import jax, jax.numpy as jnp
        import numpy as np
        NUM_HEADS = 16
        CLAMP = 10000.0
        B, Nq, Cq = query.shape
        Nkv = key_value.shape[1]
        H = NUM_HEADS
        D = Cq // H
        scale = D ** (-0.5)
        q = (query @ Wq + bq).reshape(B, Nq, H, D).transpose(0, 2, 1, 3)
        k = (key_value @ Wk + bk).reshape(B, Nkv, H, D).transpose(0, 2, 1, 3)
        v = (key_value @ Wv + bv).reshape(B, Nkv, H, D).transpose(0, 2, 1, 3)
        attn = jnp.einsum('bhqd,bhkd->bhqk', q, k) * scale
        attn = jnp.clip(attn, -CLAMP, CLAMP)
        attn = jax.nn.softmax(attn, axis=-1)
        attn = jnp.where(jnp.any(jnp.isnan(attn)), jnp.asarray(1.0 / Nkv, attn.dtype), attn)
        x = jnp.einsum('bhqk,bhkd->bqhd', attn, v).reshape(B, Nq, Cq)
        return x @ Wo + bo

    def _L2_ffn_ref(x, ln1_g, ln1_b, attn_w, ln2_g, ln2_b, gate_w, gate_proj, up_proj, down_proj):
        import jax, jax.numpy as jnp
        import numpy as np
        HIDDEN = 128
        INTER = 512
        NUM_EXPERTS = 8
        TOP_K = 2
        EPS = 1e-05

        def _layer_norm(x, g, b):
            m = jnp.mean(x, axis=-1, keepdims=True)
            v = jnp.mean(jnp.square(x - m), axis=-1, keepdims=True)
            return (x - m) * jax.lax.rsqrt(v + EPS) * g + b
        B, S, H = x.shape
        h = x + jnp.einsum('bsh,oh->bso', _layer_norm(x, ln1_g, ln1_b), attn_w)
        t = _layer_norm(h, ln2_g, ln2_b).reshape(-1, H)
        T = t.shape[0]
        logits = jnp.einsum('th,eh->te', t, gate_w)
        top_vals, top_idx = jax.lax.top_k(logits, TOP_K)
        rw = jax.nn.softmax(top_vals, axis=-1)
        comb = jnp.zeros((T, NUM_EXPERTS), dtype=t.dtype)
        comb = comb.at[jnp.arange(T)[:, None], top_idx].add(rw)
        out = jnp.zeros_like(t)
        for e in range(NUM_EXPERTS):
            g = jnp.einsum('th,ih->ti', t, gate_proj[e])
            u = jnp.einsum('th,ih->ti', t, up_proj[e])
            oe = jnp.einsum('ti,hi->th', jax.nn.silu(g) * u, down_proj[e])
            out = out + comb[:, e:e + 1] * oe
        return h + out.reshape(B, S, H)

    def _L3_xattn_ref(x, context, Wq, Wk, Wv, Wo, bo):
        import jax, jax.numpy as jnp
        import numpy as np
        HEADS = 16
        DIM_HEAD = 64
        SCALE = DIM_HEAD ** (-0.5)
        QUERY_DIM = 128
        CONTEXT_DIM = 96
        INNER_DIM = HEADS * DIM_HEAD
        B, Nq, _ = x.shape
        Nk = context.shape[1]
        q = x @ Wq
        k = context @ Wk
        v = context @ Wv
        q = q.reshape(B, Nq, HEADS, DIM_HEAD).transpose(0, 2, 1, 3)
        k = k.reshape(B, Nk, HEADS, DIM_HEAD).transpose(0, 2, 1, 3)
        v = v.reshape(B, Nk, HEADS, DIM_HEAD).transpose(0, 2, 1, 3)
        sim = jnp.einsum('bhid,bhjd->bhij', q, k) * SCALE
        attn = jax.nn.softmax(sim, axis=-1)
        out = jnp.einsum('bhij,bhjd->bhid', attn, v)
        out = out.transpose(0, 2, 1, 3).reshape(B, Nq, INNER_DIM)
        return out @ Wo + bo

    def _L3_ffn_ref(x, gate_w, gate_b, w1, b1, w2, b2):
        import jax, jax.numpy as jnp
        import numpy as np
        B, S, H, F, E, K = (4, 256, 128, 512, 8, 2)
        Bb, Ss, Hh = x.shape
        xf = x.reshape(-1, Hh)
        gate = jax.nn.softmax(xf @ gate_w + gate_b)
        topv, topi = jax.lax.top_k(gate, K)
        topv = topv / topv.sum(-1, keepdims=True)
        combine = (jax.nn.one_hot(topi, gate.shape[-1], dtype=xf.dtype) * topv[..., None]).sum(1)

        def body(acc, p):
            w1e, b1e, w2e, b2e, ce = p
            h = jax.nn.relu(xf @ w1e + b1e)
            y = h @ w2e + b2e
            return (acc + y * ce[:, None], None)
        acc0 = jnp.zeros_like(xf)
        out, _ = jax.lax.scan(body, acc0, (w1, b1, w2, b2, combine.T))
        return out.reshape(Bb, Ss, Hh)
    x = x + jnp.tanh(g_xattn[0]) * _L0_xattn_ref(_layernorm(x, axis=-1), ctx_768, L0_xattn_W_d2v, L0_xattn_b_d2v, L0_xattn_W_img, L0_xattn_b_img, L0_xattn_W_txt, L0_xattn_b_txt, L0_xattn_W_att0, L0_xattn_b_att0, L0_xattn_W_att1, L0_xattn_b_att1, L0_xattn_W_f1, L0_xattn_b_f1, L0_xattn_W_f2, L0_xattn_b_f2)
    x = x + jnp.tanh(g_ffn[0]) * _L0_ffn_ref(_layernorm(x, axis=-1), L0_ffn_w_gate, L0_ffn_w_up, L0_ffn_w_down)
    x = x + jnp.tanh(g_xattn[1]) * _L1_xattn_ref(_layernorm(x, axis=-1), ctx_768, L1_xattn_W_Q, L1_xattn_W_K, L1_xattn_W_V, L1_xattn_W_O, L1_xattn_ln_lat_g, L1_xattn_ln_lat_b, L1_xattn_ln_in_g, L1_xattn_ln_in_b)
    x = x + jnp.tanh(g_ffn[1]) * _L1_ffn_ref(_layernorm(x, axis=-1), L1_ffn_switch_w, L1_ffn_switch_b, L1_ffn_w1, L1_ffn_b1, L1_ffn_w2, L1_ffn_b2)
    x = x + jnp.tanh(g_xattn[2]) * _L2_xattn_ref(_layernorm(x, axis=-1), ctx_768, L2_xattn_Wq, L2_xattn_bq, L2_xattn_Wk, L2_xattn_bk, L2_xattn_Wv, L2_xattn_bv, L2_xattn_Wo, L2_xattn_bo)
    x = x + jnp.tanh(g_ffn[2]) * _L2_ffn_ref(_layernorm(x, axis=-1), L2_ffn_ln1_g, L2_ffn_ln1_b, L2_ffn_attn_w, L2_ffn_ln2_g, L2_ffn_ln2_b, L2_ffn_gate_w, L2_ffn_gate_proj, L2_ffn_up_proj, L2_ffn_down_proj)
    x = x + jnp.tanh(g_xattn[3]) * _L3_xattn_ref(_layernorm(x, axis=-1), ctx_768, L3_xattn_Wq, L3_xattn_Wk, L3_xattn_Wv, L3_xattn_Wo, L3_xattn_bo)
    x = x + jnp.tanh(g_ffn[3]) * _L3_ffn_ref(_layernorm(x, axis=-1), L3_ffn_gate_w, L3_ffn_gate_b, L3_ffn_w1, L3_ffn_b1, L3_ffn_w2, L3_ffn_b2)
    return x

_drawn_inputs = setup_inputs


def setup_inputs(seed=0):
    import zlib

    import numpy as np

    out = dict(_drawn_inputs(seed))
    spreads = {'L0_xattn_b_d2v': (0.0, 0.1),
     'L0_xattn_b_img': (0.0, 0.1),
     'L0_xattn_b_txt': (0.0, 0.1),
     'L0_xattn_b_att0': (0.0, 0.1),
     'L0_xattn_b_att1': (0.0, 0.1),
     'L0_xattn_b_f1': (0.0, 0.1),
     'L0_xattn_b_f2': (0.0, 0.1),
     'L1_xattn_ln_lat_g': (1.0, 0.2),
     'L1_xattn_ln_lat_b': (0.0, 0.1),
     'L1_xattn_ln_in_g': (1.0, 0.2),
     'L1_xattn_ln_in_b': (0.0, 0.1),
     'L1_ffn_switch_b': (0.0, 0.1),
     'L1_ffn_b1': (0.0, 0.1),
     'L1_ffn_b2': (0.0, 0.1),
     'L2_xattn_bq': (0.0, 0.1),
     'L2_xattn_bk': (0.0, 0.8),
     'L2_xattn_bv': (0.0, 0.1),
     'L2_xattn_bo': (0.0, 0.1),
     'L2_ffn_ln1_g': (1.0, 0.2),
     'L2_ffn_ln1_b': (0.0, 0.1),
     'L2_ffn_ln2_g': (1.0, 0.6),
     'L2_ffn_ln2_b': (0.0, 0.411),
     'L3_xattn_bo': (0.0, 0.1),
     'L3_ffn_gate_b': (0.0, 0.1),
     'L3_ffn_b1': (0.0, 0.1),
     'L3_ffn_b2': (0.0, 0.1)}
    factors = {}
    for name, (base, spread) in spreads.items():
        noise = np.random.default_rng([zlib.crc32(name.encode()), seed]).standard_normal(out[name].shape)
        drawn = base * np.exp(spread * noise) if base else spread * noise
        out[name] = jnp.asarray(drawn.astype(out[name].dtype))
    for name, factor in factors.items():
        out[name] = (out[name] * factor).astype(out[name].dtype)
    return out
```

```python
from contextlib import ExitStack

import numpy as np

import concourse.bass as bass
from concourse import mybir

F32 = mybir.dt.float32
BF16 = mybir.dt.bfloat16
ALU = mybir.AluOpType
ACT = mybir.ActivationFunctionType
AX = mybir.AxisListType
RED = bass.bass_isa.ReduceOp

P = 128
B, S, D, C = 32, 64, 128, 96
T = B * S
NT = T // P
NG = B // 4
GT = 4 * S
CH = 512
NC = T // CH
E = 8
F = 512
NF = F // P
I0 = 384
NI = I0 // P
BLK = 32
EPS = 1e-5
MAGIC = 1.5 * 2.0 ** 23
UNITS = 4
LAYERS = 4


class Own:

    def __init__(self, eng, sem, default):
        self.eng, self.sem, self.default = eng, sem, default
        self.base, self.n, self.pending = {}, {}, []

    def __call__(self, ins, name=None, by=1):
        name = name or self.default
        ins.then_inc(self.sem(name), by)
        self.add(name, by)
        return ins

    def add(self, name, by):
        self.n[name] = self.n.get(name, 0) + by
        if name not in self.pending:
            self.pending.append(name)

    def wait(self):
        for name in self.pending:
            self.eng.wait_ge(self.sem(name), self.base.get(name, 0) + self.n[name])
        self.pending = []

    def enter(self, i, steps):
        self.outer, self.steps = dict(self.n), steps
        for name, k in steps.items():
            self.base[name] = self.n.get(name, 0) + i * k
            self.n[name] = 0

    def leave(self, turns):
        for name, k in self.steps.items():
            assert self.n[name] == k, (name, self.n[name], k)
            self.n[name] = self.outer.get(name, 0) + turns * k
        self.base, self.pending = {}, list(self.steps)


def flamingo_kernel(nc, a, out, last=2 * LAYERS):
    ctx = ExitStack()
    with ctx:
        def sb(name, shape, dt=F32):
            return ctx.enter_context(nc.sbuf_tensor(name, shape, dt))

        sems = {}

        def sem(name):
            if name not in sems:
                sems[name] = ctx.enter_context(nc.semaphore(name))
            return sems[name]

        ps = ctx.enter_context(nc.psum_tensor("ps", [P, 8, CH], F32))

        ident = sb("ident", [P, P])
        identb = sb("identb", [P, P], BF16)
        ones = sb("ones", [1, P])
        headmask = {1: sb("headmask1", [P, 2]), 2: sb("headmask2", [P, 4])}
        gates = sb("gates", [P, 8])
        invcount = sb("invcount", [P, 7])
        rank = sb("rank", [P, E])

        x = sb("x", [P, NT, D])
        xh = sb("xh", [P, NT, D])
        xnT = sb("xnT", [P, T])
        ctxT = sb("ctxT", [C, T])
        ctxnT = sb("ctxnT", [C, T])
        bst = sb("bst", [P, NT, 6])
        mv = sb("mv", [P, NT, 2])
        st1 = sb("st1", [P, NT])
        st2 = sb("st2", [P, NT])
        rstd = sb("rstd", [P, NT])
        rstd2 = sb("rstd2", [P, NT])

        arena = sb("arena", [P, 22528])
        def view(lo, n, p=P):
            return arena[0:p, lo:lo + n]

        W0 = [("d2v", 0, 96), ("img", 96, 128), ("txt", 224, 128), ("att0", 352, 128), ("att1", 480, 128),
              ("f1", 608, 1024), ("f2", 1632, 512)]
        COUNT0 = [P * C, P * P, P * P, P * P, P * P, 512 * 256, 512 * P]
        w0 = sb("w0", [P, 2144])
        q0 = sb("q0", [P, 2144], BF16)
        q0T = sb("q0T", [P, 17, P], BF16)
        wsum = sb("wsum", [P, 7])
        wtot = sb("wtot", [P, 7])
        wscale = sb("wscale", [P, 7])
        whalf = sb("whalf", [P, 7])
        wnhalf = sb("wnhalf", [P, 7])
        bias0 = sb("bias0", [P, 9])
        batt = sb("batt", [P, 2, P])
        bf2 = sb("bf2", [P, P])
        amax = sb("amax", [P, 16])
        amaxp = sb("amaxp", [P, 1])
        amaxg = sb("amaxg", [P, 1])
        iscale = sb("iscale", [P, 1])
        irecip = sb("irecip", [P, 1])
        oscale = sb("oscale", [P, 4])
        wff = sb("wff", [P, 9, P])
        wffs = sb("wffs", [P, 36])
        wffr = sb("wffr", [P, 36])
        wffT = sb("wffT", [P, 9, P])

        WIN = {1: P, 2: P, 3: 1024}
        HEADS = {1: 8, 2: 16, 3: 16}
        wq = {l: sb(f"wq{l}", [P, WIN[l]]) for l in (1, 2, 3)}
        wk = {l: sb(f"wk{l}", [C, WIN[l]]) for l in (1, 2, 3)}
        wv = {l: sb(f"wv{l}", [C, WIN[l]]) for l in (1, 2, 3)}
        wo = {1: sb("wo1", [P, 1, P]), 2: sb("wo2", [P, 1, P]), 3: sb("wo3", [P, 8, P])}
        bqk = sb("bqk", [P, 2])
        rows = sb("rows", [1, 3, P])
        lng = sb("lng", [P, 8])
        gw = {1: sb("gw1", [P, E]), 2: sb("gw2", [P, E]), 3: sb("gw3", [P, E])}
        gwn = sb("gwn", [E, P])
        gb = sb("gb", [1, 2, E])
        attw = sb("attw", [P, P])
        attwT = sb("attwT", [P, P])
        b1 = {1: sb("b1_1", [P, E, NF]), 3: sb("b1_3", [P, E, NF])}
        wexp = sb("wexp", [P, 2, 12, P])
        b2 = sb("b2", [1, 2, P])
        b1s = sb("b1s", [P, 2, NF])
        comb = sb("comb", [P, NT, E])
        lg = sb("lg", [P, NT, E])
        oh1 = sb("oh1", [P, NT, E])
        oh2 = sb("oh2", [P, NT, E])
        tmpe = sb("tmpe", [P, NT, E])
        v1 = sb("v1", [P, NT])
        v2 = sb("v2", [P, NT])
        v3 = sb("v3", [P, NT])

        loads = {}
        block = ctx.enter_context(nc.Block())

        def expert_loads(l):
            if l == 1:
                w1, w2 = a["L1_ffn_w1"], a["L1_ffn_w2"]
            elif l == 3:
                w1, w2 = a["L3_ffn_w1"], a["L3_ffn_w2"]
            if l in (1, 3):
                return [(w1, 0, lambda s: s.rearrange("e k (f n) -> k e f n", n=P)),
                        (w2, 4, lambda s: s.rearrange("e (f k) n -> k e f n", k=P))]
            return [(a["L2_ffn_gate_proj"], 0, lambda s: s.rearrange("e (f k) n -> k e f n", k=P)),
                    (a["L2_ffn_up_proj"], 4, lambda s: s.rearrange("e (f k) n -> k e f n", k=P)),
                    (a["L2_ffn_down_proj"], 8, lambda s: s.rearrange("e k (f n) -> k e f n", n=P))]

        N_LOADS = {1: 3, 2: 3, 3: 3}

        @block.sync
        def _(sp):
            def load(dst, src, s):
                loads[s.name] = loads.get(s.name, 0) + 1
                sp.dma_start(dst, src, allow_slow_non_contiguous=True).then_inc(s, 16)

            xr = a["x"].rearrange("b s d -> (b s) d").rearrange("(j p) d -> p j d", p=P)
            cr = a["ctx_768"].rearrange("b s d -> (b s) d").rearrange("(j p) d -> p j d", p=P)
            load(x[:, :, :], xr, sem("loaded_x"))
            load(view(0, NT * C).rearrange("p (j d) -> p j d", d=C), cr, sem("loaded_ctx"))
            w = sem("loaded_w0")
            load(w0[:, 0:96], a["L0_xattn_W_d2v"], w)
            load(w0[:, 96:224], a["L0_xattn_W_img"], w)
            load(w0[:, 224:352], a["L0_xattn_W_txt"], w)
            for i, nm in enumerate(("L0_xattn_W_att0", "L0_xattn_W_att1")):
                for h in range(2):
                    load(w0[64 * h:64 * h + 64, 352 + 128 * i:480 + 128 * i], a[nm], w)
            load(w0[:, 608:1632].rearrange("p (c n) -> p c n", c=4),
                 a["L0_xattn_W_f1"].rearrange("(c p) n -> p c n", p=P), w)
            load(w0[:, 1632:2144], a["L0_xattn_W_f2"], w)

            def col(v):
                return v.rearrange("(p o) -> p o", o=1)
            for i, nm in enumerate(("b_d2v", "b_img", "b_txt")):
                load(bias0[:, i:i + 1], col(a["L0_xattn_" + nm]), w)
            for i, nm in enumerate(("L0_xattn_b_att0", "L0_xattn_b_att1")):
                for h in range(2):
                    load(bias0[64 * h:64 * h + 64, 3 + i:4 + i], col(a[nm]), w)
                    load(batt[:, i, 64 * h:64 * h + 64], a[nm].rearrange("(o n) -> o n", o=1).partition_broadcast(P), w)
            load(bias0[:, 5:9], a["L0_xattn_b_f1"].rearrange("(f p) -> p f", p=P), w)
            load(bf2[:, :], a["L0_xattn_b_f2"].rearrange("(o n) -> o n", o=1).partition_broadcast(P), w)
            load(gates[:, 0:4], a["g_xattn"].rearrange("(o n) -> o n", o=1).partition_broadcast(P), w)
            load(gates[:, 4:8], a["g_ffn"].rearrange("(o n) -> o n", o=1).partition_broadcast(P), w)
            for i, nm in enumerate(("w_gate", "w_up")):
                load(wff[:, 3 * i:3 * i + 3, :], a["L0_ffn_" + nm].rearrange("(c p) n -> p c n", p=P), sem("loaded_wff"))
            load(wff[:, 6:9, :], a["L0_ffn_w_down"].rearrange("p (c n) -> p c n", c=3), sem("loaded_wff"))
            r = sem("loaded_rest")
            load(wq[1][:, :], a["L1_xattn_W_Q"], r)
            load(wk[1][:, :], a["L1_xattn_W_K"], r)
            load(wv[1][:, :], a["L1_xattn_W_V"], r)
            load(wo[1][:, 0, :], a["L1_xattn_W_O"], r)
            for i, nm in enumerate(("L1_xattn_ln_lat_g", "L1_xattn_ln_lat_b")):
                load(lng[:, i:i + 1], col(a[nm]), r)
            for i, nm in enumerate(("L1_xattn_ln_in_g", "L1_xattn_ln_in_b")):
                load(lng[0:C, 2 + i:3 + i], col(a[nm]), r)
            for i, nm in enumerate(("ln1_g", "ln1_b", "ln2_g", "ln2_b")):
                load(lng[:, 4 + i:5 + i], col(a["L2_ffn_" + nm]), r)
            for l in (2, 3):
                load(wq[l][:, :], a[f"L{l}_xattn_Wq"], r)
                load(wk[l][:, :], a[f"L{l}_xattn_Wk"], r)
                load(wv[l][:, :], a[f"L{l}_xattn_Wv"], r)
                load(wo[l][:, :, :], a[f"L{l}_xattn_Wo"].rearrange("(c p) n -> p c n", p=P), r)
            load(bqk[:, 0:1], col(a["L2_xattn_bq"]), r)
            load(bqk[:, 1:2], col(a["L2_xattn_bk"]), r)
            row = lambda v: v.rearrange("(o n) -> o n", o=1)
            load(rows[:, 0, :], row(a["L2_xattn_bv"]), r)
            load(rows[:, 1, :], row(a["L2_xattn_bo"]), r)
            load(rows[:, 2, :], row(a["L3_xattn_bo"]), r)
            load(gw[1][:, :], a["L1_ffn_switch_w"], r)
            load(gw[3][:, :], a["L3_ffn_gate_w"], r)
            load(gwn[:, :], a["L2_ffn_gate_w"], r)
            load(gb[:, 0, :], row(a["L1_ffn_switch_b"]), r)
            load(gb[:, 1, :], row(a["L3_ffn_gate_b"]), r)
            load(attw[:, :], a["L2_ffn_attn_w"], r)
            for l in (1, 3):
                load(b1[l][:, :, :], a[f"L{l}_ffn_b1"].rearrange("e (f p) -> p e f", p=P), r)

            for l in (1, 2, 3):
                if last < 2 * l + 2:
                    continue
                srcs = expert_loads(l)

                def load_expert(e, slot):
                    for src, lo, to in srcs:
                        load(wexp[:, slot, lo:lo + NF, :], to(src)[:, bass.ds(e, 1), :, :].rearrange("k e f n -> k (e f) n"), sem(f"loaded_expert{slot}"))
                    if l != 2:
                        load(b2[:, slot, :], a[f"L{l}_ffn_b2"][bass.ds(e, 1), :], sem(f"loaded_expert{slot}"))
                if l > 1:
                    sp.wait_ge(sem(f"y_mm_e{l - 1}"), E * NC + 2)
                load_expert(0, 0)
                load_expert(1, 1)
                with sp.Fori(1, E // 2) as i:
                    for slot in range(2):
                        sp.wait_ge(sem(f"y_mm_e{l}"), 2 * NC * i + (NC * (slot - 1) + 2))
                        load_expert(2 * i + slot, slot)
            sp.wait_ge(sem("x_final"), 1)
            sp.dma_start(out.rearrange("b s d -> (b s) d").rearrange("(j p) d -> p j d", p=P), x[:, :, :]).then_inc(sem("stored"), 16)
            sp.wait_ge(sem("stored"), 16)

        N_W0, N_REST = loads[sem("loaded_w0").name], loads[sem("loaded_rest").name]

        ctok = view(0, NT * C).rearrange("p (j d) -> p j d", d=C)
        qctx = view(1536, 768).bitcast(BF16).rearrange("p (j d) -> p j d", d=C)
        rnd = view(2304, 2048)
        qT = view(4352, 1024).bitcast(BF16)
        qtok = view(5376, 1024).bitcast(BF16).rearrange("p (j d) -> p j d", d=D)
        act0 = view(6400, 2048)
        fused = view(8448, 2048)
        kT = [view(10496 + 2048 * i, 2048) for i in range(2)]
        ktok = [view(14592 + 2048 * i, 2048).rearrange("p (j d) -> p j d", d=D) for i in range(2)]
        prob = view(18688, 1024)
        probT = view(19712, 1024).rearrange("p (g n) -> p g n", g=NG)
        avg = view(20736, B)
        qavg = view(20768, B // 2).bitcast(BF16)
        smax = view(20784, 16)
        ssum = view(20800, 16)
        srec = view(20816, 16)
        h0 = view(10496, 8192).rearrange("p (f t) -> p f t", f=NF)
        qh = view(0, 4096).bitcast(BF16).rearrange("p (f t) -> p f t", f=NF)
        up0 = view(0, NI * T).rearrange("p (f t) -> p f t", f=NI)
        gate0 = view(6144, NI * T).rearrange("p (f t) -> p f t", f=NI)
        sig0 = view(12288, NI * T).rearrange("p (f t) -> p f t", f=NI)

        ctxs = view(0, GT, C)
        def att(l):
            w = WIN[l]
            o = 256
            d = {}
            d["q"] = view(o, w // P * GT).rearrange("p (c t) -> p c t", t=GT)
            o += 2048
            n = 8 if l == 3 else 128 // HEADS[l] and (32 // (P // HEADS[l]))
            d["k"] = view(o, n * GT).rearrange("p (c t) -> p c t", t=GT)
            o += 2048
            d["v"] = view(o, 2 * w).rearrange("p (h n) -> p h n", h=2)
            o += 2048
            d["p"] = view(o, 2048).rearrange("p (u n) -> p u n", u=4)
            o += 2048
            d["pt"] = view(o, 1024).rearrange("p (u h n) -> p u h n", u=2, n=P)
            o += 1024
            d["o"] = view(o, 2048)
            o += 2048
            d["ot"] = view(o, 256)
            o += 256
            d["max"], d["sum"], d["rec"] = (view(o + 32 * k, 32).rearrange("p (u n) -> p u n", u=4) for k in range(3))
            return d

        hT = view(0, 4096).rearrange("p (u f t) -> p u f t", u=2, f=NF)
        sg = view(4096, 1024).rearrange("p (u t) -> p u t", u=2)
        wexpT = view(8192, 2 * 12 * P).rearrange("p (u f n) -> p u f n", u=2, f=12)
        hres = view(12288, 2048).rearrange("p (j d) -> p j d", d=D)

        NSUB = {1: 2, 2: 4}
        SCALE = {0: 128.0 ** -0.5, 1: 0.25, 2: 8.0 ** -0.5, 3: 0.125}
        CLAMP = 10000.0 / SCALE[2]

        SQRTS = {"one": 1, "two": 2, "both": 2}
        norms = []
        plan = [("one", "ctx"), ("one", "x")]
        if last >= 2: plan += [("one", "x")]
        if last >= 3: plan += [("two", "x")]
        if last >= 4: plan += [("one", "x")]
        if last >= 5: plan += [("one", "x")]
        if last >= 6: plan += [("both", "x"), ("one", "h")]
        if last >= 7: plan += [("one", "x")]
        if last >= 8: plan += [("one", "x")]
        sq_before = [sum(SQRTS[k] for k, _ in plan[:i]) for i in range(len(plan) + 1)]

        @block.gpsimd
        def _(g):
            own = Own(g, sem, "gp_own")
            own(g.memset(ident[:, :], 0.0))
            own(g.memset(ones[:, :], 1.0))
            for i, n in ((0, COUNT0[0]), (1, COUNT0[1]), (5, COUNT0[5]), (6, COUNT0[6])):
                w = 4 if i == 1 else 1
                own(g.memset(invcount[:, i:i + w], 1.0 / n))
            for e in range(E):
                own(g.memset(rank[:, e:e + 1], float(E - e)))
            own.wait()
            own(g.affine_select(out=ident[:, :], in_=ident[:, :], compare_op=ALU.not_equal, fill=1.0, base=0,
                                pattern=[[-1, P]], channel_multiplier=1))
            own.wait()
            own(g.tensor_copy(identb[:, :], ident[:, :]), "constants")

            def sum_rows():
                g.wait_ge(sem("wsum_ready"), 1)
                g.partition_all_reduce(wtot[:, :], wsum[:, :], P, RED.add).then_inc(sem("wtot_ready"), 1)

            sum_rows()
            n_max = 6 + (5 if last >= 2 else 0)
            for k in range(n_max):
                g.wait_ge(sem("amaxp_ready"), k + 1)
                g.partition_all_reduce(amaxg[:, :], amaxp[:, :], P, RED.max).then_inc(sem("amaxg_ready"), 1)

            for l in (1, 2, 3):
                if last < 2 * l + 1:
                    continue
                src = ctxnT if l == 1 else ctxT
                g.wait_ge(sem("norm_feature"), NC * (3 if l == 1 else 1) + 0)
                g.wait_ge(sem(f"att_open_{l}"), 1)
                with g.Fori(0, NG) as i:
                    g.wait_ge(sem(f"v_mm_{l}"), 4 * i + 4 if l == 3 else i + 1)
                    g.tensor_copy(ctxs[:, :], src[:, bass.ds(i * GT, GT)]).then_inc(sem(f"ctx_staged_{l}"), 1)

        @block.vector
        def _(v):
            own = Own(v, sem, "vec_own")
            k_norm = [0]
            k_max = [0]

            def normalise(src, width, kind, outs, then=None):
                for j in range(NT):
                    own(v.bn_stats(bst[:, j, :], src[:, j, :]))
                own.wait()
                for j in range(NT):
                    own(v.bn_aggr(mv[:, j, :], bst[:, j, :]))
                own.wait()
                k = sq_before[k_norm[0]]
                v.tensor_scalar(st1[:, :], mv[:, :, 1], EPS, None, ALU.add).then_inc(sem("var_ready"), 1)
                v.wait_ge(sem("sd_ready"), k + 1)
                own(v.reciprocal(rstd[:, :], st2[:, :]))
                own.wait()
                last_r = rstd
                if kind != "one":
                    own(v.tensor_tensor(rstd2[:, :], rstd[:, :], rstd[:, :], ALU.mult))
                    own.wait()
                    own(v.tensor_tensor(rstd2[:, :], rstd2[:, :], mv[:, :, 1], ALU.mult))
                    own.wait()
                    v.tensor_scalar(st1[:, :], rstd2[:, :], EPS, None, ALU.add).then_inc(sem("var_ready"), 1)
                    v.wait_ge(sem("sd_ready"), k + 2)
                    own(v.reciprocal(rstd2[:, :], st2[:, :]))
                    own.wait()
                    own(v.tensor_tensor(rstd2[:, :], rstd2[:, :], rstd[:, :], ALU.mult))
                    own.wait()
                    last_r = rstd2
                for j in range(NT):
                    if kind == "both":
                        own(v.tensor_scalar(outs[1][:, j, :], src[:, j, :], mv[:, j, 0:1], rstd[:, j:j + 1],
                                            ALU.subtract, ALU.mult))
                    v.tensor_scalar(outs[0][:, j, :], src[:, j, :], mv[:, j, 0:1], last_r[:, j:j + 1],
                                    ALU.subtract, ALU.mult).then_inc(sem("norm_ready"), 1)
                k_norm[0] += 1

            def scale_from(parts, floor, levels):
                own.wait()
                v.tensor_reduce(amaxp[:, :], parts, AX.X, ALU.max, apply_absolute_value=True).then_inc(sem("amaxp_ready"), 1)
                k_max[0] += 1
                v.wait_ge(sem("amaxg_ready"), k_max[0])
                if floor == 1e-8:
                    own(v.tensor_scalar(iscale[:, :], amaxg[:, :], floor, 1.0 / levels, ALU.max, ALU.mult))
                else:
                    own(v.tensor_scalar(iscale[:, :], amaxg[:, :], 1.0 / levels, floor, ALU.mult, ALU.max))
                own.wait()
                own(v.reciprocal(irecip[:, :], iscale[:, :]))
                own.wait()

            def quantise(dst, src, scratch):
                own(v.tensor_scalar(scratch, src, irecip[:, 0:1], MAGIC, ALU.mult, ALU.add))
                own.wait()
                own(v.tensor_scalar(dst, scratch, MAGIC, None, ALU.subtract))

            def out_scale(i, w):
                own(v.tensor_tensor(oscale[:, i:i + 1], iscale[:, :], wscale[:, w:w + 1], ALU.mult))

            v.wait_ge(sem("constants"), 1)
            for l, n in ((1, 2), (2, 4)):
                own(v.tensor_reduce(headmask[l][:, :], ident[:, :].rearrange("p (a j d) -> p j a d", a=4, j=n),
                                    AX.XY, ALU.add))
            v.wait_ge(sem("loaded_w0"), 16 * N_W0)
            for i, (_, lo, n) in enumerate(W0):
                ins = v.tensor_reduce(wsum[:, i:i + 1], w0[:, lo:lo + n], AX.X, ALU.add, apply_absolute_value=True)
                own(ins)
            own.wait()
            v.sem_inc(sem("wsum_ready"), 1)
            v.wait_ge(sem("wtot_ready"), 1)
            own(v.tensor_tensor(wscale[:, :], wtot[:, :], invcount[:, :], ALU.mult))
            own.wait()
            own(v.tensor_scalar(wscale[:, :], wscale[:, :], 1e-5, None, ALU.max))
            own.wait()
            own(v.tensor_scalar(whalf[:, :], wscale[:, :], 0.5, None, ALU.mult))
            own(v.tensor_scalar(wnhalf[:, :], wscale[:, :], -0.5, None, ALU.mult))
            own.wait()
            for i, (_, lo, n) in enumerate(W0):
                own(v.tensor_scalar(rnd[:, 0:n], w0[:, lo:lo + n], wnhalf[:, i:i + 1], None, ALU.is_lt))
                own.wait()
                own(v.scalar_tensor_tensor(q0[:, lo:lo + n], w0[:, lo:lo + n], whalf[:, i:i + 1], rnd[:, 0:n],
                                           ALU.is_gt, ALU.subtract))
                own.wait()
            v.sem_inc(sem("q0_ready"), 1)

            v.wait_ge(sem("loaded_wff"), 48)
            wb = wff[:, :, :].rearrange("p c (k i) -> p (c k) i", i=BLK)
            own(v.tensor_reduce(wffs[:, :], wb, AX.X, ALU.max, apply_absolute_value=True))
            own.wait()
            own(v.tensor_scalar(wffs[:, :], wffs[:, :], 1.0 / 7.0, 1e-12, ALU.mult, ALU.max))
            own.wait()
            own(v.reciprocal(wffr[:, :], wffs[:, :]))
            own.wait()
            own(v.tensor_tensor(wb, wb, wffr[:, :].unsqueeze(2).to_broadcast([P, 36, BLK]), ALU.mult))
            own.wait()
            wflat = wff[:, :, :].rearrange("p c n -> p (c n)")
            own(v.tensor_scalar(wflat, wflat, MAGIC, MAGIC, ALU.add, ALU.subtract))
            own.wait()
            own(v.tensor_tensor(wb, wb, wffs[:, :].unsqueeze(2).to_broadcast([P, 36, BLK]), ALU.mult))
            own.wait()
            v.sem_inc(sem("wff_ready"), 1)

            v.wait_ge(sem("loaded_ctx"), 16)
            own(v.tensor_reduce(amax[:, 0:1], ctok[:, :, :], AX.XY, ALU.max, apply_absolute_value=True))
            scale_from(amax[:, 0:1], 1e-8, 127.0)
            quantise(view(1536, 768).bitcast(BF16), view(0, NT * C), rnd[:, 0:NT * C])
            out_scale(0, 0)
            own.wait()
            v.sem_inc(sem("qctx_ready"), 1)
            xhc = xh[:, :, 0:C]
            normalise(ctok, C, "one", [xhc])

            v.wait_ge(sem("loaded_x"), 16)
            v.wait_ge(sem("norm_feature"), 3 * NC)
            normalise(x, D, "one", [xh])
            v.wait_ge(sem("norm_ready"), 2 * NT)
            own(v.tensor_reduce(amax[:, 0:1], xh[:, :, :], AX.XY, ALU.max, apply_absolute_value=True))
            scale_from(amax[:, 0:1], 1e-8, 127.0)
            quantise(view(5376, 1024).bitcast(BF16), xh[:, :, :].rearrange("p j d -> p (j d)"), rnd)
            out_scale(1, 2)
            own.wait()
            v.sem_inc(sem("qtok_ready"), 1)

            def chunk_maxima(buf, name, base=0, n=NC):
                for c in range(n):
                    v.wait_ge(sem(name), base + c + 1)
                    own(v.tensor_reduce(amax[:, c:c + 1], buf(c), AX.X, ALU.max, apply_absolute_value=True))

            v.wait_ge(sem("lin0"), 2 * NC)
            chunk_maxima(lambda c: act0[:, CH * c:CH * c + CH], "act0_ready", NC)
            scale_from(amax[:, 0:NC], 1e-8, 127.0)
            quantise(qT, act0, rnd)
            out_scale(2, 1)
            own.wait()
            v.sem_inc(sem("qT_ready"), 1)
            chunk_maxima(lambda c: act0[:, CH * c:CH * c + CH], "act0_ready", 2 * NC)
            scale_from(amax[:, 0:NC], 1e-8, 127.0)
            own(v.tensor_reduce(avg[:, :], act0.rearrange("p (b s) -> p b s", s=S), AX.X, ALU.add))
            quantise(qT, act0, rnd)
            out_scale(3, 3)
            out_scale(0, 4)
            own.wait()
            own(v.tensor_scalar(avg[:, :], avg[:, :], 1.0 / S, None, ALU.mult))
            own.wait()
            v.sem_inc(sem("qT_ready"), 1)
            for r in range(2):
                for c in range(NC):
                    v.wait_ge(sem("ktok_mm"), NC * r + c + 1)
                    own(v.scalar_tensor_tensor(
                        ktok[r][:, 4 * c:4 * c + 4, :], ps[:, 4 + c, :].rearrange("p (j d) -> p j d", d=D),
                        oscale[:, 3:4] if r == 0 else oscale[:, 0:1],
                        batt[:, r, :].unsqueeze(1).to_broadcast([P, 4, P]), ALU.mult, ALU.add
                    ), "ktok_ready")

            for r in range(2):
                for u in range(2):
                    lo = 8 * u
                    sp_ = ps[:, u, :].rearrange("p (n s) -> p n s", s=S)
                    pr = prob[:, 512 * u:512 * u + 512].rearrange("p (n s) -> p n s", s=S)
                    v.wait_ge(sem("s0_mm"), 2 * r + u + 1)
                    own(v.tensor_reduce(smax[:, lo:lo + 8], sp_, AX.X, ALU.max))
                    own.wait()
                    v.tensor_tensor(pr, sp_, smax[:, lo:lo + 8].unsqueeze(2).to_broadcast([P, 8, S]),
                                    ALU.subtract).then_inc(sem("s0_sub"), 1)
                for u in range(2):
                    lo = 8 * u
                    pr = prob[:, 512 * u:512 * u + 512].rearrange("p (n s) -> p n s", s=S)
                    v.wait_ge(sem("s0_exp"), 2 * r + u + 1)
                    own(v.tensor_reduce(ssum[:, lo:lo + 8], pr, AX.X, ALU.add))
                    own.wait()
                    own(v.reciprocal(srec[:, lo:lo + 8], ssum[:, lo:lo + 8]))
                    own.wait()
                    v.tensor_tensor(pr, pr, srec[:, lo:lo + 8].unsqueeze(2).to_broadcast([P, 8, S]),
                                    ALU.mult).then_inc(sem("s0_prob"), 1)
                fv = fused.rearrange("p (u n c s) -> p u c n s", u=2, c=2, s=S)
                for u in range(2):
                    for c in range(2):
                        v.wait_ge(sem("av0_mm"), 4 * r + 2 * u + c + 1)
                        own(v.scalar_tensor_tensor(fv[:, u, c], ps[:, 4 + 2 * u + c, :].rearrange("p (n s) -> p n s", s=S),
                                                   0.1, fv[:, u, c], ALU.mult, ALU.add), "fused_ready")
            own.wait()
            own(v.tensor_reduce(amax[:, 0:1], fused, AX.X, ALU.max, apply_absolute_value=True))
            own(v.tensor_reduce(amax[:, 1:2], avg, AX.X, ALU.max, apply_absolute_value=True))
            scale_from(amax[:, 0:2], 1e-8, 127.0)
            quantise(qT, fused, rnd)
            own.wait()
            quantise(qavg, avg, rnd[:, 0:B])
            out_scale(1, 5)
            own.wait()
            v.sem_inc(sem("qT_ready"), 1)
            for n in range(NF * NC):
                f, c = n // NC, n % NC
                v.wait_ge(sem("h0_ready"), n + 1)
                own(v.tensor_reduce(amax[:, n:n + 1], h0[:, f, CH * c:CH * c + CH], AX.X, ALU.max,
                                    apply_absolute_value=True))
            v.wait_ge(sem("gates_ready"), 1)
            own(v.scalar_tensor_tensor(x[:, :, :], bf2[:, :].unsqueeze(1).to_broadcast([P, NT, P]), gates[:, 0:1],
                                       x[:, :, :], ALU.mult, ALU.add))
            scale_from(amax[:, 0:16], 1e-8, 127.0)
            out_scale(2, 6)
            own.wait()
            own(v.tensor_tensor(oscale[:, 2:3], oscale[:, 2:3], gates[:, 0:1], ALU.mult))
            for f in range(NF):
                own.wait()
                own(v.tensor_scalar(h0[:, f, :], h0[:, f, :], irecip[:, 0:1], MAGIC, ALU.mult, ALU.add))
                own.wait()
                v.tensor_scalar(qh[:, f, :], h0[:, f, :], MAGIC, None, ALU.subtract).then_inc(sem("qh_ready"), 1)

            def add_tiles(name, scalar, banks=(0, 1), base=0):
                for c in range(NC):
                    v.wait_ge(sem(name), c + 1)
                    own(v.scalar_tensor_tensor(x[:, 4 * c:4 * c + 4, :],
                                               ps[:, banks[c % 2], :].rearrange("p (j d) -> p j d", d=D), scalar,
                                               x[:, 4 * c:4 * c + 4, :], ALU.mult, ALU.add), name + "_used")
                own.wait()
            add_tiles("f2_mm", oscale[:, 2:3])

            def finish():
                own.wait()
                v.sem_inc(sem("x_final"), 1)
            if last == 1:
                return finish()

            normalise(x, D, "one", [xh])
            v.wait_ge(sem("norm_ready"), 3 * NT)
            own(v.tensor_reduce(amax[:, 0:1], xh[:, :, :], AX.XY, ALU.max, apply_absolute_value=True))
            scale_from(amax[:, 0:1], 1e-12, 32767.0)
            xf = xh[:, :, :].rearrange("p j d -> p (j d)")

            def requantise(buf, name=None):
                own(v.tensor_scalar(buf, buf, irecip[:, 0:1], MAGIC, ALU.mult, ALU.add))
                own.wait()
                own(v.tensor_scalar(buf, buf, MAGIC, iscale[:, 0:1], ALU.subtract, ALU.mult), name)
            requantise(xf)
            own.wait()
            v.sem_inc(sem("xq_ready"), 1)
            flat = lambda b: b[:, :, :].rearrange("p f t -> p (f t)")
            for w, buf in ((0, gate0), (1, up0)):
                for n in range(NI * NC):
                    f, c = n // NC, n % NC
                    v.wait_ge(sem("gu_ready"), NI * NC * w + n + 1)
                    own(v.tensor_reduce(amax[:, n:n + 1], buf[:, f, CH * c:CH * c + CH], AX.X, ALU.max,
                                        apply_absolute_value=True))
                scale_from(amax[:, 0:NI * NC], 1e-12, 32767.0)
                for f in range(NI):
                    requantise(buf[:, f, :], "gu_quant")
                own.wait()
            for f in range(NI):
                v.wait_ge(sem("sig_ready"), f + 1)
                own(v.tensor_scalar(sig0[:, f, :], sig0[:, f, :], 65536.0, MAGIC, ALU.mult, ALU.add))
                own.wait()
                own(v.tensor_scalar(sig0[:, f, :], sig0[:, f, :], MAGIC, 65535.0, ALU.subtract, ALU.min))
                own.wait()
                own(v.scalar_tensor_tensor(gate0[:, f, :], sig0[:, f, :], 1.0 / 65536.0, gate0[:, f, :],
                                           ALU.mult, ALU.mult))
                own.wait()
                own(v.tensor_reduce(amax[:, f:f + 1], gate0[:, f, :], AX.X, ALU.max, apply_absolute_value=True))
            scale_from(amax[:, 0:NI], 1e-12, 32767.0)
            for f in range(NI):
                requantise(gate0[:, f, :])
                own.wait()
                own(v.tensor_tensor(gate0[:, f, :], gate0[:, f, :], up0[:, f, :], ALU.mult))
                own.wait()
                own(v.tensor_reduce(amax[:, f:f + 1], gate0[:, f, :], AX.X, ALU.max, apply_absolute_value=True))
            scale_from(amax[:, 0:NI], 1e-12, 32767.0)
            for f in range(NI):
                requantise(gate0[:, f, :])
            own.wait()
            v.sem_inc(sem("o_ready"), 1)
            add_tiles("down_mm", gates[:, 4:5])
            if last == 2:
                return finish()

            def attention(l):
                t = att(l)
                sub = 4 if l != 1 else 2
                w = S * sub * 2
                n_k = 4 if l == 3 else NSUB[l]
                steps = {"vec_own": UNITS * (4 if l == 2 else 3), f"k_ready_{l}": n_k, f"s_sub_{l}": UNITS,
                         f"o_half_{l}": 4 if l == 3 else 1, f"x_added_{l}": 1}

                def scores(i, u):
                    n = 2 * sub
                    s_ = ps[:, u % 2, 0:w].rearrange("p (n s) -> p n s", s=S)
                    p_ = t["p"][:, u, 0:w].rearrange("p (n s) -> p n s", s=S)
                    v.wait_ge(sem(f"s_mm_{l}"), UNITS * i + (u + 1))
                    if l == 2:
                        own(v.tensor_scalar(p_, s_, CLAMP, -CLAMP, ALU.min, ALU.max))
                        own.wait()
                        s_ = p_
                    own(v.tensor_reduce(t["max"][:, u, 0:n], s_, AX.X, ALU.max))
                    own.wait()
                    own(v.tensor_tensor(p_, s_, t["max"][:, u, 0:n].unsqueeze(2).to_broadcast([P, n, S]),
                                        ALU.subtract), f"s_sub_{l}")

                def weigh(i, u):
                    n = 2 * sub
                    p_ = t["p"][:, u, 0:w].rearrange("p (n s) -> p n s", s=S)
                    v.wait_ge(sem(f"s_exp_{l}"), UNITS * i + (u + 1))
                    own(v.tensor_reduce(t["sum"][:, u, 0:n], p_, AX.X, ALU.add))
                    own.wait()
                    own(v.reciprocal(t["rec"][:, u, 0:n], t["sum"][:, u, 0:n]))
                    own.wait()
                    v.tensor_tensor(p_, p_, t["rec"][:, u, 0:n].unsqueeze(2).to_broadcast([P, n, S]),
                                    ALU.mult).then_inc(sem(f"prob_{l}"), 1)

                def keys(i):
                    if l != 3:
                        v.wait_ge(sem(f"k_mm_{l}"), i + 1)
                        for j in range(n_k):
                            own(v.tensor_scalar(t["k"][:, j, :], ps[:, 7, 0:GT],
                                                bqk[:, 1:2] if l == 2 else 0.0, headmask[l][:, j:j + 1],
                                                ALU.add, ALU.mult), f"k_ready_{l}")
                    else:
                        for j in range(4):
                            v.wait_ge(sem(f"k_mm_{l}"), 4 * i + (j + 1))
                            own(v.tensor_copy(t["k"][:, 2 * j:2 * j + 2, :],
                                              ps[:, 6 + j % 2, :].rearrange("p (c t) -> p c t", t=GT)),
                                f"k_ready_{l}")

                def outputs(i, quartet):
                    if l != 3:
                        v.wait_ge(sem(f"av_mm_{l}"), i + 1)
                        own(v.tensor_copy(t["o"][64:128, 0:GT], ps[64:128, 5, 0:GT]), f"o_half_{l}")
                        return
                    v.wait_ge(sem(f"av_mm_{l}"), 2 * i + (quartet + 1))
                    o_ = t["o"].rearrange("p (k h c s) -> p k h c s", k=8, h=2, c=2)
                    for hh in range(2):
                        own(v.tensor_copy(o_[:, 4 * quartet:4 * quartet + 4, hh, 1, :],
                                          ps[:, 5, :].rearrange("p (k h s) -> p k h s", k=4, h=2)[:, :, hh, :]),
                            f"o_half_{l}")

                def group(i, more):
                    weigh(i, 0)
                    scores(i, 2)
                    weigh(i, 1)
                    scores(i, 3)
                    weigh(i, 2)
                    if l == 3:
                        outputs(i, 0)
                    if more:
                        keys(i + 1)
                        scores(i + 1, 0)
                    weigh(i, 3)
                    if more:
                        scores(i + 1, 1)
                    outputs(i, 1)
                    v.wait_ge(sem(f"y_mm_{l}"), i + 1)
                    xg = x[:, bass.ds(2 * i, 2), :] if more else x[:, 2 * i:2 * i + 2, :]
                    own(v.scalar_tensor_tensor(xg, ps[:, 6, 0:GT].rearrange("p (j d) -> p j d", d=D), gates[:, l:l + 1],
                                               xg, ALU.mult, ALU.add), f"x_added_{l}")

                v.wait_ge(sem("loaded_rest"), 16 * N_REST)
                v.sem_inc(sem(f"x_added_{l}"), 1)
                own.add(f"x_added_{l}", 1)
                v.sem_inc(sem(f"s_sub_{l}"), 2)
                own.add(f"s_sub_{l}", 2)
                keys(0)
                scores(0, 0)
                scores(0, 1)
                with v.Fori(0, NG - 1) as i:
                    own.enter(i, steps)
                    group(i, True)
                    own.leave(NG - 1)
                group(NG - 1, False)
                own.wait()

            def one_hot(dst, val, vmax):
                bc = lambda q: q[:, :].unsqueeze(2).to_broadcast([P, NT, E])
                own(v.tensor_reduce(vmax[:, :], val[:, :, :], AX.X, ALU.max))
                own.wait()
                own(v.tensor_tensor(dst[:, :, :], val[:, :, :], bc(vmax), ALU.is_equal))
                own.wait()
                own(v.tensor_tensor(dst[:, :, :], dst[:, :, :], rank[:, :].unsqueeze(1).to_broadcast([P, NT, E]), ALU.mult))
                own.wait()
                own(v.tensor_reduce(v3[:, :], dst[:, :, :], AX.X, ALU.max))
                own.wait()
                own(v.tensor_tensor(dst[:, :, :], dst[:, :, :], bc(v3), ALU.is_equal))
                own.wait()

            def experts(l):
                bc = lambda q: q[:, :].unsqueeze(2).to_broadcast([P, NT, E])
                v.wait_ge(sem(f"logits_{l}"), 1)
                own(v.tensor_copy(lg[:, :, :], ps[:, 7, 0:NT * E].rearrange("p (j e) -> p j e", e=E)))
                own.wait()
                one_hot(oh1, lg, v1)
                if l == 1:
                    v.tensor_tensor(tmpe[:, :, :], lg[:, :, :], bc(v1), ALU.subtract).then_inc(sem("route_sub"), 1)
                    v.wait_ge(sem("route_exp"), 1)
                    own(v.tensor_reduce(v2[:, :], tmpe[:, :, :], AX.X, ALU.add))
                    own.wait()
                    own(v.reciprocal(v1[:, :], v2[:, :]))
                    own.wait()
                    own(v.tensor_scalar(v1[:, :], v1[:, :], gates[:, 4 + l:5 + l], None, ALU.mult))
                    own.wait()
                    own(v.tensor_tensor(comb[:, :, :], oh1[:, :, :], bc(v1), ALU.mult))
                else:
                    own(v.scalar_tensor_tensor(tmpe[:, :, :], oh1[:, :, :], -3.0e38, lg[:, :, :], ALU.mult, ALU.add))
                    own.wait()
                    one_hot(oh2, tmpe, v2)
                    v.tensor_tensor(v3[:, :], v2[:, :], v1[:, :], ALU.subtract).then_inc(sem("route_sub"), 1)
                    v.wait_ge(sem("route_exp"), l)
                    own(v.tensor_scalar(v1[:, :], v3[:, :], 1.0, None, ALU.add))
                    own.wait()
                    own(v.reciprocal(v2[:, :], v1[:, :]))
                    own.wait()
                    own(v.tensor_scalar(v2[:, :], v2[:, :], gates[:, 4 + l:5 + l], None, ALU.mult))
                    own.wait()
                    own(v.tensor_tensor(v3[:, :], v3[:, :], v2[:, :], ALU.mult))
                    own.wait()
                    own(v.tensor_tensor(comb[:, :, :], oh1[:, :, :], bc(v2), ALU.mult))
                    own(v.tensor_tensor(tmpe[:, :, :], oh2[:, :, :], bc(v3), ALU.mult))
                    own.wait()
                    own(v.tensor_tensor(comb[:, :, :], comb[:, :, :], tmpe[:, :, :], ALU.add))
                own.wait()
                v.sem_inc(sem(f"y_used_{l}"), 2)
                own.add(f"y_used_{l}", 2)

                def add_output(e, tc):
                    v.wait_ge(sem(f"y_mm_e{l}"), 4 * e + (tc + 3))
                    for k in range(4):
                        own(v.scalar_tensor_tensor(x[:, 4 * tc + k, :], ps[:, 4 + tc % 2, P * k:P * k + P],
                                                   comb[:, 4 * tc + k, bass.ds(e, 1)], x[:, 4 * tc + k, :],
                                                   ALU.mult, ALU.add), f"y_used_{l}" if k == 3 else None)

                def gated(e, tc):
                    for f in range(NF):
                        v.wait_ge(sem("silu_ready"), 16 * e + (4 * tc + f + 1))
                        if f == 0:
                            v.wait_ge(sem(f"y_mm_e{l}"), 4 * e + (tc + 1))
                        own(v.tensor_tensor(hT[:, tc % 2, f, :], sg[:, f % 2, :], ps[:, 2 + f % 2, :], ALU.mult), f"h_ready_{l}")

                steps = {"vec_own": 2 * 3 * NC, f"y_used_{l}": 2 * NC}
                if l == 2:
                    steps["h_ready_2"] = 2 * NF * NC
                    v.sem_inc(sem("h_ready_2"), 2)
                    own.add("h_ready_2", 2)
                with v.Fori(0, E // 2) as i:
                    own.enter(i, steps)
                    for s_ in range(2):
                        e = 2 * i + s_
                        for tc in range(NC):
                            if l == 2:
                                gated(e, tc)
                                if tc:
                                    add_output(e, tc - 1)
                            else:
                                add_output(e, tc)
                        if l == 2:
                            add_output(e, NC - 1)
                        own.wait()
                    own.leave(E // 2)
                own.wait()

            for l in (1, 2, 3):
                normalise(x, D, "two" if l == 1 else "one", [xh])
                v.sem_inc(sem(f"att_open_{l}"), 1)
                attention(l)
                if last == 2 * l + 1:
                    return finish()
                if l != 2:
                    normalise(x, D, "one", [xh])
                else:
                    normalise(x, D, "both", [xh, hres])
                    own.wait()
                    for c in range(NC):
                        v.wait_ge(sem("attw_mm"), c + 1)
                        own(v.tensor_tensor(hres[:, 4 * c:4 * c + 4, :], hres[:, 4 * c:4 * c + 4, :],
                                            ps[:, 4 + c % 2, :].rearrange("p (j d) -> p j d", d=D), ALU.add), "hres_ready")
                    own.wait()
                    own(v.scalar_tensor_tensor(x[:, :, :], hres[:, :, :], gates[:, 6:7], x[:, :, :], ALU.mult, ALU.add))
                    normalise(hres, D, "one", [xh])
                experts(l)
                if last == 2 * l + 2:
                    return finish()

        @block.scalar
        def _(s):
            own = Own(s, sem, "act_own")
            k_norm = [0]
            m_tr = [0]

            def deviations(kind="one"):
                for _ in range(SQRTS[kind]):
                    k_norm[0] += 1
                    s.wait_ge(sem("var_ready"), k_norm[0])
                    s.activation(st2[:, :], st1[:, :], ACT.Sqrt).then_inc(sem("sd_ready"), 1)

            def to_feature(dst, w=P, g=None, b=None):
                m = m_tr[0]
                for c in range(NC):
                    s.wait_ge(sem("norm_T"), NC * m + c + 1)
                    o, i_ = dst[0:w, CH * c:CH * c + CH], ps[0:w, c % 2, :]
                    if g is None:
                        ins = s.copy(o, i_)
                    else:
                        ins = s.activation(o, i_, ACT.Identity, bias=b, scale=g)
                    ins.then_inc(sem("norm_feature"), 1)
                m_tr[0] += 1

            s.wait_ge(sem("loaded_w0"), 16 * N_W0)
            s.activation(gates[:, :], gates[:, :], ACT.Tanh).then_inc(sem("gates_ready"), 1)
            for n in range(3):
                s.wait_ge(sem("q0_T"), n + 1)
                k = min(8, 17 - 8 * n)
                src = ps[:, n, :].bitcast(BF16).rearrange("p (k n) -> p k n", n=P)
                if n == 0:
                    own(s.copy(q0T[0:C, 0, :], src[0:C, 0, :]))
                    s.copy(q0T[:, 1:8, :], src[:, 1:8, :]).then_inc(sem("q0T_ready"), 1)
                else:
                    s.copy(q0T[:, 8 * n:8 * n + k, :], src[:, 0:k, :]).then_inc(sem("q0T_ready"), 1)
            for n in range(3):
                k = min(4, 9 - 4 * n)
                s.wait_ge(sem("wff_T"), n + 1)
                s.copy(wffT[:, 4 * n:4 * n + k, :], ps[:, 3 + n, 0:P * k].rearrange("p (k n) -> p k n", n=P)
                       ).then_inc(sem("wffT_ready"), 1)
            to_feature(ctxT, C)
            for n in range(2):
                s.wait_ge(sem("qctx_T"), n + 1)
                s.copy(qT[0:C, 1024 * n:1024 * n + 1024], ps[0:C, 2 + n, :].bitcast(BF16)).then_inc(sem("qctxT_ready"), 1)
            deviations()
            s.wait_ge(sem("loaded_rest"), 16 * N_REST)
            def linear(base, name, dst, sc, bi, banks=4):
                for c in range(NC):
                    s.wait_ge(sem("lin0"), base + c + 1)
                    s.activation(dst[:, CH * c:CH * c + CH], ps[:, 4 + c, :], ACT.Identity, bias=bias0[:, bi:bi + 1],
                                 scale=oscale[:, sc:sc + 1]).then_inc(sem(name), 1)
            linear(0, "act0_ready", act0, 0, 0)
            m_tr[0] = 1
            for c in range(NC):
                s.wait_ge(sem("norm_T"), NC + c + 1)
                s.activation(ctxnT[0:C, CH * c:CH * c + CH], ps[0:C, c % 2, :], ACT.Identity, bias=lng[0:C, 3:4],
                             scale=lng[0:C, 2:3]).then_inc(sem("norm_feature"), 2)
            m_tr[0] = 2
            deviations()
            for n in range(2):
                s.wait_ge(sem("qtok_T"), n + 1)
                s.copy(qT[:, 1024 * n:1024 * n + 1024], ps[:, 2 + n, :].bitcast(BF16)).then_inc(sem("qtokT_ready"), 1)
            linear(NC, "fused0_ready", fused, 1, 2)
            s.sem_inc(sem("act0_ready"), NC)
            linear(2 * NC, "act0_ready", act0, 2, 1)
            for r in range(2):
                for c in range(NC):
                    s.wait_ge(sem("lin0"), (3 + r) * NC + c + 1)
                    s.activation(kT[r][:, CH * c:CH * c + CH], ps[:, c, :], ACT.Identity,
                                 bias=bias0[:, 3 + r:4 + r], scale=oscale[:, 3:4] if r == 0 else oscale[:, 0:1]
                                 ).then_inc(sem("kT_ready"), 1)
            for r in range(2):
                for u in range(2):
                    s.wait_ge(sem("s0_sub"), 2 * r + u + 1)
                    pr = prob[:, 512 * u:512 * u + 512]
                    s.activation(pr, pr, ACT.Exp, scale=SCALE[0]).then_inc(sem("s0_exp"), 1)
                for u in range(2):
                    s.wait_ge(sem("pT0_mm"), 2 * r + u + 1)
                    s.copy(probT[:, 4 * u:4 * u + 4, :], ps[:, 2 + u, :].rearrange("p (g n) -> p g n", n=P)
                           ).then_inc(sem("probT0_ready"), 1)
            for n in range(NF * NC):
                f, c = n // NC, n % NC
                s.wait_ge(sem("f1_mm"), n + 1)
                s.activation(h0[:, f, CH * c:CH * c + CH], ps[:, n % 4, :], ACT.Relu, bias=bias0[:, 5 + f:6 + f],
                             scale=oscale[:, 1:2]).then_inc(sem("h0_ready"), 1)
            if last == 1:
                return

            deviations()
            to_feature(xnT)
            for w, buf in ((0, gate0), (1, up0)):
                for n in range(NI * NC):
                    f, c = n // NC, n % NC
                    s.wait_ge(sem("gu_mm"), NI * NC * w + n + 1)
                    s.copy(buf[:, f, CH * c:CH * c + CH], ps[:, n % 4, :]).then_inc(sem("gu_ready"), 1)
                    if w == 1 and c == NC - 1:
                        s.wait_ge(sem("gu_quant"), f + 1)
                        s.activation(sig0[:, f, :], gate0[:, f, :], ACT.Sigmoid).then_inc(sem("sig_ready"), 1)
            if last == 2:
                return

            def attention(l):
                t = att(l)
                sub = 4 if l != 1 else 2
                w = S * sub * 2

                def expo(i, u):
                    s.wait_ge(sem(f"s_sub_{l}"), UNITS * i + (u + 3))
                    p_ = t["p"][:, u, 0:w]
                    s.activation(p_, p_, ACT.Exp, scale=SCALE[l]).then_inc(sem(f"s_exp_{l}"), 1)

                def probT(i, u):
                    s.wait_ge(sem(f"pT_mm_{l}"), UNITS * i + (u + 1))
                    s.copy(t["pt"][:, u % 2, 0:sub, :], ps[:, 2 + u % 2, 0:sub * P].rearrange("p (h n) -> p h n", n=P)
                           ).then_inc(sem(f"pT_ready_{l}"), 1)

                def queries(i):
                    if l == 3:
                        for j in range(4):
                            s.wait_ge(sem(f"q_mm_{l}"), 4 * i + (j + 1))
                            s.copy(t["q"][:, 2 * j:2 * j + 2, :], ps[:, 6 + j % 2, :].rearrange("p (c t) -> p c t", t=GT)
                                   ).then_inc(sem(f"q_ready_{l}"), 1)
                        return
                    s.wait_ge(sem(f"q_mm_{l}"), i + 1)
                    if l == 2:
                        ins = s.activation(t["q"][:, 0, :], ps[:, 6, 0:GT], ACT.Identity, bias=bqk[:, 0:1])
                    else:
                        ins = s.copy(t["q"][:, 0, :], ps[:, 6, 0:GT])
                    ins.then_inc(sem(f"q_ready_{l}"), 1)

                def values(i):
                    if l == 3:
                        for j in range(4):
                            s.wait_ge(sem(f"v_mm_{l}"), 4 * i + (j + 5))
                            s.copy(t["v"][:, j // 2, 512 * (j % 2):512 * (j % 2) + 512], ps[:, 7 - j % 2, :]
                                   ).then_inc(sem(f"v_ready_{l}"), 1)
                        return
                    s.wait_ge(sem(f"v_mm_{l}"), i + 2)
                    s.copy(t["v"][:, :, :], ps[:, 7, 0:GT].rearrange("p (h n) -> p h n", h=2)
                           ).then_inc(sem(f"v_ready_{l}"), 1)

                def outputs(i, quartet):
                    if l != 3:
                        s.wait_ge(sem(f"av_mm_{l}"), i + 1)
                        s.copy(t["o"][0:64, 0:GT], ps[0:64, 4, 0:GT]).then_inc(sem(f"o_other_{l}"), 1)
                        s.wait_ge(sem(f"oT_mm_{l}"), i + 1)
                        s.copy(t["ot"], ps[:, 7, 0:GT]).then_inc(sem(f"oT_ready_{l}"), 1)
                        return
                    s.wait_ge(sem(f"av_mm_{l}"), 2 * i + (quartet + 1))
                    o_ = t["o"].rearrange("p (k h c s) -> p k h c s", k=8, h=2, c=2)
                    for hh in range(2):
                        s.copy(o_[:, 4 * quartet:4 * quartet + 4, hh, 0, :],
                               ps[:, 4, :].rearrange("p (k h s) -> p k h s", k=4, h=2)[:, :, hh, :]
                               ).then_inc(sem(f"o_other_{l}"), 1)

                def group(i, more):
                    values(i)
                    probT(i, 0)
                    expo(i, 2)
                    probT(i, 1)
                    expo(i, 3)
                    if l == 3:
                        outputs(i, 0)
                    if more:
                        queries(i + 1)
                    probT(i, 2)
                    if more:
                        expo(i + 1, 0)
                    probT(i, 3)
                    if more:
                        expo(i + 1, 1)
                    outputs(i, 1)

                queries(0)
                expo(0, 0)
                expo(0, 1)
                with s.Fori(0, NG - 1) as i:
                    group(i, True)
                group(NG - 1, False)

            def experts(l):
                s.wait_ge(sem("route_sub"), l)
                if l == 1:
                    s.activation(tmpe[:, :, :], tmpe[:, :, :], ACT.Exp).then_inc(sem("route_exp"), 1)
                else:
                    s.activation(v3[:, :], v3[:, :], ACT.Exp).then_inc(sem("route_exp"), 1)
                if l == 2:
                    with s.Fori(0, E // 2) as i:
                        for slot in range(2):
                            e = 2 * i + slot
                            for n in range(3):
                                s.wait_ge(sem("wexp_T"), 3 * e + (n + 1))
                                s.copy(wexpT[:, slot, 4 * n:4 * n + 4, :], ps[:, 6, :].rearrange("p (f n) -> p f n", n=P)
                                       ).then_inc(sem("wexpT_ready"), 1)
                            for n in range(4 * NC):
                                s.wait_ge(sem(f"h_mm_{l}"), 16 * e + (n + 1))
                                s.wait_ge(sem(f"h_ready_{l}"), 16 * e + (n + 1))
                                s.activation(sg[:, n % 2, :], ps[:, n % 2, :], ACT.Silu).then_inc(sem("silu_ready"), 1)
                    return
                fn = ACT.Gelu_apprx_tanh if l == 1 else ACT.Relu
                s.sem_inc(sem(f"h_ready_{l}"), 4)
                with s.Fori(0, E // 2) as i:
                    own.enter(i, {"act_own": 2})
                    for slot in range(2):
                        e = 2 * i + slot
                        own(s.copy(b1s[:, slot, :], b1[l][:, bass.ds(e, 1), :].rearrange("p e f -> p (e f)")))
                        own.wait()
                        for tc in range(NC):
                            s.wait_ge(sem(f"y_mm_e{l}"), 4 * e + (tc + 1))
                            for f in range(NF):
                                s.wait_ge(sem(f"h_mm_{l}"), 16 * e + (4 * tc + f + 1))
                                s.activation(hT[:, tc % 2, f, :], ps[:, f, :], fn, bias=b1s[:, slot, f:f + 1]
                                             ).then_inc(sem(f"h_ready_{l}"), 1)
                    own.leave(E // 2)
                own.wait()

            for l in (1, 2, 3):
                deviations("two" if l == 1 else "one")
                if l == 1:
                    to_feature(xnT, g=lng[:, 0:1], b=lng[:, 1:2])
                else:
                    to_feature(xnT)
                attention(l)
                if last == 2 * l + 1:
                    return
                if l == 2:
                    deviations("both")
                    to_feature(xnT, g=lng[:, 4:5], b=lng[:, 5:6])
                    s.wait_ge(sem("prep2_T"), 1)
                    s.copy(attwT[:, :], ps[:, 7, 0:P])
                    s.copy(gw[2][:, :], ps[:, 7, P:P + E]).then_inc(sem("prep2_ready"), 1)
                    deviations()
                    s.wait_ge(sem("attw_mm"), NC)
                    to_feature(xnT, g=lng[:, 6:7], b=lng[:, 7:8])
                else:
                    deviations()
                    to_feature(xnT)
                experts(l)
                if last == 2 * l + 2:
                    return

        @block.tensor
        def _(t_):
            pe = t_
            m_tr = [0]
            k_norm = [0]

            def tiles_T(src, w, wait, feature):
                m = m_tr[0]
                for c in range(NC):
                    if c >= 2:
                        pe.wait_ge(sem("norm_feature"), feature + c - 1)
                    for k in range(4):
                        j = 4 * c + k
                        if wait:
                            pe.wait_ge(sem("norm_ready"), NT * k_norm[0] + j + 1)
                        ins = pe.transpose(ps[0:w, c % 2, P * k:P * k + P], src[:, j, :], ident[:, :])
                    ins.then_inc(sem("norm_T"), 1)
                m_tr[0] += 1
                if wait:
                    k_norm[0] += 1

            pe.wait_ge(sem("constants"), 1)
            pe.wait_ge(sem("q0_ready"), 1)
            for n in range(17):
                src = q0[:, 0:96] if n == 0 else q0[:, 96 + 128 * (n - 1):96 + 128 * n]
                o = ps[0:src.shape[1], n // 8, :].bitcast(BF16)[:, P * (n % 8):P * (n % 8) + P]
                ins = pe.transpose(o, src, identb[:, :])
                if n % 8 == 7 or n == 16:
                    ins.then_inc(sem("q0_T"), 1)
            pe.wait_ge(sem("wff_ready"), 1)
            for n in range(9):
                ins = pe.transpose(ps[:, 3 + n // 4, P * (n % 4):P * (n % 4) + P], wff[:, n, :], ident[:, :])
                if n % 4 == 3 or n == 8:
                    ins.then_inc(sem("wff_T"), 1)
            pe.wait_ge(sem("loaded_ctx"), 16)
            pe.wait_ge(sem("q0T_ready"), 3)
            tiles_T(ctok, C, False, 0)

            def bf_tiles_T(src, w, name):
                for j in range(NT):
                    o = ps[0:w, 2 + j // 8, :].bitcast(BF16)[:, P * (j % 8):P * (j % 8) + P]
                    ins = pe.transpose(o, src[:, j, :], identb[:, :])
                    if j % 8 == 7:
                        ins.then_inc(sem(name), 1)
            pe.wait_ge(sem("qctx_ready"), 1)
            bf_tiles_T(qctx, C, "qctx_T")
            pe.wait_ge(sem("qctxT_ready"), 2)
            pe.wait_ge(sem("wffT_ready"), 3)
            for c in range(NC):
                pe.matmul(ps[:, 4 + c, :], q0T[0:C, 0, :], qT[0:C, CH * c:CH * c + CH], start=True, stop=True
                          ).then_inc(sem("lin0"), 1)
            pe.wait_ge(sem("norm_feature"), NC)
            for c in range(NC):
                if c >= 2:
                    pe.wait_ge(sem("norm_feature"), NC + 2 * (c - 1))
                for k in range(4):
                    j = 4 * c + k
                    pe.wait_ge(sem("norm_ready"), j + 1)
                    ins = pe.transpose(ps[0:C, c % 2, P * k:P * k + P], xh[:, j, 0:C], ident[:, :])
                ins.then_inc(sem("norm_T"), 1)
            m_tr[0] = 2
            k_norm[0] = 2
            pe.wait_ge(sem("qtok_ready"), 1)
            bf_tiles_T(qtok, D, "qtok_T")
            pe.wait_ge(sem("qtokT_ready"), 2)
            pe.wait_ge(sem("act0_ready"), NC)
            for c in range(NC):
                pe.matmul(ps[:, 4 + c, :], q0T[:, 2, :], qT[:, CH * c:CH * c + CH], start=True, stop=True
                          ).then_inc(sem("lin0"), 1)
            pe.wait_ge(sem("fused0_ready"), NC)
            pe.wait_ge(sem("qT_ready"), 1)
            for c in range(NC):
                pe.matmul(ps[:, 4 + c, :], q0T[:, 1, :], qT[:, CH * c:CH * c + CH], start=True, stop=True
                          ).then_inc(sem("lin0"), 1)
            pe.wait_ge(sem("act0_ready"), 3 * NC)
            pe.wait_ge(sem("qT_ready"), 2)
            for r in range(2):
                for c in range(NC):
                    if r:
                        pe.wait_ge(sem("kT_ready"), c + 1)
                    pe.matmul(ps[:, c, :], q0T[:, 3 + r, :], qT[:, CH * c:CH * c + CH], start=True, stop=True
                              ).then_inc(sem("lin0"), 1)
                for c in range(NC):
                    if r:
                        pe.wait_ge(sem("ktok_ready"), c + 1)
                    for k in range(4):
                        j = 4 * c + k
                        ins = pe.matmul(ps[:, 4 + c, P * k:P * k + P], qT[:, P * j:P * j + P], q0T[:, 3 + r, :],
                                        start=True, stop=True)
                    ins.then_inc(sem("ktok_mm"), 1)
            pe.wait_ge(sem("kT_ready"), 2 * NC)
            pe.wait_ge(sem("ktok_ready"), 2 * NC)
            for r in range(2):
                if r:
                    pe.wait_ge(sem("fused_ready"), 4)
                for g in range(NG):
                    for c in range(2):
                        for hh in range(2):
                            b = 4 * g + 2 * hh + c
                            n = 2 * (g % 4) + c
                            ins = pe.matmul(ps[64 * hh:64 * hh + 64, g // 4, S * n:S * n + S],
                                            fused[:, S * b:S * b + S], kT[r][:, S * b:S * b + S], start=True, stop=True)
                    if g % 4 == 3:
                        ins.then_inc(sem("s0_mm"), 1)
                for u in range(2):
                    pe.wait_ge(sem("s0_prob"), 2 * r + u + 1)
                    for g in range(4):
                        ins = pe.transpose(ps[:, 2 + u, P * g:P * g + P], prob[:, 512 * u + P * g:512 * u + P * g + P],
                                           ident[:, :])
                    ins.then_inc(sem("pT0_mm"), 1)
                for u in range(2):
                    pe.wait_ge(sem("probT0_ready"), 2 * r + u + 1)
                    for c in range(2):
                        for g in range(4):
                            for hh in range(2):
                                j = 2 * (4 * u + g) + hh
                                n = 2 * g + hh
                                ins = pe.matmul(ps[:, 4 + 2 * u + c, S * n:S * n + S],
                                                ktok[r][64 * c:64 * c + 64, j, :],
                                                probT[64 * c:64 * c + 64, 4 * u + g, 64 * hh:64 * hh + 64],
                                                start=True, stop=True)
                        ins.then_inc(sem("av0_mm"), 1)
            pe.wait_ge(sem("qT_ready"), 3)
            for n in range(NF * NC):
                f, c = n // NC, n % NC
                if n >= 4:
                    pe.wait_ge(sem("h0_ready"), n - 3)
                pe.matmul(ps[:, n % 4, :], q0T[:, 5 + 2 * f, :], qT[:, CH * c:CH * c + CH], start=True, stop=False)
                pe.matmul(ps[:, n % 4, :], q0T[:, 6 + 2 * f, :],
                          qavg[:, 8 * c:8 * c + 8].unsqueeze(2).to_broadcast([P, 8, S]),
                          start=False, stop=True).then_inc(sem("f1_mm"), 1)

            def token_products(name, n, lhsT, rhs):
                for c in range(NC):
                    if c >= 2:
                        pe.wait_ge(sem(name + "_used"), c - 1)
                    for k in range(4):
                        j = 4 * c + k
                        for f in range(n):
                            ins = pe.matmul(ps[:, c % 2, P * k:P * k + P], lhsT(f, j), rhs(f), start=(f == 0),
                                            stop=(f == n - 1))
                    ins.then_inc(sem(name), 1)
            pe.wait_ge(sem("qh_ready"), NF)
            pe.wait_ge(sem("h0_ready"), NF * NC)
            token_products("f2_mm", NF, lambda f, j: qh[:, f, P * j:P * j + P], lambda f: q0T[:, 13 + f, :])
            if last == 1:
                return

            pe.wait_ge(sem("xq_ready"), 1)
            feature = [3 * NC]

            def norm_T():
                tiles_T(xh, D, True, feature[0])
                feature[0] += NC
                pe.wait_ge(sem("norm_feature"), feature[0])
            norm_T()
            for w in range(2):
                for n in range(NI * NC):
                    f, c = n // NC, n % NC
                    if n + w >= 4 or w:
                        pe.wait_ge(sem("gu_ready"), NI * NC * w + n - 3)
                    pe.matmul(ps[:, n % 4, :], wffT[:, 3 * w + f, :], xnT[:, CH * c:CH * c + CH], start=True, stop=True
                              ).then_inc(sem("gu_mm"), 1)
            pe.wait_ge(sem("o_ready"), 1)
            token_products("down_mm", NI, lambda f, j: gate0[:, f, P * j:P * j + P], lambda f: wffT[:, 6 + f, :])
            if last == 2:
                return

            def attention(l):
                t = att(l)
                d = WIN[l] // HEADS[l]
                sub = 4 if l != 1 else 2
                nkk = {1: 2, 2: 4, 3: 4}[l]

                def apart():
                    pe.sem_inc(sem("waited"), 1)

                def at_group(src, i):
                    return src[:, i * GT:i * GT + GT] if isinstance(i, int) else src[:, bass.ds(i * GT, GT)]

                def queries_keys(i):
                    xg = at_group(xnT, i)
                    cg = at_group(ctxnT if l == 1 else ctxT, i)
                    if l != 3:
                        if not (isinstance(i, int) and i == 0):
                            pe.wait_ge(sem(f"x_added_{l}"), i)
                        pe.matmul(ps[:, 6, 0:GT], wq[l][:, :], xg, start=True, stop=True).then_inc(sem(f"q_mm_{l}"), 1)
                        pe.matmul(ps[:, 7, 0:GT], wk[l][:, :], cg, start=True, stop=True).then_inc(sem(f"k_mm_{l}"), 1)
                        return
                    for j in range(4):
                        if j >= 2:
                            pe.wait_ge(sem(f"q_ready_{l}"), 4 * i + (j - 1))
                        for k in range(2):
                            n = 2 * j + k
                            ins = pe.matmul(ps[:, 6 + j % 2, GT * k:GT * k + GT], wq[l][:, P * n:P * n + P], xg,
                                            start=True, stop=True)
                        ins.then_inc(sem(f"q_mm_{l}"), 1)
                    for j in range(4):
                        if j < 2:
                            pe.wait_ge(sem(f"q_ready_{l}"), 4 * i + (j + 3))
                        else:
                            pe.wait_ge(sem(f"k_ready_{l}"), 4 * i + (j - 1))
                        for k in range(2):
                            n = 2 * j + k
                            ins = pe.matmul(ps[:, 6 + j % 2, GT * k:GT * k + GT], wk[l][:, P * n:P * n + P], cg,
                                            start=True, stop=True)
                        ins.then_inc(sem(f"k_mm_{l}"), 1)

                def value_rows(i):
                    pe.wait_ge(sem(f"ctx_staged_{l}"), i + 1)
                    if l != 3:
                        for hh in range(2):
                            o = ps[:, 7, P * hh:P * hh + P]
                            ins = pe.matmul(o, ctxs[:, P * hh:P * hh + P], wv[l][:, :], start=True, stop=(l == 1))
                            if l == 2:
                                ins = pe.matmul(o, ones[:, :], rows[:, 0, :], start=False, stop=True)
                        ins.then_inc(sem(f"v_mm_{l}"), 1)
                        return
                    for j in range(4):
                        if j == 1:
                            pe.wait_ge(sem(f"x_added_{l}"), i + 1)
                        elif j > 1:
                            pe.wait_ge(sem(f"v_ready_{l}"), 4 * i + (j - 1))
                        hh, half = j // 2, j % 2
                        pe.matmul(ps[:, 7 - j % 2, :], ctxs[:, P * hh:P * hh + P], wv[l][:, 512 * half:512 * half + 512],
                                  start=True, stop=True).then_inc(sem(f"v_mm_{l}"), 1)

                def scores(i, u):
                    pe.wait_ge(sem(f"s_sub_{l}"), UNITS * i + (u + 1))
                    if u == 0:
                        pe.wait_ge(sem(f"q_ready_{l}"), (4 if l == 3 else 1) * (i + 1))
                        pe.wait_ge(sem(f"k_ready_{l}"), nkk * (i + 1))
                    apart()
                    for c in range(2):
                        for hh in range(2):
                            lo = S * (2 * hh + c)
                            if l != 3:
                                r = 32 * u
                                o = ps[64 * hh:64 * hh + 64, u % 2, 0:2 * sub * S]
                                ins = pe.matmul(o.rearrange("p (h c s) -> p h c s", c=2, s=S)[:, :, c, :], t["q"][r:r + 32, 0, lo:lo + S],
                                                t["k"][r:r + 32, :, lo:lo + S], start=True, stop=True)
                            else:
                                r = 64 * (u % 2)
                                for k in range(4):
                                    ch = 4 * (u // 2) + k
                                    ins = pe.matmul(ps[64 * hh:64 * hh + 64, u % 2, S * (2 * k + c):S * (2 * k + c) + S],
                                                    t["q"][r:r + 64, ch, lo:lo + S], t["k"][r:r + 64, ch, lo:lo + S],
                                                    start=True, stop=True)
                    ins.then_inc(sem(f"s_mm_{l}"), 1)

                def turn(i, u):
                    pe.wait_ge(sem(f"prob_{l}"), UNITS * i + (u + 1))
                    for k in range(sub):
                        ins = pe.transpose(ps[:, 2 + u % 2, P * k:P * k + P], t["p"][:, u, P * k:P * k + P], ident[:, :])
                    ins.then_inc(sem(f"pT_mm_{l}"), 1)

                def values(i, u):
                    pe.wait_ge(sem(f"pT_ready_{l}"), UNITS * i + (u + 1))
                    apart()
                    for c in range(2):
                        r = 64 * c
                        for hh in range(2):
                            for k in range(sub):
                                pt = t["pt"][r:r + 64, u % 2, k, 64 * hh:64 * hh + 64]
                                if l != 3:
                                    h = sub * u + k
                                    o = ps[r:r + 64, 4 + c, P * hh + d * h:P * hh + d * h + d]
                                    ins = pe.matmul(o, pt, t["v"][r:r + 64, hh, d * h:d * h + d], start=True, stop=True)
                                else:
                                    ch = 4 * (u // 2) + k
                                    h = 2 * ch + u % 2
                                    q = 64 * (u % 2)
                                    o = ps[q:q + 64, 4 + c, P * k + S * hh:P * k + S * hh + S]
                                    ins = pe.matmul(o, t["v"][r:r + 64, hh, d * h:d * h + d], pt, start=True, stop=True)
                    if (l == 3 and u % 2) or u == 3:
                        ins.then_inc(sem(f"av_mm_{l}"), 1)

                def project_out(i):
                    if l != 3:
                        pe.wait_ge(sem(f"o_half_{l}"), i + 1)
                        pe.wait_ge(sem(f"o_other_{l}"), i + 1)
                        for hh in range(2):
                            ins = pe.transpose(ps[:, 7, P * hh:P * hh + P], t["o"][:, P * hh:P * hh + P], ident[:, :])
                        ins.then_inc(sem(f"oT_mm_{l}"), 1)
                        pe.wait_ge(sem(f"oT_ready_{l}"), i + 1)
                    else:
                        pe.wait_ge(sem(f"o_half_{l}"), 4 * i + 4)
                        pe.wait_ge(sem(f"o_other_{l}"), 4 * i + 4)
                    for hh in range(2):
                        o = ps[:, 6, P * hh:P * hh + P]
                        n = WIN[l] // P
                        for k in range(n):
                            lt = t["ot"][:, P * hh:P * hh + P] if l != 3 else \
                                t["o"].rearrange("p (k n) -> p k n", k=8)[:, k, P * hh:P * hh + P]
                            ins = pe.matmul(o, lt, wo[l][:, k, :], start=(k == 0), stop=(l == 1 and k == n - 1))
                        if l > 1:
                            ins = pe.matmul(o, ones[:, :], rows[:, l - 1, :], start=False, stop=True)
                    ins.then_inc(sem(f"y_mm_{l}"), 1)

                def group(i, more):
                    value_rows(i)
                    scores(i, 2)
                    pe.wait_ge(sem(f"v_ready_{l}"), 4 * i + 4 if l == 3 else i + 1)
                    turn(i, 0)
                    values(i, 0)
                    scores(i, 3)
                    turn(i, 1)
                    values(i, 1)
                    if more:
                        queries_keys(i + 1)
                        scores(i + 1, 0)
                    if l == 3:
                        pe.wait_ge(sem(f"o_half_{l}"), 4 * i + 2)
                        pe.wait_ge(sem(f"o_other_{l}"), 4 * i + 2)
                    turn(i, 2)
                    values(i, 2)
                    if more:
                        scores(i + 1, 1)
                    turn(i, 3)
                    values(i, 3)
                    project_out(i)

                pe.nop().then_inc(sem(f"v_mm_{l}"), 4 if l == 3 else 1)
                queries_keys(0)
                scores(0, 0)
                scores(0, 1)
                with pe.Fori(0, NG - 1) as i:
                    group(i, True)
                group(NG - 1, False)

            def experts(l):
                for j in range(NT):
                    o = ps[:, 7, E * j:E * j + E]
                    ins = pe.matmul(o, xnT[:, P * j:P * j + P], gw[l][:, :], start=True, stop=(l == 2))
                    if l != 2:
                        ins = pe.matmul(o, ones[:, :], gb[:, l // 2, :], start=False, stop=True)
                ins.then_inc(sem(f"logits_{l}"), 1)
                pe.nop().then_inc(sem(f"y_mm_e{l}"), 2)
                loads_before = 0 if l == 1 else (E // 2) * 16 * (3 if l == 2 else 6)

                def hidden(e, slot, tc):
                    for f in range(NF):
                        n = 4 * tc + f
                        xt = xnT[:, CH * tc:CH * tc + CH]
                        pe.wait_ge(sem(f"h_ready_{l}"), 16 * e + (n + 1))
                        if l != 2:
                            pe.matmul(ps[:, f, :], wexp[:, slot, f, :], xt, start=True, stop=True
                                      ).then_inc(sem(f"h_mm_{l}"), 1)
                        else:
                            pe.matmul(ps[:, n % 2, :], wexpT[:, slot, f, :], xt, start=True, stop=True)
                            pe.matmul(ps[:, 2 + n % 2, :], wexpT[:, slot, 4 + f, :], xt, start=True, stop=True
                                      ).then_inc(sem(f"h_mm_{l}"), 1)

                def output(e, slot, tc):
                    pe.wait_ge(sem(f"y_used_{l}"), 4 * e + (tc + 1))
                    pe.wait_ge(sem(f"h_ready_{l}"), 16 * e + (4 * tc + 4 + (4 if l != 2 else 2)))
                    for k in range(4):
                        o = ps[:, 4 + tc % 2, P * k:P * k + P]
                        for f in range(NF):
                            w = wexp[:, slot, 4 + f, :] if l != 2 else wexpT[:, slot, 8 + f, :]
                            ins = pe.matmul(o, hT[:, tc % 2, f, P * k:P * k + P], w, start=(f == 0),
                                            stop=(l == 2 and f == NF - 1))
                        if l != 2:
                            ins = pe.matmul(o, ones[:, :], b2[:, slot, :], start=False, stop=True)
                    ins.then_inc(sem(f"y_mm_e{l}"), 1)

                with pe.Fori(0, E // 2) as i:
                    for slot in range(2):
                        e = 2 * i + slot
                        pe.wait_ge(sem(f"loaded_expert{slot}"), loads_before + 16 * 3 * (i + 1))
                        if l == 2:
                            for n in range(3):
                                if n:
                                    pe.wait_ge(sem("wexpT_ready"), 3 * e + n)
                                for k in range(4):
                                    ins = pe.transpose(ps[:, 6, P * k:P * k + P], wexp[:, slot, 4 * n + k, :], ident[:, :])
                                ins.then_inc(sem("wexp_T"), 1)
                            pe.wait_ge(sem("wexpT_ready"), 3 * e + 3)
                        hidden(e, slot, 0)
                        for tc in range(1, NC):
                            hidden(e, slot, tc)
                            output(e, slot, tc - 1)
                        output(e, slot, NC - 1)

            for l in (1, 2, 3):
                norm_T()
                attention(l)
                if last == 2 * l + 1:
                    return
                norm_T()
                if l == 2:
                    pe.transpose(ps[:, 7, 0:P], attw[:, :], ident[:, :])
                    pe.transpose(ps[:, 7, P:P + E], gwn[:, :], ident[0:E, 0:E]).then_inc(sem("prep2_T"), 1)
                    pe.wait_ge(sem("prep2_ready"), 1)
                    for c in range(NC):
                        if c >= 2:
                            pe.wait_ge(sem("hres_ready"), c - 1)
                        for k in range(4):
                            j = 4 * c + k
                            ins = pe.matmul(ps[:, 4 + c % 2, P * k:P * k + P], xnT[:, P * j:P * j + P], attwT[:, :],
                                            start=True, stop=True)
                        ins.then_inc(sem("attw_mm"), 1)
                    norm_T()
                experts(l)
                if last == 2 * l + 2:
                    return


_OUTS = [((B, S, D), "float32")]


def kernel(**inputs):
    import numpy as _np
    import concourse.bacc as _bacc
    from concourse import mybir as _mybir
    from concourse.bass_utils import run_bass_kernel_spmd as _run

    nc = _bacc.Bacc("TRN2", target_bir_lowering=False, num_devices=1)
    arrays, args = {}, {}
    for name, value in inputs.items():
        arr = _np.ascontiguousarray(value)
        arrays[f"in_{name}"] = arr
        args[name] = nc.dram_tensor(f"in_{name}", arr.shape, _mybir.dt.from_np(arr.dtype), kind="ExternalInput").ap()
    shape, dtype = _OUTS[0]
    out = nc.dram_tensor("out_0", shape, _mybir.dt.from_np(_np.dtype(dtype)), kind="ExternalOutput").ap()
    flamingo_kernel(nc, args, out)
    r = _run(nc, [arrays], core_ids=[0])
    return r.results[0]["out_0"]
```

```python
from contextlib import ExitStack

import numpy as np

import concourse.bass as bass
from concourse import mybir

F32 = mybir.dt.float32
BF16 = mybir.dt.bfloat16
I32 = mybir.dt.int32
U32 = mybir.dt.uint32
ALU = mybir.AluOpType
ACT = mybir.ActivationFunctionType
AX = mybir.AxisListType
RED = bass.bass_isa.ReduceOp

P = 128
B, S, D, C = 32, 64, 128, 96
T = B * S
NT = T // P
NG = B // 4
GT = 4 * S
CH = 512
NC = T // CH
E = 8
F = 512
NF = F // P
I0 = 384
NI = I0 // P
BLK = 32
EPS = 1e-5
TABLE = 14080
ARENA = TABLE + 3 * E * F
MAGIC = 1.5 * 2.0 ** 23
TOPK = {1: 1, 2: 2, 3: 2}
NQ = {l: -(-(TOPK[l] * NT + E - 1) // 4) * 4 for l in TOPK}
QB = {l: sum(NQ[m] for m in TOPK if m < l) for l in TOPK}
HMM = {1: 1, 2: 2, 3: 1}
HB = {l: sum(NQ[m] * HMM[m] for m in TOPK if m < l) for l in TOPK}
KB = {l: sum(TOPK[m] for m in TOPK if m < l) for l in TOPK}
GB = {l: NG * (l - 1) for l in TOPK}
UB = {l: 4 * GB[l] for l in TOPK}
WE = {1: 2 * F + D + NF, 2: 3 * F, 3: 2 * F + D + NF}
UNITS = 4
LAYERS = 4


class Own:

    def __init__(self, eng, sem, default):
        self.eng, self.sem, self.default = eng, sem, default
        self.base, self.n, self.pending = {}, {}, []

    def __call__(self, ins, name=None, by=1):
        name = name or self.default
        ins.then_inc(self.sem(name), by)
        self.add(name, by)
        return ins

    def add(self, name, by):
        self.n[name] = self.n.get(name, 0) + by
        if name not in self.pending:
            self.pending.append(name)

    def wait(self):
        for name in self.pending:
            self.eng.wait_ge(self.sem(name), self.base.get(name, 0) + self.n[name])
        self.pending = []

    def enter(self, i, steps):
        self.outer, self.steps = dict(self.n), steps
        for name, k in steps.items():
            self.base[name] = self.n.get(name, 0) + i * k
            self.n[name] = 0

    def leave(self, turns):
        for name, k in self.steps.items():
            assert self.n[name] == k, (name, self.n[name], k)
            self.n[name] = self.outer.get(name, 0) + turns * k
        self.base, self.pending = {}, list(self.steps)


def flamingo_kernel(nc, a, out, last=2 * LAYERS):
    ctx = ExitStack()
    with ctx:
        def sb(name, shape, dt=F32):
            return ctx.enter_context(nc.sbuf_tensor(name, shape, dt))

        sems = {}

        def sem(name):
            if name not in sems:
                sems[name] = ctx.enter_context(nc.semaphore(name))
            return sems[name]

        ps = ctx.enter_context(nc.psum_tensor("ps", [P, 8, CH], F32))

        ident = sb("ident", [P, P])
        identb = sb("identb", [P, P], BF16)
        ones = sb("ones", [1, P])
        headmask = {1: sb("headmask1", [P, 2]), 2: sb("headmask2", [P, 4])}
        gates = sb("gates", [P, 8])
        invcount = sb("invcount", [P, 7])
        before = sb("before", [P, P], BF16)
        onesb = sb("onesb", [P, P], BF16)
        zero = sb("zero", [P, D])
        magic = sb("magic", [P, 1])
        tile_i = sb("tile_i", [1, max(NQ.values())], I32)
        tile_f = sb("tile_f", [1, max(NQ.values())])
        rank = sb("rank", [P, E])

        x = sb("x", [P, NT, D])
        xh = sb("xh", [P, NT, D])
        xnT = sb("xnT", [P, T])
        ctxT = sb("ctxT", [C, T])
        ctxnT = sb("ctxnT", [C, T])
        bst = sb("bst", [P, NT, 6])
        mv = sb("mv", [P, NT, 2])
        st1 = sb("st1", [P, NT])
        st2 = sb("st2", [P, NT])
        rstd = sb("rstd", [P, NT])
        rstd2 = sb("rstd2", [P, NT])

        arena = sb("arena", [P, ARENA])
        def view(lo, n, p=P):
            return arena[0:p, lo:lo + n]

        W0 = [("d2v", 0, 96), ("img", 96, 128), ("txt", 224, 128), ("att0", 352, 128), ("att1", 480, 128),
              ("f1", 608, 1024), ("f2", 1632, 512)]
        COUNT0 = [P * C, P * P, P * P, P * P, P * P, 512 * 256, 512 * P]
        w0 = sb("w0", [P, 2144])
        q0 = sb("q0", [P, 2144], BF16)
        q0T = sb("q0T", [P, 17, P], BF16)
        wsum = sb("wsum", [P, 7])
        wtot = sb("wtot", [P, 7])
        wscale = sb("wscale", [P, 7])
        whalf = sb("whalf", [P, 7])
        wnhalf = sb("wnhalf", [P, 7])
        bias0 = sb("bias0", [P, 9])
        batt = sb("batt", [P, 2, P])
        bf2 = sb("bf2", [P, P])
        amax = sb("amax", [P, 16])
        amaxp = sb("amaxp", [P, 1])
        amaxg = sb("amaxg", [P, 1])
        iscale = sb("iscale", [P, 1])
        irecip = sb("irecip", [P, 1])
        oscale = sb("oscale", [P, 4])
        wff = sb("wff", [P, 9, P])
        wffs = sb("wffs", [P, 36])
        wffr = sb("wffr", [P, 36])
        wffT = sb("wffT", [P, 9, P])

        WIN = {1: P, 2: P, 3: 1024}
        HEADS = {1: 8, 2: 16, 3: 16}
        wq = {l: sb(f"wq{l}", [P, WIN[l]]) for l in (1, 2, 3)}
        wk = {l: sb(f"wk{l}", [C, WIN[l]]) for l in (1, 2, 3)}
        wv = {l: sb(f"wv{l}", [C, WIN[l]]) for l in (1, 2, 3)}
        wo = {1: sb("wo1", [P, 1, P]), 2: sb("wo2", [P, 1, P]), 3: sb("wo3", [P, 8, P])}
        bqk = sb("bqk", [P, 2])
        rows = sb("rows", [1, 2, P])
        bv2 = sb("bv2", [P, 1])
        bvs = sb("bvs", [P, P])
        offset = sb("offset", [P, P])
        lng = sb("lng", [P, 8])
        gw = {1: sb("gw1", [P, E]), 2: sb("gw2", [P, E]), 3: sb("gw3", [P, E])}
        gwn = sb("gwn", [E, P])
        gb = sb("gb", [P, 2, E])
        attw = sb("attw", [P, P])
        attwT = sb("attwT", [P, P])
        lg = sb("lg", [P, NT, E])
        oh1 = sb("oh1", [P, NT, E])
        oh2 = sb("oh2", [P, NT, E])
        ohb = sb("ohb", [P, NT * E], BF16)
        tmpe = sb("tmpe", [P, NT, E])
        tiles_a = sb("tiles_a", [P, 2 * E])
        tiles_b = sb("tiles_b", [P, 2 * E])
        firstrow = sb("firstrow", [P, E])
        rowf = sb("rowf", [P, NT])
        row = sb("row", [P, 2, NT], U32)
        reached = sb("reached", [1, max(NQ.values()), E])
        expert_f = sb("expert_f", [1, max(NQ.values())])
        expert_of = sb("expert_of", [1, max(NQ.values())], I32)
        idle = sb("idle", [P, 32])
        v1 = sb("v1", [P, NT])
        v2 = sb("v2", [P, NT])
        v3 = sb("v3", [P, NT])

        sorted_x = nc.dram_tensor("sorted_x", (max(NQ.values()) * P, D), F32, kind="Internal").ap()
        sorted_y = nc.dram_tensor("sorted_y", (max(NQ.values()) * P, D), F32, kind="Internal").ap()

        loads = {}
        N_PAR = {}
        block = ctx.enter_context(nc.Block())

        def table(l):
            return view(TABLE, E * WE[l]).rearrange("p (e n) -> p e n", e=E)

        hT = view(0, 1024).rearrange("p (u f t) -> p u f t", u=2, f=NF)
        sg = view(1024, 1024).rearrange("p (u t) -> p u t", u=2)
        xq = view(2048, 512).rearrange("p (s d) -> p s d", s=4)
        xqT = view(2560, 256).rearrange("p (u t) -> p u t", u=2)
        wst = view(2816, 4 * 3 * F).rearrange("p (s n) -> p s n", s=4)
        yall = view(8960, max(NQ.values()) * D).rearrange("p (q d) -> p q d", d=D)
        ytok = view(8960, 2 * NT * D).rearrange("p (k j d) -> p k j d", k=2, d=D)
        hres = view(0, 2048).rearrange("p (j d) -> p j d", d=D)

        @block.sync
        def _(sp):
            def load(dst, src, s):
                loads[s.name] = loads.get(s.name, 0) + 1
                sp.dma_start(dst, src, allow_slow_non_contiguous=True).then_inc(s, 16)

            xr = a["x"].rearrange("b s d -> (b s) d").rearrange("(j p) d -> p j d", p=P)
            cr = a["ctx_768"].rearrange("b s d -> (b s) d").rearrange("(j p) d -> p j d", p=P)
            load(x[:, :, :], xr, sem("loaded_x"))
            load(view(0, NT * C).rearrange("p (j d) -> p j d", d=C), cr, sem("loaded_ctx"))
            w = sem("loaded_w0")
            load(w0[:, 0:96], a["L0_xattn_W_d2v"], w)
            load(w0[:, 96:224], a["L0_xattn_W_img"], w)
            load(w0[:, 224:352], a["L0_xattn_W_txt"], w)
            for i, nm in enumerate(("L0_xattn_W_att0", "L0_xattn_W_att1")):
                for h in range(2):
                    load(w0[64 * h:64 * h + 64, 352 + 128 * i:480 + 128 * i], a[nm], w)
            load(w0[:, 608:1632].rearrange("p (c n) -> p c n", c=4),
                 a["L0_xattn_W_f1"].rearrange("(c p) n -> p c n", p=P), w)
            load(w0[:, 1632:2144], a["L0_xattn_W_f2"], w)

            def col(v):
                return v.rearrange("(p o) -> p o", o=1)
            for i, nm in enumerate(("b_d2v", "b_img", "b_txt")):
                load(bias0[:, i:i + 1], col(a["L0_xattn_" + nm]), w)
            for i, nm in enumerate(("L0_xattn_b_att0", "L0_xattn_b_att1")):
                for h in range(2):
                    load(bias0[64 * h:64 * h + 64, 3 + i:4 + i], col(a[nm]), w)
                    load(batt[:, i, 64 * h:64 * h + 64], a[nm].rearrange("(o n) -> o n", o=1).partition_broadcast(P), w)
            load(bias0[:, 5:9], a["L0_xattn_b_f1"].rearrange("(f p) -> p f", p=P), w)
            load(bf2[:, :], a["L0_xattn_b_f2"].rearrange("(o n) -> o n", o=1).partition_broadcast(P), w)
            load(gates[:, 0:4], a["g_xattn"].rearrange("(o n) -> o n", o=1).partition_broadcast(P), w)
            load(gates[:, 4:8], a["g_ffn"].rearrange("(o n) -> o n", o=1).partition_broadcast(P), w)
            for i, nm in enumerate(("w_gate", "w_up")):
                load(wff[:, 3 * i:3 * i + 3, :], a["L0_ffn_" + nm].rearrange("(c p) n -> p c n", p=P), sem("loaded_wff"))
            load(wff[:, 6:9, :], a["L0_ffn_w_down"].rearrange("p (c n) -> p c n", c=3), sem("loaded_wff"))
            r = sem("loaded_rest")
            load(wq[1][:, :], a["L1_xattn_W_Q"], r)
            load(wk[1][:, :], a["L1_xattn_W_K"], r)
            load(wv[1][:, :], a["L1_xattn_W_V"], r)
            load(wo[1][:, 0, :], a["L1_xattn_W_O"], r)
            for i, nm in enumerate(("L1_xattn_ln_lat_g", "L1_xattn_ln_lat_b")):
                load(lng[:, i:i + 1], col(a[nm]), r)
            for i, nm in enumerate(("L1_xattn_ln_in_g", "L1_xattn_ln_in_b")):
                load(lng[0:C, 2 + i:3 + i], col(a[nm]), r)
            for i, nm in enumerate(("ln1_g", "ln1_b", "ln2_g", "ln2_b")):
                load(lng[:, 4 + i:5 + i], col(a["L2_ffn_" + nm]), r)
            for l in (2, 3):
                load(wq[l][:, :], a[f"L{l}_xattn_Wq"], r)
                load(wk[l][:, :], a[f"L{l}_xattn_Wk"], r)
                load(wv[l][:, :], a[f"L{l}_xattn_Wv"], r)
                load(wo[l][:, :, :], a[f"L{l}_xattn_Wo"].rearrange("(c p) n -> p c n", p=P), r)
            load(bqk[:, 0:1], col(a["L2_xattn_bq"]), r)
            load(bqk[:, 1:2], col(a["L2_xattn_bk"]), r)
            row = lambda v: v.rearrange("(o n) -> o n", o=1)
            load(bv2[:, :], col(a["L2_xattn_bv"]), r)
            load(rows[:, 0, :], row(a["L2_xattn_bo"]), r)
            load(rows[:, 1, :], row(a["L3_xattn_bo"]), r)
            load(gw[1][:, :], a["L1_ffn_switch_w"], r)
            load(gw[3][:, :], a["L3_ffn_gate_w"], r)
            load(gwn[:, :], a["L2_ffn_gate_w"], r)
            load(gb[:, 0, :], row(a["L1_ffn_switch_b"]).partition_broadcast(P), r)
            load(gb[:, 1, :], row(a["L3_ffn_gate_b"]).partition_broadcast(P), r)
            load(attw[:, :], a["L2_ffn_attn_w"], r)
            sp.wait_ge(sem("constants"), 1)
            load(sorted_x.rearrange("(q p) d -> p q d", p=P), zero[:, :].unsqueeze(1).to_broadcast([P, max(NQ.values()), D]),
                 sem("sorted_cleared"))

            for l in (1, 2, 3):
                if last < 2 * l + 2:
                    continue
                t, par = table(l), sem("loaded_experts")
                if l == 1:
                    sp.wait_ge(sem("att_open"), 1)
                else:
                    sp.wait_ge(sem("w_staged"), QB[l])
                if l == 2:
                    for i, nm in enumerate(("gate_proj", "up_proj")):
                        for e in range(E):
                            load(t[:, e, F * i:F * i + F].rearrange("p (f n) -> p f n", n=P),
                                 a["L2_ffn_" + nm][e].rearrange("(f k) n -> k f n", k=P), par)
                    load(t[:, :, 2 * F:3 * F], a["L2_ffn_down_proj"].rearrange("e k n -> k e n"), par)
                else:
                    load(t[:, :, 0:F], a[f"L{l}_ffn_w1"].rearrange("e k n -> k e n"), par)
                    for e in range(E):
                        load(t[:, e, F:2 * F].rearrange("p (f n) -> p f n", n=P),
                             a[f"L{l}_ffn_w2"][e].rearrange("(f k) n -> k f n", k=P), par)
                    load(t[:, :, 2 * F:2 * F + D], a[f"L{l}_ffn_b2"].partition_broadcast(P), par)
                    for e in range(E):
                        load(t[:, e, 2 * F + D:2 * F + D + NF],
                             a[f"L{l}_ffn_b1"][e].rearrange("(f p) -> p f", p=P), par)
                N_PAR[l] = loads[par.name]

                def load_tile(i, s_):
                    rows_ = sorted_x[bass.ds((4 * i + s_) * P, P), :] if not isinstance(i, int) else \
                        sorted_x[(4 * i + s_) * P:(4 * i + s_ + 1) * P, :]
                    sp.dma_start(xq[:, s_, :], rows_).then_inc(sem(f"xq_loaded{s_}"), 16)

                def store_tiles(i):
                    sp.wait_ge(sem("y_taken"), QB[l] + 4 * i + 6)
                    if isinstance(i, int):
                        dst, src = sorted_y[4 * i * P:4 * (i + 1) * P, :], yall[:, 4 * i:4 * i + 4, :]
                    else:
                        dst, src = sorted_y[bass.ds(i * 4 * P, 4 * P), :], yall[:, bass.ds(4 * i, 4), :]
                    sp.dma_start(dst.rearrange("(q p) d -> p q d", p=P), src).then_inc(sem("y_stored"), 16)

                turns = NQ[l] // 4
                sp.wait_ge(sem("scattered"), 16 * NT * (KB[l] + TOPK[l]))
                for s_ in range(4):
                    load_tile(0, s_)
                for s_ in range(4):
                    sp.wait_ge(sem("xq_T"), QB[l] + s_ + 1)
                    load_tile(1, s_)
                with sp.Fori(2, turns) as i:
                    for s_ in range(4):
                        sp.wait_ge(sem("xq_T"), 4 * i + (QB[l] + s_ - 3))
                        load_tile(i, s_)
                    store_tiles(i - 2)
                store_tiles(turns - 2)
                store_tiles(turns - 1)
            sp.wait_ge(sem("x_final"), 1)
            sp.dma_start(out.rearrange("b s d -> (b s) d").rearrange("(j p) d -> p j d", p=P), x[:, :, :]).then_inc(sem("stored"), 16)
            sp.wait_ge(sem("stored"), 16)

        N_PAR.update({l: N_PAR.get(l, 0) for l in TOPK})
        N_W0, N_REST = loads[sem("loaded_w0").name], loads[sem("loaded_rest").name]

        ctok = view(0, NT * C).rearrange("p (j d) -> p j d", d=C)
        qctx = view(1536, 768).bitcast(BF16).rearrange("p (j d) -> p j d", d=C)
        rnd = view(2304, 2048)
        qT = view(4352, 1024).bitcast(BF16)
        qtok = view(5376, 1024).bitcast(BF16).rearrange("p (j d) -> p j d", d=D)
        act0 = view(6400, 2048)
        fused = view(8448, 2048)
        kT = [view(10496 + 2048 * i, 2048) for i in range(2)]
        ktok = [view(14592 + 2048 * i, 2048).rearrange("p (j d) -> p j d", d=D) for i in range(2)]
        prob = view(18688, 1024)
        probT = view(19712, 1024).rearrange("p (g n) -> p g n", g=NG)
        avg = view(20736, B)
        qavg = view(20768, B // 2).bitcast(BF16)
        smax = view(20784, 16)
        ssum = view(20800, 16)
        srec = view(20816, 16)
        h0 = view(10496, 8192).rearrange("p (f t) -> p f t", f=NF)
        qh = view(0, 4096).bitcast(BF16).rearrange("p (f t) -> p f t", f=NF)
        up0 = view(0, NI * T).rearrange("p (f t) -> p f t", f=NI)
        gate0 = view(6144, NI * T).rearrange("p (f t) -> p f t", f=NI)
        sig0 = view(12288, NI * T).rearrange("p (f t) -> p f t", f=NI)

        NSUB = {1: 2, 2: 4}
        ctxs = view(0, GT, C)
        def att(l):
            w = WIN[l]
            o = 256
            d = {}
            d["q"] = view(o, w // P * GT).rearrange("p (c t) -> p c t", t=GT)
            o += 2048
            n = 8 if l == 3 else 128 // HEADS[l] and (32 // (P // HEADS[l]))
            d["k"] = view(o, n * GT).rearrange("p (c t) -> p c t", t=GT)
            o += 2048
            if l == 3:
                d["v"] = view(o, 2 * w).rearrange("p (h n) -> p h n", h=2)
            else:
                n, dh = NSUB[l], P // HEADS[l]
                d["v"] = view(o, 8 * n * (64 + dh)).rearrange("p (b n) -> p b n", b=8)
                d["v_own"] = d["v"].rearrange("p b (j x) -> p b j x", j=n)
                d["v_all"] = view(o, 8 * n * (64 + dh))
            o += 2304
            d["p"] = view(o, 2048).rearrange("p (u n) -> p u n", u=4)
            o += 2048
            d["pt"] = view(o, 1024).rearrange("p (u h n) -> p u h n", u=2, n=P)
            o += 1024
            d["o"] = view(o, 2048)
            o += 2048
            d["ot"] = view(o, 256)
            o += 256
            d["max"], d["sum"], d["rec"] = (view(o + 32 * k, 32).rearrange("p (u n) -> p u n", u=4) for k in range(3))
            return d

        SCALE = {0: 128.0 ** -0.5, 1: 0.25, 2: 8.0 ** -0.5, 3: 0.125}
        CLAMP = 10000.0 / SCALE[2]

        SQRTS = {"one": 1, "two": 2, "both": 2}
        plan = [("one", "ctx"), ("one", "x")]
        if last >= 2: plan += [("one", "x")]
        if last >= 3: plan += [("two", "x")]
        if last >= 4: plan += [("one", "x")]
        if last >= 5: plan += [("one", "x")]
        if last >= 6: plan += [("both", "x"), ("one", "h")]
        if last >= 7: plan += [("one", "x")]
        if last >= 8: plan += [("one", "x")]
        sq_before = [sum(SQRTS[k] for k, _ in plan[:i]) for i in range(len(plan) + 1)]

        @block.gpsimd
        def _(g):
            own = Own(g, sem, "gp_own")
            own(g.memset(ident[:, :], 0.0))
            own(g.memset(ones[:, :], 1.0))
            own(g.memset(onesb[:, :], 1.0))
            own(g.memset(zero[:, :], 0.0))
            own(g.memset(magic[:, :], MAGIC))
            own(g.memset(tiles_a[:, :], 0.0))
            own(g.memset(tiles_b[:, :], 0.0))
            own(g.iota(tile_i[:, :], pattern=[[1, max(NQ.values())]], base=0, channel_multiplier=0))
            for i, n in ((0, COUNT0[0]), (1, COUNT0[1]), (5, COUNT0[5]), (6, COUNT0[6])):
                w = 4 if i == 1 else 1
                own(g.memset(invcount[:, i:i + w], 1.0 / n))
            for e in range(E):
                own(g.memset(rank[:, e:e + 1], float(E - e)))
            own.wait()
            own(g.affine_select(out=ident[:, :], in_=ident[:, :], compare_op=ALU.not_equal, fill=1.0, base=0,
                                pattern=[[-1, P]], channel_multiplier=1))
            own(g.affine_select(out=before[:, :], in_=onesb[:, :], compare_op=ALU.is_gt, fill=0.0, base=0,
                                pattern=[[1, P]], channel_multiplier=-1))
            own.wait()
            own(g.tensor_copy(identb[:, :], ident[:, :]), "constants")

            def sum_rows():
                g.wait_ge(sem("wsum_ready"), 1)
                g.partition_all_reduce(wtot[:, :], wsum[:, :], P, RED.add).then_inc(sem("wtot_ready"), 1)

            sum_rows()
            n_max = 6 + (5 if last >= 2 else 0)
            for k in range(n_max):
                g.wait_ge(sem("amaxp_ready"), k + 1)
                g.partition_all_reduce(amaxg[:, :], amaxp[:, :], P, RED.max).then_inc(sem("amaxg_ready"), 1)

            for l in (1, 2, 3):
                if last < 2 * l + 1:
                    continue
                src = ctxnT if l == 1 else ctxT
                g.wait_ge(sem("norm_feature"), NC * (3 if l == 1 else 1) + 0)
                g.wait_ge(sem("att_open"), l)
                if l != 3:
                    g.memset(att(l)["v_all"], 0.0).then_inc(sem("v_cleared"), 1)
                with g.Fori(0, NG) as i:
                    g.wait_ge(sem(f"v_mm_{l}"), 4 * i + 4 if l == 3 else i + 1)
                    g.tensor_copy(ctxs[:, :], src[:, bass.ds(i * GT, GT)]).then_inc(sem("ctx_staged"), 1)
                if last < 2 * l + 2:
                    continue
                if l == 1:
                    g.wait_ge(sem("sorted_cleared"), 16)
                for k in range(TOPK[l]):
                    g.wait_ge(sem("row_ready"), KB[l] + k + 1)
                    for j in range(NT):
                        g.indirect_dma_start(sorted_x, bass.IndirectOffsetOnAxis(row[:, k, j:j + 1], 0), xh[:, j, :], None
                                             ).then_inc(sem("scattered"), 16)
                g.wait_ge(sem("y_stored"), 16 * (QB[l] + NQ[l]) // 4)
                for j in range(NT):
                    for k in range(TOPK[l]):
                        g.indirect_dma_start(ytok[:, k, j, :], None, sorted_y[0:NQ[l] * P, :], bass.IndirectOffsetOnAxis(row[:, k, j:j + 1], 0)
                                             ).then_inc(sem(f"gathered{j // 4}"), 16)

        @block.vector
        def _(v):
            own = Own(v, sem, "vec_own")
            k_norm = [0]
            k_max = [0]

            def statistics(src, tiles):
                for j in tiles:
                    own(v.bn_stats(bst[:, j, :], src[:, j, :]))

            def normalise(src, width, kind, outs, done=0):
                statistics(src, range(done, NT))
                own.wait()
                for j in range(NT):
                    own(v.bn_aggr(mv[:, j, :], bst[:, j, :]))
                own.wait()
                k = sq_before[k_norm[0]]
                v.tensor_scalar(st1[:, :], mv[:, :, 1], EPS, None, ALU.add).then_inc(sem("var_ready"), 1)
                v.wait_ge(sem("sd_ready"), k + 1)
                own(v.reciprocal(rstd[:, :], st2[:, :]))
                own.wait()
                last_r = rstd
                if kind != "one":
                    own(v.tensor_tensor(rstd2[:, :], rstd[:, :], rstd[:, :], ALU.mult))
                    own.wait()
                    own(v.tensor_tensor(rstd2[:, :], rstd2[:, :], mv[:, :, 1], ALU.mult))
                    own.wait()
                    v.tensor_scalar(st1[:, :], rstd2[:, :], EPS, None, ALU.add).then_inc(sem("var_ready"), 1)
                    v.wait_ge(sem("sd_ready"), k + 2)
                    own(v.reciprocal(rstd2[:, :], st2[:, :]))
                    own.wait()
                    own(v.tensor_tensor(rstd2[:, :], rstd2[:, :], rstd[:, :], ALU.mult))
                    own.wait()
                    last_r = rstd2
                for j in range(NT):
                    if kind == "both":
                        own(v.tensor_scalar(outs[1][:, j, :], src[:, j, :], mv[:, j, 0:1], rstd[:, j:j + 1],
                                            ALU.subtract, ALU.mult))
                    v.tensor_scalar(outs[0][:, j, :], src[:, j, :], mv[:, j, 0:1], last_r[:, j:j + 1],
                                    ALU.subtract, ALU.mult).then_inc(sem("norm_ready"), 1)
                k_norm[0] += 1

            def scale_from(parts, floor, levels):
                own.wait()
                v.tensor_reduce(amaxp[:, :], parts, AX.X, ALU.max, apply_absolute_value=True).then_inc(sem("amaxp_ready"), 1)
                k_max[0] += 1
                v.wait_ge(sem("amaxg_ready"), k_max[0])
                if floor == 1e-8:
                    own(v.tensor_scalar(iscale[:, :], amaxg[:, :], floor, 1.0 / levels, ALU.max, ALU.mult))
                else:
                    own(v.tensor_scalar(iscale[:, :], amaxg[:, :], 1.0 / levels, floor, ALU.mult, ALU.max))
                own.wait()
                own(v.reciprocal(irecip[:, :], iscale[:, :]))
                own.wait()

            def quantise(dst, src, scratch):
                own(v.tensor_scalar(scratch, src, irecip[:, 0:1], MAGIC, ALU.mult, ALU.add))
                own.wait()
                own(v.tensor_scalar(dst, scratch, MAGIC, None, ALU.subtract))

            def out_scale(i, w):
                own(v.tensor_tensor(oscale[:, i:i + 1], iscale[:, :], wscale[:, w:w + 1], ALU.mult))

            v.wait_ge(sem("constants"), 1)
            for l, n in ((1, 2), (2, 4)):
                own(v.tensor_reduce(headmask[l][:, :], ident[:, :].rearrange("p (a j d) -> p j a d", a=4, j=n),
                                    AX.XY, ALU.add))
            v.wait_ge(sem("loaded_w0"), 16 * N_W0)
            for i, (_, lo, n) in enumerate(W0):
                ins = v.tensor_reduce(wsum[:, i:i + 1], w0[:, lo:lo + n], AX.X, ALU.add, apply_absolute_value=True)
                own(ins)
            own.wait()
            v.sem_inc(sem("wsum_ready"), 1)
            v.wait_ge(sem("wtot_ready"), 1)
            own(v.tensor_tensor(wscale[:, :], wtot[:, :], invcount[:, :], ALU.mult))
            own.wait()
            own(v.tensor_scalar(wscale[:, :], wscale[:, :], 1e-5, None, ALU.max))
            own.wait()
            own(v.tensor_scalar(whalf[:, :], wscale[:, :], 0.5, None, ALU.mult))
            own(v.tensor_scalar(wnhalf[:, :], wscale[:, :], -0.5, None, ALU.mult))
            own.wait()
            for i, (_, lo, n) in enumerate(W0):
                own(v.tensor_scalar(rnd[:, 0:n], w0[:, lo:lo + n], wnhalf[:, i:i + 1], None, ALU.is_lt))
                own.wait()
                own(v.scalar_tensor_tensor(q0[:, lo:lo + n], w0[:, lo:lo + n], whalf[:, i:i + 1], rnd[:, 0:n],
                                           ALU.is_gt, ALU.subtract))
                own.wait()
            v.sem_inc(sem("q0_ready"), 1)

            v.wait_ge(sem("loaded_wff"), 48)
            wb = wff[:, :, :].rearrange("p c (k i) -> p (c k) i", i=BLK)
            own(v.tensor_reduce(wffs[:, :], wb, AX.X, ALU.max, apply_absolute_value=True))
            own.wait()
            own(v.tensor_scalar(wffs[:, :], wffs[:, :], 1.0 / 7.0, 1e-12, ALU.mult, ALU.max))
            own.wait()
            own(v.reciprocal(wffr[:, :], wffs[:, :]))
            own.wait()
            own(v.tensor_tensor(wb, wb, wffr[:, :].unsqueeze(2).to_broadcast([P, 36, BLK]), ALU.mult))
            own.wait()
            wflat = wff[:, :, :].rearrange("p c n -> p (c n)")
            own(v.tensor_scalar(wflat, wflat, MAGIC, MAGIC, ALU.add, ALU.subtract))
            own.wait()
            own(v.tensor_tensor(wb, wb, wffs[:, :].unsqueeze(2).to_broadcast([P, 36, BLK]), ALU.mult))
            own.wait()
            v.sem_inc(sem("wff_ready"), 1)

            v.wait_ge(sem("loaded_ctx"), 16)
            own(v.tensor_reduce(amax[:, 0:1], ctok[:, :, :], AX.XY, ALU.max, apply_absolute_value=True))
            scale_from(amax[:, 0:1], 1e-8, 127.0)
            quantise(view(1536, 768).bitcast(BF16), view(0, NT * C), rnd[:, 0:NT * C])
            out_scale(0, 0)
            own.wait()
            v.sem_inc(sem("qctx_ready"), 1)
            xhc = xh[:, :, 0:C]
            normalise(ctok, C, "one", [xhc])

            v.wait_ge(sem("loaded_x"), 16)
            v.wait_ge(sem("norm_feature"), 3 * NC)
            normalise(x, D, "one", [xh])
            v.wait_ge(sem("norm_ready"), 2 * NT)
            own(v.tensor_reduce(amax[:, 0:1], xh[:, :, :], AX.XY, ALU.max, apply_absolute_value=True))
            scale_from(amax[:, 0:1], 1e-8, 127.0)
            quantise(view(5376, 1024).bitcast(BF16), xh[:, :, :].rearrange("p j d -> p (j d)"), rnd)
            out_scale(1, 2)
            own.wait()
            v.sem_inc(sem("qtok_ready"), 1)

            def chunk_maxima(buf, name, base=0, n=NC):
                for c in range(n):
                    v.wait_ge(sem(name), base + c + 1)
                    own(v.tensor_reduce(amax[:, c:c + 1], buf(c), AX.X, ALU.max, apply_absolute_value=True))

            v.wait_ge(sem("lin0"), 2 * NC)
            chunk_maxima(lambda c: act0[:, CH * c:CH * c + CH], "act0_ready", NC)
            scale_from(amax[:, 0:NC], 1e-8, 127.0)
            quantise(qT, act0, rnd)
            out_scale(2, 1)
            own.wait()
            v.sem_inc(sem("qT_ready"), 1)
            chunk_maxima(lambda c: act0[:, CH * c:CH * c + CH], "act0_ready", 2 * NC)
            scale_from(amax[:, 0:NC], 1e-8, 127.0)
            own(v.tensor_reduce(avg[:, :], act0.rearrange("p (b s) -> p b s", s=S), AX.X, ALU.add))
            quantise(qT, act0, rnd)
            out_scale(3, 3)
            out_scale(0, 4)
            own.wait()
            own(v.tensor_scalar(avg[:, :], avg[:, :], 1.0 / S, None, ALU.mult))
            own.wait()
            v.sem_inc(sem("qT_ready"), 1)
            for r in range(2):
                for c in range(NC):
                    v.wait_ge(sem("ktok_mm"), NC * r + c + 1)
                    own(v.scalar_tensor_tensor(
                        ktok[r][:, 4 * c:4 * c + 4, :], ps[:, 4 + c, :].rearrange("p (j d) -> p j d", d=D),
                        oscale[:, 3:4] if r == 0 else oscale[:, 0:1],
                        batt[:, r, :].unsqueeze(1).to_broadcast([P, 4, P]), ALU.mult, ALU.add
                    ), "ktok_ready")

            for r in range(2):
                for u in range(2):
                    lo = 8 * u
                    sp_ = ps[:, u, :].rearrange("p (n s) -> p n s", s=S)
                    pr = prob[:, 512 * u:512 * u + 512].rearrange("p (n s) -> p n s", s=S)
                    v.wait_ge(sem("s0_mm"), 2 * r + u + 1)
                    own(v.tensor_reduce(smax[:, lo:lo + 8], sp_, AX.X, ALU.max))
                    own.wait()
                    v.tensor_tensor(pr, sp_, smax[:, lo:lo + 8].unsqueeze(2).to_broadcast([P, 8, S]),
                                    ALU.subtract).then_inc(sem("s0_sub"), 1)
                for u in range(2):
                    lo = 8 * u
                    pr = prob[:, 512 * u:512 * u + 512].rearrange("p (n s) -> p n s", s=S)
                    v.wait_ge(sem("s0_exp"), 2 * r + u + 1)
                    own(v.tensor_reduce(ssum[:, lo:lo + 8], pr, AX.X, ALU.add))
                    own.wait()
                    own(v.reciprocal(srec[:, lo:lo + 8], ssum[:, lo:lo + 8]))
                    own.wait()
                    v.tensor_tensor(pr, pr, srec[:, lo:lo + 8].unsqueeze(2).to_broadcast([P, 8, S]),
                                    ALU.mult).then_inc(sem("s0_prob"), 1)
                fv = fused.rearrange("p (u n c s) -> p u c n s", u=2, c=2, s=S)
                for u in range(2):
                    for c in range(2):
                        v.wait_ge(sem("av0_mm"), 4 * r + 2 * u + c + 1)
                        own(v.scalar_tensor_tensor(fv[:, u, c], ps[:, 4 + 2 * u + c, :].rearrange("p (n s) -> p n s", s=S),
                                                   0.1, fv[:, u, c], ALU.mult, ALU.add), "fused_ready")
            own.wait()
            own(v.tensor_reduce(amax[:, 0:1], fused, AX.X, ALU.max, apply_absolute_value=True))
            own(v.tensor_reduce(amax[:, 1:2], avg, AX.X, ALU.max, apply_absolute_value=True))
            scale_from(amax[:, 0:2], 1e-8, 127.0)
            quantise(qT, fused, rnd)
            own.wait()
            quantise(qavg, avg, rnd[:, 0:B])
            out_scale(1, 5)
            own.wait()
            v.sem_inc(sem("qT_ready"), 1)
            for n in range(NF * NC):
                f, c = n // NC, n % NC
                v.wait_ge(sem("h0_ready"), n + 1)
                own(v.tensor_reduce(amax[:, n:n + 1], h0[:, f, CH * c:CH * c + CH], AX.X, ALU.max,
                                    apply_absolute_value=True))
            v.wait_ge(sem("gates_ready"), 1)
            own(v.scalar_tensor_tensor(x[:, :, :], bf2[:, :].unsqueeze(1).to_broadcast([P, NT, P]), gates[:, 0:1],
                                       x[:, :, :], ALU.mult, ALU.add))
            scale_from(amax[:, 0:16], 1e-8, 127.0)
            out_scale(2, 6)
            own.wait()
            own(v.tensor_tensor(oscale[:, 2:3], oscale[:, 2:3], gates[:, 0:1], ALU.mult))
            for f in range(NF):
                own.wait()
                own(v.tensor_scalar(h0[:, f, :], h0[:, f, :], irecip[:, 0:1], MAGIC, ALU.mult, ALU.add))
                own.wait()
                v.tensor_scalar(qh[:, f, :], h0[:, f, :], MAGIC, None, ALU.subtract).then_inc(sem("qh_ready"), 1)

            def add_tiles(name, scalar, banks=(0, 1), base=0):
                for c in range(NC):
                    v.wait_ge(sem(name), c + 1)
                    own(v.scalar_tensor_tensor(x[:, 4 * c:4 * c + 4, :],
                                               ps[:, banks[c % len(banks)], :].rearrange("p (j d) -> p j d", d=D), scalar,
                                               x[:, 4 * c:4 * c + 4, :], ALU.mult, ALU.add), name + "_used")
                    own.wait()
                    if c < NC - 1:
                        statistics(x, range(4 * c, 4 * c + 4))
                own.wait()
            add_tiles("f2_mm", oscale[:, 2:3])

            def finish():
                own.wait()
                v.sem_inc(sem("x_final"), 1)
            if last == 1:
                return finish()

            normalise(x, D, "one", [xh], NT - 4)
            v.wait_ge(sem("norm_ready"), 3 * NT)
            own(v.tensor_reduce(amax[:, 0:1], xh[:, :, :], AX.XY, ALU.max, apply_absolute_value=True))
            scale_from(amax[:, 0:1], 1e-12, 32767.0)
            xf = xh[:, :, :].rearrange("p j d -> p (j d)")

            def requantise(buf, name=None, rounded=0):
                if rounded:
                    v.wait_ge(sem("rounded"), rounded)
                else:
                    own(v.tensor_scalar(buf, buf, irecip[:, 0:1], MAGIC, ALU.mult, ALU.add))
                    own.wait()
                own(v.tensor_scalar(buf, buf, MAGIC, iscale[:, 0:1], ALU.subtract, ALU.mult), name)
            requantise(xf)
            own.wait()
            v.sem_inc(sem("xq_ready"), 1)
            flat = lambda b: b[:, :, :].rearrange("p f t -> p (f t)")
            for w, buf in ((0, gate0), (1, up0)):
                for n in range(NI * NC):
                    f, c = n // NC, n % NC
                    v.wait_ge(sem("gu_ready"), NI * NC * w + n + 1)
                    own(v.tensor_reduce(amax[:, n:n + 1], buf[:, f, CH * c:CH * c + CH], AX.X, ALU.max,
                                        apply_absolute_value=True))
                scale_from(amax[:, 0:NI * NC], 1e-12, 32767.0)
                if w:
                    v.sem_inc(sem("scale_ready"), 1)
                for f in range(NI):
                    requantise(buf[:, f, :], "gu_quant", w * f)
                own.wait()
            for f in range(NI):
                v.wait_ge(sem("sig_ready"), f + 1)
                own(v.tensor_scalar(sig0[:, f, :], sig0[:, f, :], MAGIC, 65535.0, ALU.subtract, ALU.min))
                own.wait()
                own(v.scalar_tensor_tensor(gate0[:, f, :], sig0[:, f, :], 1.0 / 65536.0, gate0[:, f, :],
                                           ALU.mult, ALU.mult))
                own.wait()
                own(v.tensor_reduce(amax[:, f:f + 1], gate0[:, f, :], AX.X, ALU.max, apply_absolute_value=True))
            scale_from(amax[:, 0:NI], 1e-12, 32767.0)
            v.sem_inc(sem("scale_ready"), 1)
            for f in range(NI):
                requantise(gate0[:, f, :], None, f and NI - 1 + f)
                own.wait()
                own(v.tensor_tensor(gate0[:, f, :], gate0[:, f, :], up0[:, f, :], ALU.mult))
                own.wait()
                own(v.tensor_reduce(amax[:, f:f + 1], gate0[:, f, :], AX.X, ALU.max, apply_absolute_value=True))
            scale_from(amax[:, 0:NI], 1e-12, 32767.0)
            v.sem_inc(sem("scale_ready"), 1)
            for f in range(NI):
                requantise(gate0[:, f, :], "o_ready", f and 2 * (NI - 1) + f)
            add_tiles("down_mm", gates[:, 4:5], banks=(0, 1, 2, 3))
            if last == 2:
                return finish()

            def attention(l):
                t = att(l)
                sub = 4 if l != 1 else 2
                w = S * sub * 2
                n_k = 4 if l == 3 else NSUB[l]
                steps = {"vec_own": UNITS * (4 if l == 2 else 3) + 2, f"k_ready_{l}": n_k, f"s_sub_{l}": UNITS,
                         f"x_added_{l}": 1}
                if l == 3:
                    steps["o_half_3"] = 4

                def scores(i, u):
                    n = 2 * sub
                    s_ = ps[:, u % 2, 0:w].rearrange("p (n s) -> p n s", s=S)
                    p_ = t["p"][:, u, 0:w].rearrange("p (n s) -> p n s", s=S)
                    v.wait_ge(sem("s_mm"), UNITS * i + (UB[l] + u + 1))
                    if l == 2:
                        own(v.tensor_scalar(p_, s_, CLAMP, -CLAMP, ALU.min, ALU.max))
                        own.wait()
                        s_ = p_
                    own(v.tensor_reduce(t["max"][:, u, 0:n], s_, AX.X, ALU.max))
                    own.wait()
                    own(v.tensor_tensor(p_, s_, t["max"][:, u, 0:n].unsqueeze(2).to_broadcast([P, n, S]),
                                        ALU.subtract), f"s_sub_{l}")

                def weigh(i, u):
                    n = 2 * sub
                    p_ = t["p"][:, u, 0:w].rearrange("p (n s) -> p n s", s=S)
                    v.wait_ge(sem("s_exp"), UNITS * i + (UB[l] + u + 1))
                    own(v.tensor_reduce(t["sum"][:, u, 0:n], p_, AX.X, ALU.add))
                    own.wait()
                    own(v.reciprocal(t["rec"][:, u, 0:n], t["sum"][:, u, 0:n]))
                    own.wait()
                    v.tensor_tensor(p_, p_, t["rec"][:, u, 0:n].unsqueeze(2).to_broadcast([P, n, S]),
                                    ALU.mult).then_inc(sem("prob"), 1)

                def keys(i):
                    if l != 3:
                        if l == 2:
                            v.wait_ge(sem("k_biased"), i + 1)
                            for j in range(n_k):
                                own(v.tensor_scalar(t["k"][:, j, :], t["ot"], headmask[l][:, j:j + 1], None, ALU.mult),
                                    f"k_ready_{l}")
                            return
                        v.wait_ge(sem(f"k_mm_{l}"), i + 1)
                        for j in range(n_k):
                            own(v.tensor_scalar(t["k"][:, j, :], ps[:, 7, 0:GT],
                                                bqk[:, 1:2] if l == 2 else 0.0, headmask[l][:, j:j + 1],
                                                ALU.add, ALU.mult), f"k_ready_{l}")
                    else:
                        for j in range(4):
                            v.wait_ge(sem(f"k_mm_{l}"), 4 * i + (j + 1))
                            own(v.tensor_copy(t["k"][:, 2 * j:2 * j + 2, :],
                                              ps[:, 6 + j % 2, :].rearrange("p (c t) -> p c t", t=GT)),
                                f"k_ready_{l}")

                def outputs(i, quartet):
                    v.wait_ge(sem(f"av_mm_{l}"), 2 * i + (quartet + 1))
                    o_ = t["o"].rearrange("p (k h c s) -> p k h c s", k=8, h=2, c=2)
                    for hh in range(2):
                        own(v.tensor_copy(o_[:, 4 * quartet:4 * quartet + 4, hh, 1, :],
                                          ps[:, 5, :].rearrange("p (k h s) -> p k h s", k=4, h=2)[:, :, hh, :]),
                            f"o_half_{l}")

                def add_group(i):
                    v.wait_ge(sem("att_mm"), i + (GB[l] + 1))
                    xg = x[:, 2 * i:2 * i + 2, :] if isinstance(i, int) else x[:, bass.ds(2 * i, 2), :]
                    own(v.scalar_tensor_tensor(xg, ps[:, 6, 0:GT].rearrange("p (j d) -> p j d", d=D), gates[:, l:l + 1],
                                               xg, ALU.mult, ALU.add), f"x_added_{l}")

                def group(i, first=False, more=True):
                    weigh(i, 1)
                    scores(i, 2)
                    if not first:
                        add_group(i - 1)
                    weigh(i, 2)
                    scores(i, 3)
                    if more:
                        keys(i + 1)
                    weigh(i, 3)
                    if l == 3:
                        outputs(i, 0)
                    if more:
                        scores(i + 1, 0)
                        weigh(i + 1, 0)
                        scores(i + 1, 1)
                    if l == 3:
                        outputs(i, 1)
                    if not first:
                        def tile(q, h):
                            return q[:, 2 * (i - 1) + h, :] if isinstance(i, int) else \
                                q[:, bass.ds(2 * (i - 1) + h, 1), :].rearrange("p o d -> p (o d)")
                        own.wait()
                        for h in range(2):
                            own(v.bn_stats(tile(bst, h), tile(x, h)))

                v.wait_ge(sem("loaded_rest"), 16 * N_REST)
                v.sem_inc(sem(f"x_added_{l}"), 1)
                own.add(f"x_added_{l}", 1)
                v.sem_inc(sem(f"s_sub_{l}"), 2)
                own.add(f"s_sub_{l}", 2)
                if l == 2:
                    v.tensor_copy(bvs[:, :], bv2[:, 0:1].to_broadcast([P, P])).then_inc(sem("bvs_ready"), 1)
                if l > 1:
                    v.wait_ge(sem("offset_mm"), l - 1)
                    own(v.tensor_scalar(offset[:, :], ps[:, 4, 0:P], gates[:, l:l + 1], None, ALU.mult), "offset_ready")
                keys(0)
                scores(0, 0)
                weigh(0, 0)
                scores(0, 1)
                if l > 1:
                    own.wait()
                    own(v.tensor_tensor(x[:, :, :], x[:, :, :], offset[:, :].unsqueeze(1).to_broadcast([P, NT, P]), ALU.add))
                    own.wait()
                group(0, first=True)
                own.wait()
                with v.Fori(1, NG - 1) as i:
                    own.enter(i - 1, steps)
                    group(i)
                    own.leave(NG - 2)
                group(NG - 1, more=False)
                add_group(NG - 1)
                own.wait()

            def one_hot(dst, val, vmax):
                bc = lambda q: q[:, :].unsqueeze(2).to_broadcast([P, NT, E])
                own(v.tensor_reduce(vmax[:, :], val[:, :, :], AX.X, ALU.max))
                own.wait()
                own(v.tensor_tensor(dst[:, :, :], val[:, :, :], bc(vmax), ALU.is_equal))
                own.wait()
                own(v.tensor_tensor(dst[:, :, :], dst[:, :, :], rank[:, :].unsqueeze(1).to_broadcast([P, NT, E]), ALU.mult))
                own.wait()
                own(v.tensor_reduce(v3[:, :], dst[:, :, :], AX.X, ALU.max))
                own.wait()
                own(v.tensor_tensor(dst[:, :, :], dst[:, :, :], bc(v3), ALU.is_equal))
                own.wait()

            def experts(l):
                bc = lambda q: q[:, :].unsqueeze(2).to_broadcast([P, NT, E])
                flat = lambda q: q[:, :, :].rearrange("p j e -> p (j e)")
                if l == 1:
                    own(v.tensor_copy(tile_f[:, :], tile_i[:, :]))
                v.wait_ge(sem("logits"), l)
                logits = ps[:, 7, 0:NT * E].rearrange("p (j e) -> p j e", e=E)
                if l == 2:
                    own(v.tensor_copy(lg[:, :, :], logits))
                else:
                    own(v.tensor_tensor(lg[:, :, :], logits, gb[:, l // 2, :].unsqueeze(1).to_broadcast([P, NT, E]), ALU.add))
                own.wait()
                one_hot(oh1, lg, v1)
                if l == 1:
                    v.tensor_copy(ohb[:, :], flat(oh1)).then_inc(sem("choice_ready"), 1)
                    v.tensor_tensor(tmpe[:, :, :], lg[:, :, :], bc(v1), ALU.subtract).then_inc(sem("route_sub"), 1)
                    v.wait_ge(sem("route_exp"), 1)
                    own(v.tensor_reduce(v2[:, :], tmpe[:, :, :], AX.X, ALU.add))
                    own.wait()
                    own(v.reciprocal(v1[:, :], v2[:, :]))
                    own.wait()
                    own(v.tensor_scalar(v1[:, :], v1[:, :], gates[:, 4 + l:5 + l], None, ALU.mult))
                    weights = (v1,)
                else:
                    own(v.scalar_tensor_tensor(tmpe[:, :, :], oh1[:, :, :], -3.0e38, lg[:, :, :], ALU.mult, ALU.add))
                    own.wait()
                    one_hot(oh2, tmpe, v2)
                    v.tensor_tensor(ohb[:, :], flat(oh1), flat(oh2), ALU.add).then_inc(sem("choice_ready"), 1)
                    v.tensor_tensor(v3[:, :], v2[:, :], v1[:, :], ALU.subtract).then_inc(sem("route_sub"), 1)
                    v.wait_ge(sem("route_exp"), l)
                    own(v.tensor_scalar(v1[:, :], v3[:, :], 1.0, None, ALU.add))
                    own.wait()
                    own(v.reciprocal(v2[:, :], v1[:, :]))
                    own.wait()
                    own(v.tensor_scalar(v2[:, :], v2[:, :], gates[:, 4 + l:5 + l], None, ALU.mult))
                    own.wait()
                    own(v.tensor_tensor(v3[:, :], v3[:, :], v2[:, :], ALU.mult))
                    weights = (v2, v3)

                v.wait_ge(sem("places_mm"), l)
                own(v.tensor_scalar(tiles_a[:, E:], ps[:, 5, 0:E], 1.0 / P, 63.5 / P, ALU.mult, ALU.add))
                own.wait()
                own(v.tensor_scalar(tiles_a[:, E:], tiles_a[:, E:], MAGIC, None, ALU.add))
                own.wait()
                own(v.tensor_scalar(tiles_a[:, E:], tiles_a[:, E:], MAGIC, None, ALU.subtract))
                for k, (dst, src) in enumerate(((tiles_b, tiles_a), (tiles_a, tiles_b), (tiles_b, tiles_a))):
                    own.wait()
                    own(v.tensor_tensor(dst[:, E:], src[:, E:], src[:, E - 2 ** k:2 * E - 2 ** k], ALU.add))
                own.wait()
                first = tiles_b[:, E - 1:2 * E - 1]
                own(v.tensor_scalar(firstrow[:, :], first, float(P), None, ALU.mult))
                own.wait()
                own(v.tensor_tensor(tmpe[:, :, :], ps[:, 6, 0:NT * E].rearrange("p (j e) -> p j e", e=E),
                                    firstrow[:, :].unsqueeze(1).to_broadcast([P, NT, E]), ALU.add))
                for k, oh in enumerate((oh1, oh2)[:TOPK[l]]):
                    own.wait()
                    own(v.tensor_tensor(oh[:, :, :], oh[:, :, :], tmpe[:, :, :], ALU.mult))
                    own.wait()
                    own(v.tensor_reduce(rowf[:, :], oh[:, :, :], AX.X, ALU.add))
                    own.wait()
                    v.tensor_copy(row[:, k, :], rowf[:, :]).then_inc(sem("row_ready"), 1)
                    v.wait_ge(sem("row_ready"), KB[l] + k + 1)
                nq = NQ[l]
                own(v.tensor_tensor(reached[:, 0:nq, :], tile_f[:, 0:nq].unsqueeze(2).to_broadcast([1, nq, E]),
                                    tiles_b[0:1, E - 1:2 * E - 1].unsqueeze(1).to_broadcast([1, nq, E]), ALU.is_ge))
                own.wait()
                own(v.tensor_reduce(expert_f[:, 0:nq], reached[:, 0:nq, :], AX.X, ALU.add))
                own.wait()
                own(v.tensor_scalar(expert_of[:, 0:nq], expert_f[:, 0:nq], 1.0, None, ALU.subtract))
                own.wait()

                def stage(i, s_):
                    e = v.value_load(expert_of[0:1, 4 * i + s_:4 * i + s_ + 1] if isinstance(i, int) else
                                     expert_of[0:1, bass.ds(4 * i + s_, 1)], min_val=0, max_val=E - 1)
                    if not (isinstance(i, int) and 4 * i + s_ < 4):
                        v.wait_ge(sem("y_mm"), 4 * i + (QB[l] + s_ - 3))
                        v.wait_ge(sem("y_taken"), 4 * i + (QB[l] + s_ - 1))
                    v.tensor_copy(wst[:, s_ % 4, 0:WE[l]].unsqueeze(1), table(l)[:, bass.ds(e, 1), :]
                                  ).then_inc(sem("w_staged"), 1)

                def take_output(i, s_):
                    v.wait_ge(sem("y_mm"), 4 * i + (QB[l] + s_ + 1))
                    y = yall[:, 4 * i + s_, :] if isinstance(i, int) else \
                        yall[:, bass.ds(4 * i + s_, 1), :].rearrange("p o d -> p (o d)")
                    src = ps[:, 4 + s_ % 2, 0:P]
                    if l == 2:
                        ins = v.tensor_copy(y, src)
                    else:
                        ins = v.tensor_tensor(y, src, wst[:, s_ % 4, 2 * F:2 * F + D], ALU.add)
                    ins.then_inc(sem("y_taken"), 1)

                def turn(i, first=False, final=False):
                    for s_ in range(4):
                        if not (final and s_ >= 2):
                            stage(i, s_ + 2)
                        if l == 2:
                            v.wait_ge(sem("h_mm"), 8 * i + (HB[l] + 2 * s_ + 2))
                            v.wait_ge(sem("silu_ready"), 4 * i + (s_ + 1))
                            v.tensor_tensor(hT[:, s_ % 2, :, :].rearrange("p f t -> p (f t)"), sg[:, s_ % 2, :], ps[:, 2 + s_ % 2, :], ALU.mult
                                            ).then_inc(sem("gated_ready"), 1)
                        if not (first and s_ == 0):
                            take_output(i, s_ - 1)

                v.wait_ge(sem("loaded_experts"), 16 * N_PAR[l])
                if l == 1:
                    v.sem_inc(sem("y_taken"), 2)
                if l == 2:
                    v.wait_ge(sem("wexpT_ready"), 3 * E)
                stage(0, 0)
                stage(0, 1)
                turn(0, first=True)
                with v.Fori(1, nq // 4 - 1) as i:
                    turn(i)
                turn(nq // 4 - 1, final=True)
                take_output(nq // 4 - 1, 3)

                for n in range(4):
                    v.wait_ge(sem(f"gathered{n}"), 16 * 4 * (KB[l] + TOPK[l]))
                    for k, w in enumerate(weights):
                        own.wait()
                        for j in range(4 * n, 4 * n + 4):
                            own(v.scalar_tensor_tensor(x[:, j, :], ytok[:, k, j, :], w[:, j:j + 1], x[:, j, :],
                                                       ALU.mult, ALU.add))
                    if n < 3:
                        own.wait()
                        statistics(x, range(4 * n, 4 * n + 4))
                own.wait()

            for l in (1, 2, 3):
                normalise(x, D, "two" if l == 1 else "one", [xh], NT - 4)
                v.sem_inc(sem("att_open"), 1)
                attention(l)
                if last == 2 * l + 1:
                    return finish()
                if l != 2:
                    normalise(x, D, "one", [xh], NT - 2)
                else:
                    normalise(x, D, "both", [xh, hres], NT - 2)
                    own.wait()
                    for c in range(NC):
                        v.wait_ge(sem("attw_mm"), c + 1)
                        own(v.tensor_tensor(hres[:, 4 * c:4 * c + 4, :], hres[:, 4 * c:4 * c + 4, :],
                                            ps[:, 4 + c % 2, :].rearrange("p (j d) -> p j d", d=D), ALU.add), "hres_ready")
                    own.wait()
                    own(v.scalar_tensor_tensor(x[:, :, :], hres[:, :, :], gates[:, 6:7], x[:, :, :], ALU.mult, ALU.add))
                    normalise(hres, D, "one", [xh])
                experts(l)
                if last == 2 * l + 2:
                    return finish()

        @block.scalar
        def _(s):
            own = Own(s, sem, "act_own")
            k_norm = [0]
            m_tr = [0]

            k_idle = [0]

            def fetch_table(fn):
                s.activation(idle[:, k_idle[0]:k_idle[0] + 1], ident[:, 0:1], fn)
                k_idle[0] += 1

            def deviations(kind="one"):
                fetch_table(ACT.Sqrt)
                for _ in range(SQRTS[kind]):
                    k_norm[0] += 1
                    s.wait_ge(sem("var_ready"), k_norm[0])
                    s.activation(st2[:, :], st1[:, :], ACT.Sqrt).then_inc(sem("sd_ready"), 1)

            def to_feature(dst, w=P, g=None, b=None):
                m = m_tr[0]
                for c in range(NC):
                    s.wait_ge(sem("norm_T"), NC * m + c + 1)
                    o, i_ = dst[0:w, CH * c:CH * c + CH], ps[0:w, c % 2, :]
                    if g is None:
                        ins = s.copy(o, i_)
                    else:
                        ins = s.activation(o, i_, ACT.Identity, bias=b, scale=g)
                    ins.then_inc(sem("norm_feature"), 1)
                m_tr[0] += 1

            s.wait_ge(sem("constants"), 1)
            fetch_table(ACT.Tanh)
            s.wait_ge(sem("loaded_w0"), 16 * N_W0)
            s.activation(gates[:, :], gates[:, :], ACT.Tanh).then_inc(sem("gates_ready"), 1)
            for n in range(3):
                s.wait_ge(sem("q0_T"), n + 1)
                k = min(8, 17 - 8 * n)
                src = ps[:, n, :].bitcast(BF16).rearrange("p (k n) -> p k n", n=P)
                if n == 0:
                    own(s.copy(q0T[0:C, 0, :], src[0:C, 0, :]))
                    s.copy(q0T[:, 1:8, :], src[:, 1:8, :]).then_inc(sem("q0T_ready"), 1)
                else:
                    s.copy(q0T[:, 8 * n:8 * n + k, :], src[:, 0:k, :]).then_inc(sem("q0T_ready"), 1)
            for n in range(3):
                k = min(4, 9 - 4 * n)
                s.wait_ge(sem("wff_T"), n + 1)
                s.copy(wffT[:, 4 * n:4 * n + k, :], ps[:, 3 + n, 0:P * k].rearrange("p (k n) -> p k n", n=P)
                       ).then_inc(sem("wffT_ready"), 1)
            to_feature(ctxT, C)
            for n in range(2):
                s.wait_ge(sem("qctx_T"), n + 1)
                s.copy(qT[0:C, 1024 * n:1024 * n + 1024], ps[0:C, 2 + n, :].bitcast(BF16)).then_inc(sem("qctxT_ready"), 1)
            deviations()
            s.wait_ge(sem("loaded_rest"), 16 * N_REST)
            def linear(base, name, dst, sc, bi, banks=4):
                for c in range(NC):
                    s.wait_ge(sem("lin0"), base + c + 1)
                    s.activation(dst[:, CH * c:CH * c + CH], ps[:, 4 + c, :], ACT.Identity, bias=bias0[:, bi:bi + 1],
                                 scale=oscale[:, sc:sc + 1]).then_inc(sem(name), 1)
            linear(0, "act0_ready", act0, 0, 0)
            m_tr[0] = 1
            for c in range(NC):
                s.wait_ge(sem("norm_T"), NC + c + 1)
                s.activation(ctxnT[0:C, CH * c:CH * c + CH], ps[0:C, c % 2, :], ACT.Identity, bias=lng[0:C, 3:4],
                             scale=lng[0:C, 2:3]).then_inc(sem("norm_feature"), 2)
            m_tr[0] = 2
            deviations()
            for n in range(2):
                s.wait_ge(sem("qtok_T"), n + 1)
                s.copy(qT[:, 1024 * n:1024 * n + 1024], ps[:, 2 + n, :].bitcast(BF16)).then_inc(sem("qtokT_ready"), 1)
            linear(NC, "fused0_ready", fused, 1, 2)
            s.sem_inc(sem("act0_ready"), NC)
            linear(2 * NC, "act0_ready", act0, 2, 1)
            for r in range(2):
                for c in range(NC):
                    s.wait_ge(sem("lin0"), (3 + r) * NC + c + 1)
                    s.activation(kT[r][:, CH * c:CH * c + CH], ps[:, c, :], ACT.Identity,
                                 bias=bias0[:, 3 + r:4 + r], scale=oscale[:, 3:4] if r == 0 else oscale[:, 0:1]
                                 ).then_inc(sem("kT_ready"), 1)
            for r in range(2):
                for u in range(2):
                    s.wait_ge(sem("s0_sub"), 2 * r + u + 1)
                    pr = prob[:, 512 * u:512 * u + 512]
                    s.activation(pr, pr, ACT.Exp, scale=SCALE[0]).then_inc(sem("s0_exp"), 1)
                for u in range(2):
                    s.wait_ge(sem("pT0_mm"), 2 * r + u + 1)
                    s.copy(probT[:, 4 * u:4 * u + 4, :], ps[:, 2 + u, :].rearrange("p (g n) -> p g n", n=P)
                           ).then_inc(sem("probT0_ready"), 1)
            for n in range(NF * NC):
                f, c = n // NC, n % NC
                s.wait_ge(sem("f1_mm"), n + 1)
                s.activation(h0[:, f, CH * c:CH * c + CH], ps[:, n % 4, :], ACT.Relu, bias=bias0[:, 5 + f:6 + f],
                             scale=oscale[:, 1:2]).then_inc(sem("h0_ready"), 1)
            if last == 1:
                return

            deviations()
            to_feature(xnT)
            for w, buf in ((0, gate0), (1, up0)):
                for n in range(NI * NC):
                    f, c = n // NC, n % NC
                    s.wait_ge(sem("gu_mm"), NI * NC * w + n + 1)
                    s.copy(buf[:, f, CH * c:CH * c + CH], ps[:, n % 4, :]).then_inc(sem("gu_ready"), 1)
                    if w == 1 and c == NC - 1:
                        s.wait_ge(sem("gu_quant"), f + 1)
                        own(s.activation(sig0[:, f, :], gate0[:, f, :], ACT.Sigmoid))
                        own.wait()
                        s.activation(sig0[:, f, :], sig0[:, f, :], ACT.Identity, bias=magic[:, 0:1], scale=65536.0
                                     ).then_inc(sem("sig_ready"), 1)
            for n, buf in enumerate((up0, gate0, gate0)):
                s.wait_ge(sem("scale_ready"), n + 1)
                for f in range(1, NI):
                    s.activation(buf[:, f, :], buf[:, f, :], ACT.Identity, bias=magic[:, 0:1], scale=irecip[:, 0:1]
                                 ).then_inc(sem("rounded"), 1)
            if last == 2:
                return

            def attention(l):
                t = att(l)
                sub = 4 if l != 1 else 2
                w = S * sub * 2

                def expo(i, u):
                    s.wait_ge(sem(f"s_sub_{l}"), UNITS * i + (u + 3))
                    p_ = t["p"][:, u, 0:w]
                    s.activation(p_, p_, ACT.Exp, scale=SCALE[l]).then_inc(sem("s_exp"), 1)

                def probT(i, u):
                    s.wait_ge(sem("pT_mm"), UNITS * i + (UB[l] + u + 1))
                    s.copy(t["pt"][:, u % 2, 0:sub, :], ps[:, 2 + u % 2, 0:sub * P].rearrange("p (h n) -> p h n", n=P)
                           ).then_inc(sem("pT_ready"), 1)

                def queries(i):
                    if l == 3:
                        for j in range(4):
                            s.wait_ge(sem(f"q_mm_{l}"), 4 * i + (j + 1))
                            s.copy(t["q"][:, 2 * j:2 * j + 2, :], ps[:, 6 + j % 2, :].rearrange("p (c t) -> p c t", t=GT)
                                   ).then_inc(sem(f"q_ready_{l}"), 1)
                        return
                    s.wait_ge(sem(f"q_mm_{l}"), i + 1)
                    if l == 2:
                        ins = s.activation(t["q"][:, 0, :], ps[:, 6, 0:GT], ACT.Identity, bias=bqk[:, 0:1])
                        ins.then_inc(sem(f"q_ready_{l}"), 1)
                        s.wait_ge(sem(f"k_mm_{l}"), i + 1)
                        s.activation(t["ot"], ps[:, 7, 0:GT], ACT.Identity, bias=bqk[:, 1:2]).then_inc(sem("k_biased"), 1)
                        return
                    else:
                        ins = s.copy(t["q"][:, 0, :], ps[:, 6, 0:GT])
                    ins.then_inc(sem(f"q_ready_{l}"), 1)

                def values(i):
                    if l == 3:
                        for j in range(4):
                            s.wait_ge(sem(f"v_mm_{l}"), 4 * i + (j + 5))
                            s.copy(t["v"][:, j // 2, 512 * (j % 2):512 * (j % 2) + 512], ps[:, 7 - j % 2, :]
                                   ).then_inc(sem(f"v_ready_{l}"), 1)
                        return
                    s.wait_ge(sem(f"v_mm_{l}"), i + 2)
                    dh = P // HEADS[l]
                    for c in range(2):
                        r = slice(64 * c, 64 * c + 64)
                        ins = s.copy(t["v_own"][r, :, :, 32 * c:32 * c + dh],
                                     ps[r, 7, 0:GT].rearrange("p (b j d) -> p b j d", b=8, d=dh))
                    ins.then_inc(sem(f"v_ready_{l}"), 1)

                def outputs(i, quartet):
                    s.wait_ge(sem(f"av_mm_{l}"), 2 * i + (quartet + 1))
                    o_ = t["o"].rearrange("p (k h c s) -> p k h c s", k=8, h=2, c=2)
                    for hh in range(2):
                        s.copy(o_[:, 4 * quartet:4 * quartet + 4, hh, 0, :],
                               ps[:, 4, :].rearrange("p (k h s) -> p k h s", k=4, h=2)[:, :, hh, :]
                               ).then_inc(sem(f"o_other_{l}"), 1)

                def narrow(i, u):
                    if l == 3:
                        return
                    s.wait_ge(sem(f"av_mm_{l}"), UNITS * i + (u + 1))
                    for c in range(2):
                        ins = s.copy(t["o"][32 * u:32 * u + 32, 0:GT].rearrange("p (h c s) -> p h c s", h=2, c=2)[:, :, c, :],
                                     ps[32 * c:32 * c + 32, 4 + u % 2, 0:P].rearrange("p (h s) -> p h s", h=2))
                    ins.then_inc(sem(f"o_other_{l}"), 1)

                def group(i, more):
                    if l != 3:
                        expo(i, 1)
                    values(i)
                    if l == 3:
                        expo(i, 1)
                    probT(i, 0)
                    expo(i, 2)
                    narrow(i, 0)
                    probT(i, 1)
                    if more:
                        queries(i + 1)
                    expo(i, 3)
                    narrow(i, 1)
                    probT(i, 2)
                    if l == 3:
                        outputs(i, 0)
                    if more:
                        expo(i + 1, 0)
                    narrow(i, 2)
                    probT(i, 3)
                    narrow(i, 3)
                    if l == 3:
                        outputs(i, 1)

                if l != 3:
                    s.wait_ge(sem("v_cleared"), l)
                    s.sem_inc(sem(f"o_other_{l}"), 2)
                fetch_table(ACT.Exp)
                queries(0)
                expo(0, 0)
                with s.Fori(0, NG - 1) as i:
                    group(i, True)
                group(NG - 1, False)

            def experts(l):
                fetch_table(ACT.Exp)
                s.wait_ge(sem("route_sub"), l)
                if l == 1:
                    s.activation(tmpe[:, :, :], tmpe[:, :, :], ACT.Exp).then_inc(sem("route_exp"), 1)
                else:
                    s.activation(v3[:, :], v3[:, :], ACT.Exp).then_inc(sem("route_exp"), 1)
                if l == 2:
                    t = table(l)
                    for n in range(3 * E):
                        s.wait_ge(sem("wexp_T"), n + 1)
                        s.copy(t[:, n // 3, F * (n % 3):F * (n % 3) + F], ps[:, n % 4, :]).then_inc(sem("wexpT_ready"), 1)
                fn = ACT.Gelu_apprx_tanh if l == 1 else ACT.Relu

                def operand(i, s_):
                    s.wait_ge(sem("xq_T"), 4 * i + (QB[l] + s_ + 1))
                    o, src = xqT[:, s_ % 2, :], ps[:, 6 + s_ % 2, 0:P]
                    if l == 2:
                        ins = s.activation(o, src, ACT.Identity, bias=lng[:, 7:8], scale=lng[:, 6:7])
                    else:
                        ins = s.copy(o, src)
                    ins.then_inc(sem("xqT_ready"), 1)

                def hidden(i, s_):
                    if l == 2:
                        s.wait_ge(sem("h_mm"), 8 * i + (HB[l] + 2 * s_ + 1))
                        s.activation(sg[:, s_ % 2, :], ps[:, s_ % 2, :], ACT.Silu).then_inc(sem("silu_ready"), 1)
                        return
                    b1 = wst[:, s_ % 4, 2 * F + D:2 * F + D + NF]
                    s.wait_ge(sem("h_mm"), 4 * i + (HB[l] + s_ + 1))
                    for f in range(NF):
                        s.activation(hT[:, s_ % 2, f, :], ps[:, s_ % 2, P * f:P * f + P], fn, bias=b1[:, f:f + 1]
                                     ).then_inc(sem("hidden_ready"), 1)

                fetch_table(fn if l != 2 else ACT.Silu)
                operand(0, 0)
                turns = NQ[l] // 4

                def turn(i, final=False):
                    for s_ in range(4):
                        if not (final and s_ == 3):
                            operand(i, s_ + 1)
                        hidden(i, s_)
                with s.Fori(0, turns - 1) as i:
                    turn(i)
                turn(turns - 1, final=True)

            for l in (1, 2, 3):
                deviations("two" if l == 1 else "one")
                if l == 1:
                    to_feature(xnT, g=lng[:, 0:1], b=lng[:, 1:2])
                else:
                    to_feature(xnT)
                attention(l)
                if last == 2 * l + 1:
                    return
                if l == 2:
                    deviations("both")
                    to_feature(xnT, g=lng[:, 4:5], b=lng[:, 5:6])
                    s.wait_ge(sem("prep2_T"), 1)
                    s.copy(attwT[:, :], ps[:, 7, 0:P])
                    s.copy(gw[2][:, :], ps[:, 7, P:P + E]).then_inc(sem("prep2_ready"), 1)
                    deviations()
                    s.wait_ge(sem("attw_mm"), NC)
                    to_feature(xnT, g=lng[:, 6:7], b=lng[:, 7:8])
                else:
                    deviations()
                    to_feature(xnT)
                experts(l)
                if last == 2 * l + 2:
                    return

        @block.tensor
        def _(t_):
            pe = t_
            m_tr = [0]
            k_norm = [0]

            def tiles_T(src, w, wait, feature):
                m = m_tr[0]
                for c in range(NC):
                    if c >= 2:
                        pe.wait_ge(sem("norm_feature"), feature + c - 1)
                    for k in range(4):
                        j = 4 * c + k
                        if wait:
                            pe.wait_ge(sem("norm_ready"), NT * k_norm[0] + j + 1)
                        ins = pe.transpose(ps[0:w, c % 2, P * k:P * k + P], src[:, j, :], ident[:, :])
                    ins.then_inc(sem("norm_T"), 1)
                m_tr[0] += 1
                if wait:
                    k_norm[0] += 1

            pe.wait_ge(sem("constants"), 1)
            pe.wait_ge(sem("q0_ready"), 1)
            for n in range(17):
                src = q0[:, 0:96] if n == 0 else q0[:, 96 + 128 * (n - 1):96 + 128 * n]
                o = ps[0:src.shape[1], n // 8, :].bitcast(BF16)[:, P * (n % 8):P * (n % 8) + P]
                ins = pe.transpose(o, src, identb[:, :])
                if n % 8 == 7 or n == 16:
                    ins.then_inc(sem("q0_T"), 1)
            pe.wait_ge(sem("wff_ready"), 1)
            for n in range(9):
                ins = pe.transpose(ps[:, 3 + n // 4, P * (n % 4):P * (n % 4) + P], wff[:, n, :], ident[:, :])
                if n % 4 == 3 or n == 8:
                    ins.then_inc(sem("wff_T"), 1)
            pe.wait_ge(sem("loaded_ctx"), 16)
            pe.wait_ge(sem("q0T_ready"), 3)
            tiles_T(ctok, C, False, 0)

            def bf_tiles_T(src, w, name):
                for j in range(NT):
                    o = ps[0:w, 2 + j // 8, :].bitcast(BF16)[:, P * (j % 8):P * (j % 8) + P]
                    ins = pe.transpose(o, src[:, j, :], identb[:, :])
                    if j % 8 == 7:
                        ins.then_inc(sem(name), 1)
            pe.wait_ge(sem("qctx_ready"), 1)
            bf_tiles_T(qctx, C, "qctx_T")
            pe.wait_ge(sem("qctxT_ready"), 2)
            pe.wait_ge(sem("wffT_ready"), 3)
            for c in range(NC):
                pe.matmul(ps[:, 4 + c, :], q0T[0:C, 0, :], qT[0:C, CH * c:CH * c + CH], start=True, stop=True
                          ).then_inc(sem("lin0"), 1)
            pe.wait_ge(sem("norm_feature"), NC)
            for c in range(NC):
                if c >= 2:
                    pe.wait_ge(sem("norm_feature"), NC + 2 * (c - 1))
                for k in range(4):
                    j = 4 * c + k
                    pe.wait_ge(sem("norm_ready"), j + 1)
                    ins = pe.transpose(ps[0:C, c % 2, P * k:P * k + P], xh[:, j, 0:C], ident[:, :])
                ins.then_inc(sem("norm_T"), 1)
            m_tr[0] = 2
            k_norm[0] = 2
            pe.wait_ge(sem("qtok_ready"), 1)
            bf_tiles_T(qtok, D, "qtok_T")
            pe.wait_ge(sem("qtokT_ready"), 2)
            pe.wait_ge(sem("act0_ready"), NC)
            for c in range(NC):
                pe.matmul(ps[:, 4 + c, :], q0T[:, 2, :], qT[:, CH * c:CH * c + CH], start=True, stop=True
                          ).then_inc(sem("lin0"), 1)
            pe.wait_ge(sem("fused0_ready"), NC)
            pe.wait_ge(sem("qT_ready"), 1)
            for c in range(NC):
                pe.matmul(ps[:, 4 + c, :], q0T[:, 1, :], qT[:, CH * c:CH * c + CH], start=True, stop=True
                          ).then_inc(sem("lin0"), 1)
            pe.wait_ge(sem("act0_ready"), 3 * NC)
            pe.wait_ge(sem("qT_ready"), 2)
            for r in range(2):
                for c in range(NC):
                    if r:
                        pe.wait_ge(sem("kT_ready"), c + 1)
                    pe.matmul(ps[:, c, :], q0T[:, 3 + r, :], qT[:, CH * c:CH * c + CH], start=True, stop=True
                              ).then_inc(sem("lin0"), 1)
                for c in range(NC):
                    if r:
                        pe.wait_ge(sem("ktok_ready"), c + 1)
                    for k in range(4):
                        j = 4 * c + k
                        ins = pe.matmul(ps[:, 4 + c, P * k:P * k + P], qT[:, P * j:P * j + P], q0T[:, 3 + r, :],
                                        start=True, stop=True)
                    ins.then_inc(sem("ktok_mm"), 1)
            pe.wait_ge(sem("kT_ready"), 2 * NC)
            pe.wait_ge(sem("ktok_ready"), 2 * NC)
            for r in range(2):
                if r:
                    pe.wait_ge(sem("fused_ready"), 4)
                for g in range(NG):
                    for c in range(2):
                        for hh in range(2):
                            b = 4 * g + 2 * hh + c
                            n = 2 * (g % 4) + c
                            ins = pe.matmul(ps[64 * hh:64 * hh + 64, g // 4, S * n:S * n + S],
                                            fused[:, S * b:S * b + S], kT[r][:, S * b:S * b + S], start=True, stop=True)
                    if g % 4 == 3:
                        ins.then_inc(sem("s0_mm"), 1)
                for u in range(2):
                    pe.wait_ge(sem("s0_prob"), 2 * r + u + 1)
                    for g in range(4):
                        ins = pe.transpose(ps[:, 2 + u, P * g:P * g + P], prob[:, 512 * u + P * g:512 * u + P * g + P],
                                           ident[:, :])
                    ins.then_inc(sem("pT0_mm"), 1)
                for u in range(2):
                    pe.wait_ge(sem("probT0_ready"), 2 * r + u + 1)
                    for c in range(2):
                        for g in range(4):
                            for hh in range(2):
                                j = 2 * (4 * u + g) + hh
                                n = 2 * g + hh
                                ins = pe.matmul(ps[:, 4 + 2 * u + c, S * n:S * n + S],
                                                ktok[r][64 * c:64 * c + 64, j, :],
                                                probT[64 * c:64 * c + 64, 4 * u + g, 64 * hh:64 * hh + 64],
                                                start=True, stop=True)
                        ins.then_inc(sem("av0_mm"), 1)
            pe.wait_ge(sem("qT_ready"), 3)
            for n in range(NF * NC):
                f, c = n // NC, n % NC
                if n >= 4:
                    pe.wait_ge(sem("h0_ready"), n - 3)
                pe.matmul(ps[:, n % 4, :], q0T[:, 5 + 2 * f, :], qT[:, CH * c:CH * c + CH], start=True, stop=False)
                pe.matmul(ps[:, n % 4, :], q0T[:, 6 + 2 * f, :],
                          qavg[:, 8 * c:8 * c + 8].unsqueeze(2).to_broadcast([P, 8, S]),
                          start=False, stop=True).then_inc(sem("f1_mm"), 1)

            def token_products(name, n, lhsT, rhs):
                for c in range(NC):
                    if c >= 2:
                        pe.wait_ge(sem(name + "_used"), c - 1)
                    for k in range(4):
                        j = 4 * c + k
                        for f in range(n):
                            ins = pe.matmul(ps[:, c % 2, P * k:P * k + P], lhsT(f, j), rhs(f), start=(f == 0),
                                            stop=(f == n - 1))
                    ins.then_inc(sem(name), 1)
            pe.wait_ge(sem("qh_ready"), NF)
            pe.wait_ge(sem("h0_ready"), NF * NC)
            token_products("f2_mm", NF, lambda f, j: qh[:, f, P * j:P * j + P], lambda f: q0T[:, 13 + f, :])
            if last == 1:
                return

            pe.wait_ge(sem("xq_ready"), 1)
            feature = [3 * NC]

            def norm_T():
                tiles_T(xh, D, True, feature[0])
                feature[0] += NC
                pe.wait_ge(sem("norm_feature"), feature[0])
            norm_T()
            for w in range(2):
                for n in range(NI * NC):
                    f, c = n // NC, n % NC
                    if n + w >= 4 or w:
                        pe.wait_ge(sem("gu_ready"), NI * NC * w + n - 3)
                    pe.matmul(ps[:, n % 4, :], wffT[:, 3 * w + f, :], xnT[:, CH * c:CH * c + CH], start=True, stop=True
                              ).then_inc(sem("gu_mm"), 1)
            for f in range(NI):
                pe.wait_ge(sem("o_ready"), f + 1)
                for c in range(NC):
                    for k in range(4):
                        j = 4 * c + k
                        ins = pe.matmul(ps[:, c, P * k:P * k + P], gate0[:, f, P * j:P * j + P], wffT[:, 6 + f, :],
                                        start=(f == 0 and k == 0), stop=(f == NI - 1 and k == 3))
                    if f == NI - 1:
                        ins.then_inc(sem("down_mm"), 1)
            if last == 2:
                return

            def attention(l):
                t = att(l)
                d = WIN[l] // HEADS[l]
                sub = 4 if l != 1 else 2
                nkk = {1: 2, 2: 4, 3: 4}[l]

                def apart():
                    pe.sem_inc(sem("waited"), 1)

                def at_group(src, i):
                    return src[:, i * GT:i * GT + GT] if isinstance(i, int) else src[:, bass.ds(i * GT, GT)]

                def queries_keys(i):
                    xg = at_group(xnT, i)
                    cg = at_group(ctxnT if l == 1 else ctxT, i)
                    if not (isinstance(i, int) and i == 0):
                        pe.wait_ge(sem(f"x_added_{l}"), i)
                    if l != 3:
                        pe.matmul(ps[:, 6, 0:GT], wq[l][:, :], xg, start=True, stop=True).then_inc(sem(f"q_mm_{l}"), 1)
                        pe.matmul(ps[:, 7, 0:GT], wk[l][:, :], cg, start=True, stop=True).then_inc(sem(f"k_mm_{l}"), 1)
                        return
                    for j in range(4):
                        if j >= 2:
                            pe.wait_ge(sem(f"q_ready_{l}"), 4 * i + (j - 1))
                        for k in range(2):
                            n = 2 * j + k
                            ins = pe.matmul(ps[:, 6 + j % 2, GT * k:GT * k + GT], wq[l][:, P * n:P * n + P], xg,
                                            start=True, stop=True)
                        ins.then_inc(sem(f"q_mm_{l}"), 1)
                    for j in range(4):
                        if j < 2:
                            pe.wait_ge(sem(f"q_ready_{l}"), 4 * i + (j + 3))
                        else:
                            pe.wait_ge(sem(f"k_ready_{l}"), 4 * i + (j - 1))
                        for k in range(2):
                            n = 2 * j + k
                            ins = pe.matmul(ps[:, 6 + j % 2, GT * k:GT * k + GT], wk[l][:, P * n:P * n + P], cg,
                                            start=True, stop=True)
                        ins.then_inc(sem(f"k_mm_{l}"), 1)

                def value_rows(i):
                    pe.wait_ge(sem("ctx_staged"), i + (GB[l] + 1))
                    if l != 3:
                        for hh in range(2):
                            o = ps[:, 7, P * hh:P * hh + P]
                            ins = pe.matmul(o, ctxs[:, P * hh:P * hh + P], wv[l][:, :], start=True, stop=True)
                        ins.then_inc(sem(f"v_mm_{l}"), 1)
                        return
                    for j in range(4):
                        if j > 1:
                            pe.wait_ge(sem(f"v_ready_{l}"), 4 * i + (j - 1))
                        hh, half = j // 2, j % 2
                        pe.matmul(ps[:, 7 - j % 2, :], ctxs[:, P * hh:P * hh + P], wv[l][:, 512 * half:512 * half + 512],
                                  start=True, stop=True).then_inc(sem(f"v_mm_{l}"), 1)

                def scores(i, u):
                    pe.wait_ge(sem(f"s_sub_{l}"), UNITS * i + (u + 1))
                    if u == 0:
                        pe.wait_ge(sem(f"q_ready_{l}"), (4 if l == 3 else 1) * (i + 1))
                        pe.wait_ge(sem(f"k_ready_{l}"), nkk * (i + 1))
                    apart()
                    for c in range(2):
                        for hh in range(2):
                            lo = S * (2 * hh + c)
                            if l != 3:
                                r = 32 * u
                                o = ps[64 * hh:64 * hh + 64, u % 2, 0:2 * sub * S]
                                ins = pe.matmul(o.rearrange("p (h c s) -> p h c s", c=2, s=S)[:, :, c, :], t["q"][r:r + 32, 0, lo:lo + S],
                                                t["k"][r:r + 32, :, lo:lo + S], start=True, stop=True)
                            else:
                                r = 64 * (u % 2)
                                for k in range(4):
                                    ch = 4 * (u // 2) + k
                                    ins = pe.matmul(ps[64 * hh:64 * hh + 64, u % 2, S * (2 * k + c):S * (2 * k + c) + S],
                                                    t["q"][r:r + 64, ch, lo:lo + S], t["k"][r:r + 64, ch, lo:lo + S],
                                                    start=True, stop=True)
                    ins.then_inc(sem("s_mm"), 1)

                def turn(i, u):
                    pe.wait_ge(sem("prob"), UNITS * i + (UB[l] + u + 1))
                    for k in range(sub):
                        ins = pe.transpose(ps[:, 2 + u % 2, P * k:P * k + P], t["p"][:, u, P * k:P * k + P], ident[:, :])
                    ins.then_inc(sem("pT_mm"), 1)

                def values(i, u):
                    pe.wait_ge(sem("pT_ready"), UNITS * i + (UB[l] + u + 1))
                    if l != 3:
                        pe.wait_ge(sem(f"o_other_{l}"), UNITS * i + (u + 1))
                        for hh in range(2):
                            for k in range(sub):
                                ins = pe.matmul(ps[0:64, 4 + u % 2, S * hh:S * hh + S],
                                                t["v"][:, 4 * hh + u, 64 * k:64 * k + 64],
                                                t["pt"][:, u % 2, k, S * hh:S * hh + S], start=(k == 0), stop=(k == sub - 1))
                        ins.then_inc(sem(f"av_mm_{l}"), 1)
                        return
                    apart()
                    for c in range(2):
                        r = 64 * c
                        for hh in range(2):
                            for k in range(sub):
                                pt = t["pt"][r:r + 64, u % 2, k, 64 * hh:64 * hh + 64]
                                h = 2 * (4 * (u // 2) + k) + u % 2
                                q = 64 * (u % 2)
                                o = ps[q:q + 64, 4 + c, P * k + S * hh:P * k + S * hh + S]
                                ins = pe.matmul(o, t["v"][r:r + 64, hh, d * h:d * h + d], pt, start=True, stop=True)
                    if u % 2:
                        ins.then_inc(sem(f"av_mm_{l}"), 1)

                def project_out(i):
                    if l != 3:
                        pe.wait_ge(sem(f"o_other_{l}"), UNITS * i + 6)
                    else:
                        pe.wait_ge(sem(f"o_half_{l}"), 4 * i + 4)
                        pe.wait_ge(sem(f"o_other_{l}"), 4 * i + 4)
                    for hh in range(2):
                        o = ps[:, 6, P * hh:P * hh + P]
                        n = WIN[l] // P
                        for k in range(n):
                            lt = t["o"][:, P * hh:P * hh + P] if l != 3 else \
                                t["o"].rearrange("p (k n) -> p k n", k=8)[:, k, P * hh:P * hh + P]
                            ins = pe.matmul(o, lt, wo[l][:, k, :], start=(k == 0), stop=(k == n - 1))
                    ins.then_inc(sem("att_mm"), 1)

                def group(i, first=False, more=True):
                    value_rows(i)
                    scores(i, 2)
                    turn(i, 0)
                    pe.wait_ge(sem(f"v_ready_{l}"), 4 * i + 4 if l == 3 else i + 1)
                    if not first:
                        project_out(i - 1)
                    values(i, 0)
                    turn(i, 1)
                    scores(i, 3)
                    if more:
                        queries_keys(i + 1)
                    values(i, 1)
                    turn(i, 2)
                    if more:
                        scores(i + 1, 0)
                    if l == 3:
                        pe.wait_ge(sem(f"o_half_{l}"), 4 * i + 2)
                        pe.wait_ge(sem(f"o_other_{l}"), 4 * i + 2)
                    values(i, 2)
                    turn(i, 3)
                    if more:
                        scores(i + 1, 1)
                    values(i, 3)

                pe.nop().then_inc(sem(f"v_mm_{l}"), 4 if l == 3 else 1)
                if l > 1:
                    if l == 2:
                        pe.wait_ge(sem("bvs_ready"), 1)
                        pe.matmul(ps[:, 4, 0:P], bvs[:, :], wo[2][:, 0, :], start=True, stop=False)
                    pe.matmul(ps[:, 4, 0:P], ones[:, :], rows[:, l - 2, :], start=(l == 3), stop=True
                              ).then_inc(sem("offset_mm"), 1)
                queries_keys(0)
                scores(0, 0)
                scores(0, 1)
                if l > 1:
                    pe.wait_ge(sem("offset_ready"), l - 1)
                group(0, first=True)
                with pe.Fori(1, NG - 1) as i:
                    group(i)
                group(NG - 1, more=False)
                project_out(NG - 1)

            def experts(l):
                for j in range(NT):
                    o = ps[:, 7, E * j:E * j + E]
                    ins = pe.matmul(o, xnT[:, P * j:P * j + P], gw[l][:, :], start=True, stop=True)
                ins.then_inc(sem("logits"), 1)
                pe.wait_ge(sem("choice_ready"), l)
                w = NT * E
                pe.matmul(ps[:, 6, 0:w], before[:, :], ohb[:, :], start=True, stop=False)
                for j in range(1, NT):
                    pe.matmul(ps[:, 6, E * j:w], onesb[:, :], ohb[:, 0:w - E * j], start=False, stop=(j == NT - 1))
                for j in range(NT):
                    ins = pe.matmul(ps[:, 5, 0:E], onesb[:, :], ohb[:, E * j:E * j + E], start=(j == 0), stop=(j == NT - 1))
                ins.then_inc(sem("places_mm"), 1)
                if l == 2:
                    t = table(l)
                    pe.wait_ge(sem("loaded_experts"), 16 * N_PAR[l])
                    for n in range(3 * E):
                        if n >= 4:
                            pe.wait_ge(sem("wexpT_ready"), n - 3)
                        for f in range(NF):
                            lo = F * (n % 3) + P * f
                            ins = pe.transpose(ps[:, n % 4, P * f:P * f + P], t[:, n // 3, lo:lo + P], ident[:, :])
                        ins.then_inc(sem("wexp_T"), 1)
                    pe.wait_ge(sem("wexpT_ready"), 3 * E)

                def load_T(i, s_):
                    pe.wait_ge(sem(f"xq_loaded{s_ % 4}"), 16 * (i + (QB[l] // 4 + s_ // 4 + 1)))
                    pe.transpose(ps[:, 6 + s_ % 2, 0:P], xq[:, s_ % 4, :], ident[:, :]).then_inc(sem("xq_T"), 1)

                def hidden(i, s_):
                    pe.wait_ge(sem("xqT_ready"), 4 * i + (QB[l] + s_ + 1))
                    pe.wait_ge(sem("w_staged"), 4 * i + (QB[l] + s_ + 1))
                    for m in range(2 if l == 2 else 1):
                        for f in range(NF):
                            lo = F * m + P * f
                            ins = pe.matmul(ps[:, 2 * m + s_ % 2, P * f:P * f + P], wst[:, s_ % 4, lo:lo + P],
                                            xqT[:, s_ % 2, :], start=True, stop=True)
                        ins.then_inc(sem("h_mm"), 1)

                def output(i, s_):
                    pe.wait_ge(sem("y_taken"), 4 * i + (QB[l] + s_ + 1))
                    if l == 2:
                        pe.wait_ge(sem("gated_ready"), 4 * i + (s_ + 1))
                    else:
                        pe.wait_ge(sem("hidden_ready"), 16 * i + (4 * s_ + 4 + (0 if l == 1 else 4 * NQ[1])))
                    lo = 2 * F if l == 2 else F
                    for f in range(NF):
                        ins = pe.matmul(ps[:, 4 + s_ % 2, 0:P], hT[:, s_ % 2, f, :], wst[:, s_ % 4, lo + P * f:lo + P * f + P],
                                        start=(f == 0), stop=(f == NF - 1))
                    ins.then_inc(sem("y_mm"), 1)

                def turn(i, first=False, final=False):
                    for s_ in range(4):
                        if not (final and s_ == 3):
                            load_T(i, s_ + 1)
                        hidden(i, s_)
                        if not (first and s_ == 0):
                            output(i, s_ - 1)
                load_T(0, 0)
                turn(0, first=True)
                turns = NQ[l] // 4
                with pe.Fori(1, turns - 1) as i:
                    turn(i)
                turn(turns - 1, final=True)
                output(turns - 1, 3)

            for l in (1, 2, 3):
                norm_T()
                attention(l)
                if last == 2 * l + 1:
                    return
                norm_T()
                if l == 2:
                    pe.transpose(ps[:, 7, 0:P], attw[:, :], ident[:, :])
                    pe.transpose(ps[:, 7, P:P + E], gwn[:, :], ident[0:E, 0:E]).then_inc(sem("prep2_T"), 1)
                    pe.wait_ge(sem("prep2_ready"), 1)
                    for c in range(NC):
                        if c >= 2:
                            pe.wait_ge(sem("hres_ready"), c - 1)
                        for k in range(4):
                            j = 4 * c + k
                            ins = pe.matmul(ps[:, 4 + c % 2, P * k:P * k + P], xnT[:, P * j:P * j + P], attwT[:, :],
                                            start=True, stop=True)
                        ins.then_inc(sem("attw_mm"), 1)
                    norm_T()
                experts(l)
                if last == 2 * l + 2:
                    return


_OUTS = [((B, S, D), "float32")]


def kernel(**inputs):
    import numpy as _np
    import concourse.bacc as _bacc
    from concourse import mybir as _mybir
    from concourse.bass_utils import run_bass_kernel_spmd as _run

    nc = _bacc.Bacc("TRN2", target_bir_lowering=False, num_devices=1)
    arrays, args = {}, {}
    for name, value in inputs.items():
        arr = _np.ascontiguousarray(value)
        arrays[f"in_{name}"] = arr
        args[name] = nc.dram_tensor(f"in_{name}", arr.shape, _mybir.dt.from_np(arr.dtype), kind="ExternalInput").ap()
    shape, dtype = _OUTS[0]
    out = nc.dram_tensor("out_0", shape, _mybir.dt.from_np(_np.dtype(dtype)), kind="ExternalOutput").ap()
    flamingo_kernel(nc, args, out)
    r = _run(nc, [arrays], core_ids=[0])
    return r.results[0]["out_0"]
```
